# Optimizing a Trainium2 kernel written in Bass

```python
import numpy as np
import jax
import jax.numpy as jnp

def _softmax(x, axis=-1):
    return jax.nn.softmax(x, axis=axis)

def _gelu(x):
    return jax.nn.gelu(x, approximate=True)

def _silu(x):
    return jax.nn.silu(x)

def _sigmoid(x):
    return jax.nn.sigmoid(x)

def _layernorm(x, axis=-1, eps=1e-05):
    m = jnp.mean(x, axis=axis, keepdims=True)
    v = jnp.var(x, axis=axis, keepdims=True)
    return (x - m) / jnp.sqrt(v + eps)

def _scatter_add(tgt, idx, src, axis=0):
    return tgt.at[idx].add(src)

def _segment_sum(src, seg, n):
    return jax.ops.segment_sum(src, seg, n)
kernel_name = 'mk_gnn_preln_d2_gnn_r8_b52c8a'

def setup_inputs(seed: int=0):
    np.random.seed(seed)
    _w = jnp.asarray

    def _rec_inputs():
        import jax
        import jax.numpy as jnp
        _gk = jax.random.key(seed)
        x = -0.0003713 + 1 * jax.random.normal(jax.random.fold_in(_gk, 1), (6250, 128), jnp.float32)
        _s = jax.random.randint(jax.random.fold_in(_gk, 2), (50000,), 0, 6250, jnp.int32)
        _d = jax.random.randint(jax.random.fold_in(_gk, 3), (50000,), 0, 6250, jnp.int32)
        _loop = jnp.arange(6250, dtype=jnp.int32)
        src = jnp.concatenate([_s, _d, _loop])
        dst = jnp.concatenate([_d, _s, _loop])
        _o = jnp.argsort(dst, stable=True)
        src = src[_o]
        dst = dst[_o]
        edge_attr_128 = -4.0964e-05 + 1.00013 * jax.random.normal(jax.random.fold_in(_gk, 11), (106250, 128), jnp.float32)
        edge_weight = jax.random.uniform(jax.random.fold_in(_gk, 13), (106250,), jnp.float32, 0.0, 0.999999)
        return (x, src, dst, edge_attr_128, edge_weight)
    x, src, dst, edge_attr_128, edge_weight = _rec_inputs()

    def _L0_gnn_setup():
        import jax, jax.numpy as jnp
        import numpy as np
        N, E = (12500, 80000)
        D_IN, D_EDGE, D_OUT = (128, 128, 128)
        key = jax.random.key(seed)
        ks = jax.random.split(key, 7)
        x = jax.random.normal(ks[0], (N, D_IN), jnp.float32)
        src = jax.random.randint(ks[1], (E,), 0, N, dtype=jnp.int32)
        dst = jax.random.randint(ks[2], (E,), 0, N, dtype=jnp.int32)
        edge_index = jnp.stack([src, dst], axis=0)
        edge_weight = jax.random.uniform(ks[3], (E,), jnp.float32)
        edge_attr = jax.random.normal(ks[4], (E, D_EDGE), jnp.float32)
        W_msg = jax.random.normal(ks[5], (2 * D_IN + D_EDGE, D_OUT), jnp.float32) / jnp.sqrt(2.0 * D_IN + D_EDGE)
        W_self = jax.random.normal(ks[6], (D_IN, D_OUT), jnp.float32) / jnp.sqrt(float(D_IN))
        return {'x': x, 'edge_index': edge_index, 'edge_weight': edge_weight, 'edge_attr': edge_attr, 'W_msg': W_msg, 'W_self': W_self}
    _L0_gnn_all = _L0_gnn_setup()
    _L0_gnn_in = {k: v for k, v in _L0_gnn_all.items() if k in ('W_msg', 'W_self')}
    del _L0_gnn_all

    def _L1_gnn_setup():
        import jax, jax.numpy as jnp
        import numpy as np
        N = 6250
        E = 200000
        D_IN = 128
        D_HID = 128

        def _sage_conv(x, src, dst, W_l, b_l, W_r, num_nodes):
            msgs = x[src]
            agg = jax.ops.segment_sum(msgs, dst, num_segments=num_nodes)
            cnt = jax.ops.segment_sum(jnp.ones((src.shape[0],), x.dtype), dst, num_segments=num_nodes)
            mean = agg / jnp.maximum(cnt, 1.0)[:, None]
            return mean @ W_l.T + b_l + x @ W_r.T
        key = jax.random.key(seed)
        k_x, k_e, k1, k2, k3, k4 = jax.random.split(key, 6)
        x = jax.random.normal(k_x, (N, D_IN), dtype=jnp.float32)
        edge_index = jax.random.randint(k_e, (2, E), 0, N, dtype=jnp.int32)
        s1 = 1.0 / np.sqrt(D_IN)
        s2 = 1.0 / np.sqrt(D_HID)
        W1_l = jax.random.uniform(k1, (D_HID, D_IN), jnp.float32, -s1, s1)
        b1_l = jnp.zeros((D_HID,), jnp.float32)
        W1_r = jax.random.uniform(k2, (D_HID, D_IN), jnp.float32, -s1, s1)
        W2_l = jax.random.uniform(k3, (D_HID, D_HID), jnp.float32, -s2, s2)
        b2_l = jnp.zeros((D_HID,), jnp.float32)
        W2_r = jax.random.uniform(k4, (D_HID, D_HID), jnp.float32, -s2, s2)
        return {'x': x, 'edge_index': edge_index, 'W1_l': W1_l, 'b1_l': b1_l, 'W1_r': W1_r, 'W2_l': W2_l, 'b2_l': b2_l, 'W2_r': W2_r}
    _L1_gnn_all = _L1_gnn_setup()
    _L1_gnn_in = {k: v for k, v in _L1_gnn_all.items() if k in ('W1_l', 'b1_l', 'W1_r', 'W2_l', 'b2_l', 'W2_r')}
    del _L1_gnn_all
    return {'x': x, 'src': src, 'dst': dst, 'edge_attr_128': edge_attr_128, 'edge_weight': edge_weight, 'L0_gnn_W_msg': _L0_gnn_in['W_msg'], 'L0_gnn_W_self': _L0_gnn_in['W_self'], 'L1_gnn_W1_l': _L1_gnn_in['W1_l'], 'L1_gnn_b1_l': _L1_gnn_in['b1_l'], 'L1_gnn_W1_r': _L1_gnn_in['W1_r'], 'L1_gnn_W2_l': _L1_gnn_in['W2_l'], 'L1_gnn_b2_l': _L1_gnn_in['b2_l'], 'L1_gnn_W2_r': _L1_gnn_in['W2_r']}

def reference(x, src, dst, edge_attr_128, edge_weight, L0_gnn_W_msg, L0_gnn_W_self, L1_gnn_W1_l, L1_gnn_b1_l, L1_gnn_W1_r, L1_gnn_W2_l, L1_gnn_b2_l, L1_gnn_W2_r):
    import jax
    import jax.numpy as jnp

    def _L0_gnn_ref(x, edge_index, edge_weight, edge_attr, W_msg, W_self):
        import jax, jax.numpy as jnp
        import numpy as np
        N, E = (12500, 80000)
        D_IN, D_EDGE, D_OUT = (128, 128, 128)
        src, dst = (edge_index[0], edge_index[1])
        d = x.shape[1]
        W_i, W_j, W_e = (W_msg[:d], W_msg[d:2 * d], W_msg[2 * d:])
        h_i = x @ W_i
        h_j = x @ W_j
        msg = h_i[dst] + h_j[src] + edge_attr @ W_e
        msg = edge_weight[:, None] * msg
        agg = jax.ops.segment_sum(msg, dst, num_segments=x.shape[0])
        return agg + x @ W_self

    def _L1_gnn_ref(x, edge_index, W1_l, b1_l, W1_r, W2_l, b2_l, W2_r):
        import jax, jax.numpy as jnp
        import numpy as np
        N = 6250
        E = 200000
        D_IN = 128
        D_HID = 128

        def _sage_conv(x, src, dst, W_l, b_l, W_r, num_nodes):
            msgs = x[src]
            agg = jax.ops.segment_sum(msgs, dst, num_segments=num_nodes)
            cnt = jax.ops.segment_sum(jnp.ones((src.shape[0],), x.dtype), dst, num_segments=num_nodes)
            mean = agg / jnp.maximum(cnt, 1.0)[:, None]
            return mean @ W_l.T + b_l + x @ W_r.T
        src, dst = (edge_index[0], edge_index[1])
        num_nodes = x.shape[0]
        h = _sage_conv(x, src, dst, W1_l, b1_l, W1_r, num_nodes)
        h = jax.nn.relu(h)
        h = _sage_conv(h, src, dst, W2_l, b2_l, W2_r, num_nodes)
        return jax.nn.log_softmax(h, axis=-1)
    edge_index = jnp.stack([src, dst])
    h = jnp.maximum(_layernorm(x, axis=-1), 0.0)
    x = x + _L0_gnn_ref(h, edge_index, edge_weight, edge_attr_128, L0_gnn_W_msg, L0_gnn_W_self)
    h = jnp.maximum(_layernorm(x, axis=-1), 0.0)
    x = x + _L1_gnn_ref(h, edge_index, L1_gnn_W1_l, L1_gnn_b1_l, L1_gnn_W1_r, L1_gnn_W2_l, L1_gnn_b2_l, L1_gnn_W2_r)
    return x

_drawn_inputs = setup_inputs


def setup_inputs(seed=0):
    import zlib

    import numpy as np

    out = dict(_drawn_inputs(seed))
    spreads = {'L1_gnn_b1_l': (0.0, 0.8), 'L1_gnn_b2_l': (0.0, 0.613)}
    factors = {'L1_gnn_W1_l': 2.858, 'L1_gnn_W2_l': 2.669}
    for name, (base, spread) in spreads.items():
        noise = np.random.default_rng([zlib.crc32(name.encode()), seed]).standard_normal(out[name].shape)
        drawn = base * np.exp(spread * noise) if base else spread * noise
        out[name] = jnp.asarray(drawn.astype(out[name].dtype))
    for name, factor in factors.items():
        out[name] = (out[name] * factor).astype(out[name].dtype)
    return out
```

```python
import concourse.bass as bass
from concourse import mybir
from contextlib import ExitStack

F32 = mybir.dt.float32
F16 = mybir.dt.float16
FP8 = mybir.dt.float8e4
I32 = mybir.dt.int32
ALU = mybir.AluOpType
ACT = mybir.ActivationFunctionType
AX = mybir.AxisListType

D = 5
SL = 128
HW = 64
OW = 96
STEP = 384
HSCALE = 4096.0


class Shape:

    def __init__(self, n, e, groups):
        self.n, self.e = n, e
        self.nb = -(-n // 128)
        self.np = self.nb * 128
        self.g = -(-e // 512)
        self.ep = self.g * 512
        self.nt = self.g * 4
        self.nw = n // D
        self.wg = -(-self.nw // 128)
        self.hb = -(-(self.ep // 64) // 128)
        self.nh = -(-self.nw // HW)
        self.key = D * self.nb
        self.kx = self.key + D
        self.qg = groups
        assert n % (2 * D) == 0 and self.ep - e >= 128 and 2 * self.kx <= 512
        top = self.np - OW
        self.base = [max(0, min(top, round((512 * g + 256) * n / e) - OW // 2)) for g in range(self.g)]
        self.bank = [b // STEP for b in self.base]
        assert self.base[-1] == top

    def windows(self, hh):
        return min(HW, self.nw - HW * hh)

    def width(self, hh):
        return D * self.windows(hh)


FULL = Shape(6250, 106250, [(0, 12), (12, 24), (24, 36), (36, 45), (45, 49)])


class Queue:

    def __init__(self, sem):
        self.sem, self.n, self.ops, self.seen = sem, 0, [], {}

    def wait(self, *tokens):
        for t in tokens:
            if t is None:
                continue
            sem, v = t
            if self.seen.get(id(sem), 0) < v:
                self.seen[id(sem)] = v
                self.ops.append(lambda e, sem=sem, v=v: e.wait_ge(sem, v))

    def run(self, f):
        self.ops.append(f)

    def mark(self, f):
        self.n += 1
        self.ops.append(lambda e: f(e).then_inc(self.sem, 1))
        return (self.sem, self.n)

    def dma(self, f, ds):
        ds.n += 16
        self.ops.append(lambda e: f(e).then_inc(ds.sem, 16))
        return (ds.sem, ds.n)


class DmaSem:
    def __init__(self, sem):
        self.sem, self.n = sem, 0


class Steps:

    def __init__(self, rounds):
        self.rounds = rounds
        self.ops = {x: [] for x in ("SP", "PO", "AC", "PE", "DV")}

    def do(self, engine, f, after=None, then=None):
        ops = self.ops[engine]
        if after is not None:
            link, n = after
            ops.append(lambda e, i: e.wait_ge(link, n))
            ops.append(lambda e, i: e.sem_clear(link))
        if then is None:
            ops.append(f)
        else:
            to, by = then
            ops.append(lambda e, i: f(e, i).then_inc(to, by))


def general_path(nc, T, S, out, sem, M, P):
    NB, NP, NT = S.nb, S.np, S.nt
    rows = NP + 128
    acc = [nc.dram_tensor(f"acc{i}_d", [rows, w], F32).ap() for i, w in enumerate((258, 128, 128))]
    x1_d, h1_d, h2_d = (nc.dram_tensor(n, [NP, 128], F32).ap() for n in ("x1_d", "h1_d", "h2_d"))
    links = ("go", "to_po", "to_dv", "gathered", "eq_pe", "sums", "dv_po", "dv_pe", "dv_sp", "dv_ac", "dv", "po_dma",
             "ac_dv", "ac_sp", "ac", "pe", "stored")
    (go, to_po, to_dv, gathered, eq_pe, sums, dv_po, dv_pe, dv_sp, dv_ac, dv, po_dma,
     ac_dv, ac_sp, ac, pe, stored) = (sem("g_" + n) for n in links)
    src_r, dst_r, ew_r = (T[k].rearrange("(n o) -> n o", o=1) for k in ("src", "dst", "ew"))
    dst_c = T["dst"].rearrange("(o n) -> o n", o=1)
    C, msg, rsum, eq, eqw, junk, drow = M["C"], M["msg"], M["rsum"], M["eq"], M["eqw"], M["junk"], M["drow"]
    col, coli = M["col"], M["coli"]
    low, dummy = C[:, 0:128], C[:, 128:129]
    ds = bass.ds
    loops = []

    L = Steps(1)
    L.do("SP", lambda e, i: e.dma_start(C, T["gen"]), then=(to_dv, 16))
    L.do("DV", lambda e, i: e.memset(rsum, 0.0), (to_dv, 16), (dv, 1))
    L.do("DV", lambda e, i: e.memset(msg[:, 256:257], 1.0), (dv, 1), (dv_sp, 1))
    for n, a in enumerate(acc):
        w = a.shape[1]
        L.do("SP", lambda e, i, a=a, w=w: e.dma_start(
            a.rearrange("(b p) f -> p b f", p=128), rsum[:, 0:w].unsqueeze(1).to_broadcast([128, rows // 128, w])),
            (dv_sp, 1) if n == 0 else None, (stored, 16))
    L.do("SP", lambda e, i: e.sem_inc(go, 1), (stored, 48))
    loops.append(L)

    def settled(L, then):
        L.do("PO", lambda e, i: e.wait_ge(po_dma, 16))
        L.do("PO", lambda e, i: e.dma_reset(range(po_dma.num, po_dma.num + 1)))
        L.do("PO", lambda e, i: e.sem_clear(po_dma))
        L.do("PO", lambda e, i: e.sem_inc(then, 1))

    def edges(table, a, first):
        w = 258 if first else 128
        L = Steps(NT)
        tile = lambda v, i: v[ds(i * 128, 128), :]
        L.do("SP", lambda e, i: e.dma_start(coli[:, 0:1], tile(src_r, i)), (go, 1), (to_po, 16))
        L.do("SP", lambda e, i: e.dma_start(coli[:, 1:2], tile(dst_r, i)), None, (to_po, 16))
        L.do("SP", lambda e, i: e.dma_start(col[:, 0:1], tile(ew_r, i)), None, (to_po, 16))
        L.do("SP", lambda e, i: e.dma_start(drow, dst_c[:, ds(i * 128, 128)].to_broadcast([128, 128])), None, (to_po, 16))
        if first:
            L.do("SP", lambda e, i: e.dma_start(msg[:, 128:256], tile(T["ea"], i)), None, (to_po, 16))
        L.do("PO", lambda e, i: e.indirect_dma_start(msg[:, 0:128], None, table, bass.IndirectOffsetOnAxis(coli[:, 0:1], 0)),
             (to_po, 80 if first else 64), (po_dma, 16))
        settled(L, gathered)
        L.do("DV", lambda e, i: e.tensor_copy(col[:, 1:2], coli[:, 1:2]), (gathered, 1), (dv, 1))
        L.do("DV", lambda e, i: e.tensor_scalar(eq, drow, col[:, 1:2], 0.0, ALU.is_equal, ALU.add,
                                                accum_out=rsum[:, 257:258]), (dv, 1), (dv, 1))
        L.do("DV", lambda e, i: e.scalar_tensor_tensor(junk, drow, col[:, 1:2], low, ALU.is_equal, ALU.mult,
                                                       accum_out=col[:, 2:3]), (dv, 1), (dv, 1))
        L.do("DV", lambda e, i: e.tensor_tensor(col[:, 3:4], dummy, col[:, 1:2], ALU.subtract), (dv, 1), (dv, 1))
        L.do("DV", lambda e, i: e.scalar_tensor_tensor(col[:, 4:5], col[:, 2:3], 0.5, col[:, 3:4], ALU.is_gt, ALU.mult),
             (dv, 1), (dv, 1))
        L.do("DV", lambda e, i: e.tensor_tensor(coli[:, 2:3], col[:, 4:5], col[:, 1:2], ALU.add), (dv, 1),
             (dv, 1) if first else (eq_pe, 1))
        if first:
            L.do("DV", lambda e, i: e.tensor_scalar(eqw, eq, col[:, 0:1], None, ALU.mult), (dv, 1), (eq_pe, 1))
            L.do("PE", lambda e, i: e.matmul(P["PA"][:, 0:257], eqw, msg[:, 0:257], start=True, stop=True), (eq_pe, 1), (sums, 1))
            L.do("DV", lambda e, i: e.tensor_copy(rsum[:, 0:257], P["PA"][:, 0:257]), (sums, 1), (dv_po, 1))
        else:
            L.do("PE", lambda e, i: e.matmul(P["PA"][:, 0:128], eq, msg[:, 0:128], start=True, stop=True), (eq_pe, 1), (sums, 1))
            L.do("DV", lambda e, i: e.tensor_copy(rsum[:, 0:128], P["PA"][:, 0:128]), (sums, 1), (dv_po, 1))
        L.do("PO", lambda e, i: e.indirect_dma_start(a, bass.IndirectOffsetOnAxis(coli[:, 2:3], 0), rsum[:, 0:w], None,
                                                     compute_op=ALU.add), (dv_po, 1), (po_dma, 16))
        settled(L, go)
        loops.append(L)

    nA, nX, nH, tT, o1, o2, s1 = M["nA"], M["nX"], M["nH"], M["tT"], M["o1"], M["o2"], M["s1"]
    W, bb, idn = M["W"], M["bb"], M["idn"]
    blk = lambda v, i: v[ds(i * 128, 128), :]

    def turned(L, parts, weights, then):
        m = len(parts)
        for j, v in enumerate(parts):
            L.do("PE", lambda e, i, j=j, v=v: e.transpose(P["PA"][:, 128 * j:128 * j + 128], v, idn),
                 (dv_pe, 1) if j == 0 else None, (pe, 1) if j == m - 1 else None)
        L.do("DV", lambda e, i: e.tensor_copy(tT[:, 0:128 * m], P["PA"][:, 0:128 * m]), (pe, 1), (dv_pe, 1))
        for j, w in enumerate(weights):
            L.do("PE", lambda e, i, j=j, w=w: e.matmul(P["PB"][:, 0:128], tT[:, 128 * j:128 * j + 128], w,
                                                       start=j == 0, stop=j == m - 1),
                 (dv_pe, 1) if j == 0 else None, then if j == m - 1 else None)

    edges(M["h0_d"], acc[0], True)
    L = Steps(NB)
    L.do("SP", lambda e, i: e.dma_start(nA, blk(acc[0], i)), (go, 1), (to_dv, 16))
    L.do("SP", lambda e, i: e.dma_start(nX, blk(T["x"], i)), None, (to_dv, 16))
    L.do("SP", lambda e, i: e.dma_start(nH, blk(M["h0_d"], i)), None, (to_dv, 16))
    L.do("DV", lambda e, i: e.tensor_scalar(o1, nH, nA[:, 256:257], None, ALU.mult), (to_dv, 48), (dv_pe, 1))
    turned(L, (nA[:, 0:128], nA[:, 128:256], o1, nH), (W["WJ"], W["WE"], W["WI"], W["WS"]), (sums, 1))
    L.do("DV", lambda e, i: e.tensor_tensor(o1, P["PB"][:, 0:128], nX, ALU.add), (sums, 1), (dv, 1))
    L.do("DV", lambda e, i: e.bn_stats(s1[:, 0:6], o1), (dv, 1), (dv, 1))
    L.do("DV", lambda e, i: e.bn_aggr(s1[:, 6:8], s1[:, 0:6]), (dv, 1), (dv, 1))
    L.do("DV", lambda e, i: e.tensor_scalar(s1[:, 8:9], s1[:, 7:8], 1e-5, None, ALU.add), (dv, 1), (dv_ac, 1))
    L.do("AC", lambda e, i: e.activation(s1[:, 9:10], s1[:, 8:9], ACT.Sqrt), (dv_ac, 1), (ac_dv, 1))
    L.do("DV", lambda e, i: e.reciprocal(s1[:, 10:11], s1[:, 9:10]), (ac_dv, 1), (dv, 1))
    L.do("DV", lambda e, i: e.tensor_scalar(s1[:, 11:12], s1[:, 10:11], HSCALE, None, ALU.mult), (dv, 1), (dv, 1))
    L.do("DV", lambda e, i: e.scalar_tensor_tensor(s1[:, 12:13], s1[:, 6:7], -1.0, s1[:, 11:12], ALU.mult, ALU.mult),
         (dv, 1), (dv_ac, 1))
    L.do("AC", lambda e, i: e.activation(o2, o1, ACT.Relu, bias=s1[:, 12:13], scale=s1[:, 11:12]), (dv_ac, 1), (ac_sp, 1))
    L.do("SP", lambda e, i: e.dma_start(blk(x1_d, i), o1), (ac_sp, 1), (stored, 16))
    L.do("SP", lambda e, i: e.dma_start(blk(h1_d, i), o2), None, (stored, 16))
    L.do("SP", lambda e, i: e.sem_inc(go, 1), (stored, 32))
    loops.append(L)

    def conv(a, h_d, wl, wr, by, bias):
        L = Steps(NB)
        L.do("SP", lambda e, i: e.dma_start(nA[:, 0:128], blk(a, i)), (go, 1), (to_dv, 16))
        L.do("SP", lambda e, i: e.dma_start(nA[:, 256:258], acc[0][ds(i * 128, 128), 256:258]), None, (to_dv, 16))
        L.do("SP", lambda e, i: e.dma_start(nX, blk(x1_d, i)), None, (to_dv, 16))
        L.do("SP", lambda e, i: e.dma_start(nH, blk(h_d, i)), None, (to_dv, 16))
        L.do("DV", lambda e, i: e.tensor_scalar(s1[:, 0:1], nA[:, 257:258], 1.0, None, ALU.max), (to_dv, 64), (dv, 1))
        L.do("DV", lambda e, i: e.reciprocal(s1[:, 1:2], s1[:, 0:1]), (dv, 1), (dv, 1))
        L.do("DV", lambda e, i: e.tensor_scalar(o2, nA[:, 0:128], s1[:, 1:2], by, ALU.mult, ALU.mult), (dv, 1), (dv_pe, 1))
        turned(L, (o2, nH), (wl, wr), (sums, 1))
        L.do("DV", lambda e, i: e.tensor_tensor(o1, P["PB"][:, 0:128], bias, ALU.add), (sums, 1), (dv, 1))
        loops.append(L)
        return L

    edges(h1_d, acc[1], False)
    L = conv(acc[1], h1_d, W["W1L"], W["W1R"], 1.0 / HSCALE, bb[:, 0, :])
    L.do("DV", lambda e, i: e.tensor_scalar(o2, o1, 0.0, None, ALU.max), (dv, 1), (dv_sp, 1))
    L.do("SP", lambda e, i: e.dma_start(blk(h2_d, i), o2), (dv_sp, 1), (stored, 16))
    L.do("SP", lambda e, i: e.sem_inc(go, 1), (stored, 16))

    edges(h2_d, acc[2], False)
    L = conv(acc[2], h2_d, W["W2L"], W["W2R"], 1.0, bb[:, 1, :])
    L.do("DV", lambda e, i: e.tensor_reduce(s1[:, 2:3], o1, AX.X, ALU.max, negate=True), (dv, 1), (dv_ac, 1))
    L.do("AC", lambda e, i: e.activation(o2, o1, ACT.Exp, bias=s1[:, 2:3], accum_out=s1[:, 3:4]), (dv_ac, 1), (ac, 1))
    L.do("AC", lambda e, i: e.activation(s1[:, 4:5], s1[:, 3:4], ACT.Ln), (ac, 1), (ac_dv, 1))
    L.do("DV", lambda e, i: e.tensor_tensor(s1[:, 5:6], s1[:, 4:5], s1[:, 2:3], ALU.subtract), (ac_dv, 1), (dv, 1))
    L.do("DV", lambda e, i: e.scalar_tensor_tensor(o2, o1, s1[:, 5:6], nX, ALU.subtract, ALU.add), (dv, 1), (dv_sp, 1))
    L.do("SP", lambda e, i: e.dma_start(blk(out, i), o2), (dv_sp, 1), (stored, 16))
    L.do("SP", lambda e, i: e.sem_inc(go, 1), (stored, 16))
    L = Steps(1)
    L.do("SP", lambda e, i: e.wait_ge(go, 1))
    loops.append(L)
    return loops


def gnn_kernel(nc, T, S, out):
    NB, NP, G, NT, WG, HB = S.nb, S.np, S.g, S.nt, S.wg, S.hb
    KEY, KX, NH, NW = S.key, S.kx, S.nh, S.nw
    ctx = ExitStack()
    with ctx:
        def sb(name, shape, dt=F32):
            return ctx.enter_context(nc.sbuf_tensor(name, shape, dt))

        def sem(name):
            return ctx.enter_context(nc.semaphore(name))

        def dsem(name):
            return DmaSem(sem(name))

        h0_d = nc.dram_tensor("h0_d", [NP, 128], F32).ap()
        cs_d = nc.dram_tensor("cs_d", [2, WG * 128 * D], F32).ap()
        c_d = nc.dram_tensor("c_d", [NH, 128, NB * HW * D], FP8).ap()

        xs = sb("xs", [128, NB, 128])
        agg = sb("agg", [128, NP])
        h0 = agg[:, :].rearrange("p (b f) -> p b f", f=128)
        R = sb("R", [128, NB, 128])
        h1r = sb("h1r", [128, NB * 128])
        h1 = h1r[:, :].bitcast(F16).rearrange("p (a b f) -> p a b f", a=2, f=128)
        l0 = sb("l0", [128, max(NB * 128, 5120 + 96 * 12)])
        h2 = l0[:, 0:NB * 128].bitcast(F16).rearrange("p (a b f) -> p a b f", a=2, f=128)
        EAN, GAN, OHN, QN = 6, 16, 12, 3
        ea = l0[:, 0:3072].rearrange("p (n j f) -> p n j f", n=EAN, j=4)
        ga = l0[:, 3072:5120].rearrange("p (n f) -> p n f", n=GAN)
        oh = l0[:, 5120:5120 + OW * OHN].rearrange("p (n f) -> p n f", n=OHN)
        CW = (NB + 1) * HW * D
        cbr = sb("cbr", [128, CW // 2])
        cb = cbr[:, :].bitcast(FP8)
        win = h1r[:, :] if NB >= 3 * WG else sb("win", [128, 3 * 128 * WG])[:, :]
        wsrc = win[:, 0:128 * WG].bitcast(I32)
        wdst = win[:, 128 * WG:256 * WG].bitcast(I32)
        wew = win[:, 256 * WG:384 * WG]
        src_n = sb("src_s", [128, NT], I32)
        dst_n = sb("dst_s", [128, NT], I32)
        drel = dst_n[:, :].bitcast(F32)
        ew_n = sb("ew_s", [128, NT])
        c16 = sb("c16_s", [128, 128 + 128 * 4 + KEY * 4], F16)
        iota = c16[:, 0:OW]
        IR = c16[:, 128:640].rearrange("p (r w) -> p r w", w=4)
        IK = c16[:, 640:640 + 4 * KEY].rearrange("p (r w) -> p r w", w=4)
        early = R[:, :, :].rearrange("p b f -> p (b f)")
        early = early[:, NB * 128 - 128 * WG - G:]
        baseb = early[:, 128 * WG:128 * WG + G]
        QE = min(-(-NB // 4), 5)
        WH = 128 * ((WG + 1) // 2)
        if NB * 128 - 128 * WG - G - 512 * QE >= 3 * WH:
            tmp = R[:, :, :].rearrange("p b f -> p (b f)")[:, 512 * QE:512 * QE + 3 * WH]
        else:
            tmp = sb("tmp", [128, 3 * WH])
        tmp = tmp.rearrange("p (n k) -> p n k", n=3)
        iow = early[:, 0:64 * WG].bitcast(F16)
        d64 = early[:, 64 * WG:128 * WG].bitcast(I32).rearrange("p (w s) -> p w s", s=64)
        c32 = sb("c32_s", [128, 128 + WG])
        idn = c32[:, 0:128]
        w5 = c32[:, 128:128 + WG]
        id16 = sb("id16", [128, 128], F16)
        ones16 = sb("ones16", [128, 1], F16)
        zero16 = sb("zero16", [128, 128], F16)
        any16 = c16[:, 128:640]
        ones = sb("ones", [128, 128])
        heads = sb("heads_s", [128, HB], I32)
        hs = sb("hs", [128, HB])
        rT = sb("rT", [128, 128 * WG], F16)
        kT = sb("kT", [128, 128 * WG], F16)
        ohr = sb("ohr", [128, QN, 128, 4], F16)
        ohk = sb("ohk", [128, QN, KX, 4], F16)
        AT = sb("AT", [128, 2, 512])
        BT = sb("BT", [128, 2, 512])
        W = sb("W", [128, 8, 128])
        WI, WJ, WE, WS, W1L, W1R, W2L, W2R = (W[:, i, :] for i in range(8))
        bcol = sb("bcol", [128, 1])
        brow = sb("brow", [1, 2, 128])
        bb = sb("bb", [128, 2, 128])
        H = sb("H", [128, 2, 384])
        wn = H[:, 0, 0:256].rearrange("p (a f) -> p a f", a=2)
        diag = H[:, 1, 0:128]
        HT = sb("HT", [128, 2, 512])
        cmp = HT[:, :, :].bitcast(F16).rearrange("p a k -> p (a k)")
        cmp = (cmp, AT[:, :, :].rearrange("p a k -> p (a k)").bitcast(F16))
        st6 = sb("st6", [128, NB, 6])
        mv = sb("mv", [128, NB, 2])
        sd = sb("sd", [128, NB])
        rs = sb("rs", [128, NB])
        nb_ = sb("nb_", [128, NB])
        kk = sb("kk", [128, WG])
        idx1 = sb("idx1", [128, WG], I32)
        idx2 = sb("idx2", [128, WG], I32)
        c64 = sb("c64", [128, WG])
        cs = sb("cs", [128, 2, WG, D])
        csr = H[0:NB, 1, 128:384].rearrange("p (a f) -> p a f", a=2)
        inv = sb("inv", [128, 2, NB])
        sw = sb("sw", [128, NB])
        sc = sb("sc", [128, 8])
        sci = sb("sci", [128, 2], I32)
        fl = sb("fl", [128, 8])
        flag_f = sb("flag_f", [1, 4])
        flag = sb("flag", [1, 1], I32)
        sm = sb("sm", [128, 4, 4])
        rmax = sb("rmax", [128, NH])
        junk = sb("junk", [128, HW * D], F16)

        names = ["PA", "PB", "PC0", "PC1", "PV0", "PV1", "PM0", "PM1"]
        P = {n: ctx.enter_context(nc.psum_tensor(n, [128, 512], F32)) for n in names}
        free = dict.fromkeys(names)

        PE, DV, AC, PO, SP = (Queue(sem(n)) for n in ("s_pe", "s_dv", "s_ac", "s_po", "s_sp"))

        def mm(o, l, r, start, stop):
            return lambda e: e.matmul(o, l, r, start=start, stop=stop, skip_group_check=True)

        d_a, d_c, d_nat, d_w = dsem("d_a"), dsem("d_c"), dsem("d_nat"), dsem("d_w")
        SP.dma(lambda e: e.dma_start(heads[:, :], T["heads"]), d_a)
        t_head = SP.dma(lambda e: e.dma_start(iow, T["iow"]), d_a)
        XP = 7
        pieces = [(b, min(NB, b + XP)) for b in range(0, NB, XP)]
        xv = T["x"].rearrange("(b p) f -> p b f", p=128)
        t_x = []
        for i, (b0, b1) in enumerate(pieces):
            t_x.append(SP.dma(lambda e, b0=b0, b1=b1: e.dma_start(xs[:, b0:b1, :], xv[:, b0:b1, :]), dsem(f"d_x{i}")))
        SP.dma(lambda e: e.dma_start(c32[:, :], T["c32"]), d_c)
        t_c32 = SP.dma(lambda e: e.dma_start(c16[:, :], T["c16"]), d_c)
        AC.dma(lambda e: e.dma_start(dst_n[:, :], T["dst_n"]), d_nat)
        AC.dma(lambda e: e.dma_start(baseb, T["base"]), d_nat)
        AC.dma(lambda e: e.dma_start(ew_n[:, :], T["ew_n"]), d_nat)
        t_nat = AC.dma(lambda e: e.dma_start(src_n[:, :], T["src_n"]), d_nat)
        for i, w in enumerate(["WI", "WJ", "WE", "WS", "W1L", "W1R", "W2L", "W2R"]):
            AC.dma(lambda e, i=i, w=w: e.dma_start(W[:, i, :], T[w]), d_w)
        AC.dma(lambda e: e.dma_start(wn[:, 0, :], T["W1Ln"]), d_w)
        AC.dma(lambda e: e.dma_start(wn[:, 1, :], T["W1Rn"]), d_w)
        AC.dma(lambda e: e.dma_start(bcol[:, :], T["b1"].rearrange("(p o) -> p o", o=1)), d_w)
        AC.dma(lambda e: e.dma_start(brow[:, 0, :], T["b1"].rearrange("(o p) -> o p", o=1)), d_w)
        t_w = AC.dma(lambda e: e.dma_start(brow[:, 1, :], T["b2"].rearrange("(o p) -> o p", o=1)), d_w)

        PO.run(lambda e: e.memset(ones16[:, :], 1.0))
        PO.run(lambda e: e.memset(zero16[:, :], 0.0))
        PO.run(lambda e: e.memset(cs[:, :, :, :], 0.0))
        PO.run(lambda e: e.memset(fl[:, :], 0.0))
        PO.run(lambda e: e.memset(ohk[:, :, KEY + 1:KX, :], 0.0))
        PO.run(lambda e: e.memset(ohk[:, :, KEY:KEY + 1, :], 1.0))
        t_cst = PO.mark(lambda e: e.memset(ones[:, :], 1.0))

        DV.wait(t_head)
        t = DV.mark(lambda e: e.tensor_scalar(hs[:, :], heads[:, :], 0.5, 1.0 / D, ALU.add, ALU.mult))
        DV.wait(t)
        PE.wait(t_cst, t_head)
        PE.run(mm(P["PV0"][:, 0:WG], zero16[:, :], iow[:, 0:WG], True, False))
        t_pe = [None, None]
        for i in range(HB):
            DV.wait(t_pe[i % 2])
            c = cmp[i % 2][:, 0:128 * WG]
            t = DV.mark(lambda e, i=i, c=c: e.tensor_scalar(c, iow, hs[:, i:i + 1], None, ALU.is_gt))
            PE.wait(t)
            for w in range(WG):
                f = mm(P["PV0"][:, w:w + 1], c[:, 128 * w:128 * w + 128], ones16[:, :], False, i == HB - 1)
                if w < WG - 1:
                    PE.run(f)
            t_pe[i % 2] = PE.mark(f)
        DV.wait(t_pe[(HB - 1) % 2])
        t = DV.mark(lambda e: e.tensor_scalar(kk[:, :], P["PV0"][:, 0:WG], -1.0, 0.0, ALU.add, ALU.max))
        free["PV0"] = t
        DV.wait(t)
        t_i1 = DV.mark(lambda e: e.tensor_scalar(idx1[:, :], kk[:, :], 64.0, None, ALU.mult))

        dst_r = T["dst"].rearrange("(n o) -> n o", o=1)
        src_r = T["src"].rearrange("(n o) -> n o", o=1)
        ew_r = T["ew"].rearrange("(n o) -> n o", o=1)

        def fetch(dst, tab, idx, w, ds):
            return PO.dma(lambda e: e.indirect_dma_start(dst, None, tab, bass.IndirectOffsetOnAxis(idx[:, w:w + 1], 0)), ds)

        d_h = dsem("d_h")
        PO.wait(t_i1)
        for w in range(WG):
            t_d64 = fetch(d64[:, w, :], dst_r, idx1, w, d_h)

        def window_starts():
            nonlocal t_c64
            DV.wait(t_d64, t_c32)
            for w in range(WG):
                t = DV.mark(lambda e, w=w: e.tensor_scalar(d64[:, w, :], d64[:, w, :], w5[:, w:w + 1], 0.0,
                                                           ALU.is_lt, ALU.add, accum_out=c64[:, w:w + 1]))
            DV.wait(t)
            t = t_c64 = DV.mark(lambda e: e.scalar_tensor_tensor(kk[:, :], kk[:, :], 64.0, c64[:, :], ALU.mult, ALU.add))
            DV.wait(t)
            t_i2 = DV.mark(lambda e: e.tensor_scalar(idx2[:, :], kk[:, :], float(S.ep - SL), None, ALU.min))
            PO.wait(t_i2)
            for w in range(WG):
                fetch(wsrc[:, 128 * w:128 * w + 128], src_r, idx2, w, d_win[0 if w < (WG + 1) // 2 else 1])
                t_win[w] = fetch(wdst[:, 128 * w:128 * w + 128], dst_r, idx2, w, d_win[0 if w < (WG + 1) // 2 else 1])

        t_c64, t_win, t_ww = None, {}, {}
        d_win, d_ww = [dsem("d_win0"), dsem("d_win1")], [dsem(f"d_ww{i}") for i in range(3)]

        def window_weight(w):
            t_ww[w] = fetch(wew[:, 128 * w:128 * w + 128], ew_r, idx2, w, d_ww[w % 3])

        d_h0 = dsem("d_h0")
        t_h0 = []
        for i, (b0, b1) in enumerate(pieces):
            DV.wait(t_x[i])
            for b in range(b0, b1):
                t = DV.mark(lambda e, b=b: e.bn_stats(st6[:, b, :], xs[:, b, :]))
            DV.wait(t)
            for b in range(b0, b1):
                t = DV.mark(lambda e, b=b: e.bn_aggr(mv[:, b, :], st6[:, b, :]))
            DV.wait(t)
            t = DV.mark(lambda e, b0=b0, b1=b1: e.tensor_scalar(sd[:, b0:b1], mv[:, b0:b1, 1], 1e-5, None, ALU.add))
            AC.wait(t)
            t = AC.mark(lambda e, b0=b0, b1=b1: e.activation(sd[:, b0:b1], sd[:, b0:b1], ACT.Sqrt))
            DV.wait(t)
            t = DV.mark(lambda e, b0=b0, b1=b1: e.reciprocal(rs[:, b0:b1], sd[:, b0:b1]))
            DV.wait(t)
            t = DV.mark(lambda e, b0=b0, b1=b1: e.scalar_tensor_tensor(
                nb_[:, b0:b1], mv[:, b0:b1, 0], -1.0, rs[:, b0:b1], ALU.mult, ALU.mult))
            AC.wait(t, t_x[i])
            for b in range(b0, b1):
                t = AC.mark(lambda e, b=b: e.activation(h0[:, b, :], xs[:, b, :], ACT.Relu,
                                                        bias=nb_[:, b:b + 1], scale=rs[:, b:b + 1]))
            t_h0.append(t)
            SP.wait(t)
            t_h0d = SP.dma(lambda e, b0=b0, b1=b1: e.dma_start(
                h0_d.rearrange("(b p) f -> p b f", p=128)[:, b0:b1, :], h0[:, b0:b1, :]), d_h0)
            if i == min(3, len(pieces) - 1):
                window_starts()

        ea_v = T["ea"].rearrange("(g p j) f -> g p j f", p=128, j=4)
        d_ea = [dsem(f"d_ea{i}") for i in range(EAN)]
        d_ga = [dsem(f"d_ga{i}") for i in range(GAN)]
        t_ea, t_ga, t_oh, t_l0 = {}, {}, {}, {}

        def load_ea(g):
            if g >= G:
                return
            if g >= EAN:
                SP.wait(t_l0[4 * (g - EAN) + 3])
            t_ea[g] = SP.dma(lambda e: e.dma_start(ea[:, g % EAN, :, :], ea_v[g]), d_ea[g % EAN])

        def gather(t):
            if t >= GAN:
                PO.wait(t_l0[t - GAN])
            t_ga[t] = PO.dma(lambda e: e.indirect_dma_start(
                ga[:, t % GAN, :], None, h0_d, bass.IndirectOffsetOnAxis(src_n[:, t:t + 1], 0)), d_ga[t % GAN])

        def onehot(t):
            if t >= NT:
                return
            if t >= OHN:
                DV.wait(t_l0[t - OHN])
            t_oh[t] = DV.mark(lambda e: e.tensor_scalar(
                oh[:, t % OHN, :], iota, drel[:, t:t + 1], ew_n[:, t:t + 1], ALU.is_equal, ALU.mult))

        def tile(t):
            g = t // 4
            k = S.bank[g]
            if t == 0 or (t % 4 == 0 and S.bank[g - 1] != k):
                PE.wait(free["PA"])
                PE.run(mm(P["PA"][:, :], zero16[:, :], any16, True, False))
                PE.wait(free["PB"])
                PE.run(mm(P["PB"][:, :], zero16[:, :], any16, True, False))
            at = S.base[g] - STEP * k
            last = t == NT - 1 or (t % 4 == 3 and S.bank[g + 1] != k)
            PE.wait(t_ga[t], t_oh[t])
            PE.run(mm(P["PA"][:, at:at + OW], ga[:, t % GAN, :], oh[:, t % OHN, :], False, last))
            PE.wait(t_ea[g])
            t_l0[t] = PE.mark(mm(P["PB"][:, at:at + OW], ea[:, g % EAN, t % 4, :], oh[:, t % OHN, :], False, last))

        t_quad, t_ht = {}, [None, None]

        def quad_turn(i):
            b0, b1 = 4 * i, min(NB, 4 * i + 4)
            m = b1 - b0
            PE.wait(t_c32, t_h0[(b1 - 1) // XP], free["PM1"])
            for j in range(m):
                f = lambda e, j=j: e.transpose(P["PM1"][:, 128 * j:128 * j + 128], h0[:, b0 + j, :], idn)
                if j < m - 1:
                    PE.run(f)
            t = PE.mark(f)
            AC.wait(t, t_ht[0], t_pe[0], t_pe[1])
            free["PM1"] = t_qht[i] = AC.mark(lambda e: e.activation(HT[:, 0, 0:128 * m], P["PM1"][:, 0:128 * m], ACT.Copy))
            t_ht[0] = t_qht[i]

        t_qht = {}

        def quad_product(i):
            b0, b1 = 4 * i, min(NB, 4 * i + 4)
            m = b1 - b0
            PE.wait(t_qht[i], t_w, free["PM0"], free["PV0"])
            for bank, w in (("PM0", WS), ("PV0", WI)):
                for j in range(m):
                    f = mm(P[bank][:, 128 * j:128 * j + 128], HT[:, 0, 128 * j:128 * j + 128], w, True, True)
                    if bank == "PM0" or j < m - 1:
                        PE.run(f)
            t = PE.mark(f)
            t_ht[0] = t
            x4 = xs[:, b0:b1, :].rearrange("p b f -> p (b f)")
            DV.wait(t, t_h0[(b1 - 1) // XP])
            free["PM0"] = DV.mark(lambda e: e.tensor_tensor(x4, P["PM0"][:, 0:128 * m], x4, ALU.add))
            AC.wait(t, t_c64, t_drel, t_prep["rk", 1] if i >= QE else None)
            free["PV0"] = AC.mark(lambda e: e.activation(R[:, b0:b1, :].rearrange("p b f -> p (b f)"),
                                                         P["PV0"][:, 0:128 * m], ACT.Copy))
            t_quad[i] = (free["PM0"], free["PV0"])

        V = 128 * WG
        t_prep = {}

        parts = [(0, (WG + 1) // 2), ((WG + 1) // 2, WG)]
        r16, k16 = {}, {}

        def windows_elementwise(part):
            wa, wz = parts[part]
            c = slice(128 * wa, 128 * wz)
            n = 128 * (wz - wa)
            fT, v_ = tmp[:, 0, 0:n], tmp[:, 1, 0:n]
            ri = tmp[:, 2, 0:n].bitcast(I32)
            d_ = wdst.bitcast(F32)[:, c]
            s_ = wsrc[:, c]
            DV.wait(t_win[wz - 1], t_c32, t_prep.get(("rk", 0)))
            t = DV.mark(lambda e: e.tensor_scalar(ri, s_, 127, None, ALU.bitwise_and))
            t2 = DV.mark(lambda e: e.tensor_tensor(
                d_.rearrange("p (c s) -> p c s", s=128), wdst[:, c].rearrange("p (c s) -> p c s", s=128),
                w5[:, wa:wz].unsqueeze(2).to_broadcast([128, wz - wa, 128]), ALU.subtract))
            DV.wait(t)
            t3 = DV.mark(lambda e: e.tensor_tensor(fT, s_, ri, ALU.subtract))
            DV.wait(t2)
            t4 = DV.mark(lambda e: e.tensor_scalar(v_, d_, 0.0, None, ALU.is_ge))
            DV.wait(t4)
            t4 = DV.mark(lambda e: e.scalar_tensor_tensor(v_, d_, float(D), v_, ALU.is_lt, ALU.mult))
            DV.wait(t3)
            t3 = DV.mark(lambda e: e.scalar_tensor_tensor(fT, fT, D / 128.0, d_, ALU.mult, ALU.add))
            DV.wait(t3, t4)
            k_, r_ = s_.bitcast(F16)[:, 0:n], s_.bitcast(F16)[:, n:2 * n]
            DV.mark(lambda e: e.tensor_scalar(k_, fT, 1.0, None, ALU.add))
            t5 = DV.mark(lambda e: e.scalar_tensor_tensor(r_, ri, 1.0, v_, ALU.add, ALU.mult))
            t_prep["rk", part] = t5
            for w in range(wa, wz):
                k16[w] = k_[:, 128 * (w - wa):128 * (w - wa) + 128]
                r16[w] = r_[:, 128 * (w - wa):128 * (w - wa) + 128]

        t_rk = {}

        def windows_turn(w):
            bank = ("PM0", "PM1")[w % 2]
            PE.wait(t_prep["rk", 0 if w < parts[0][1] else 1], free[bank], t_id16)
            v = P[bank][:, :].bitcast(F16)
            PE.run(lambda e: e.transpose(v[:, 0:128], r16[w], id16[:, :]))
            t = PE.mark(lambda e: e.transpose(v[:, 128:256], k16[w], id16[:, :]))
            t_prep["turn"] = t
            AC.wait(t)
            AC.run(lambda e: e.activation(rT[:, 128 * w:128 * w + 128], v[:, 0:128], ACT.Copy))
            t = AC.mark(lambda e: e.activation(kT[:, 128 * w:128 * w + 128], v[:, 128:256], ACT.Copy))
            free[bank] = t_rk[w] = t

        def counts(w):
            pw = min(128, NW - 128 * w)
            d_ = wdst.bitcast(F32)[0:pw, 128 * w:128 * w + 128]
            j0, j1 = (HT[0:pw, 1, 128 * i:128 * i + 128] for i in (0, 1))
            DV.wait(t_cst, t_ww[w], t_prep.get("j"), *t_pe)
            for i in range(D):
                t = DV.mark(lambda e, i=i: e.tensor_scalar(j0, d_, float(i), 0.0, ALU.is_equal, ALU.add,
                                                           accum_out=cs[0:pw, 0, w, i:i + 1]))
                t2 = DV.mark(lambda e, i=i: e.scalar_tensor_tensor(j1, d_, float(i), wew[0:pw, 128 * w:128 * w + 128],
                                                                   ALU.is_equal, ALU.mult,
                                                                   accum_out=cs[0:pw, 1, w, i:i + 1]))
                DV.wait(t, t2)
            t_prep["j"] = t2

        d_cs = dsem("d_cs")

        def spread_counts():
            nonlocal t_cs
            SP.wait(t_prep["j"])
            for i in range(2):
                t = SP.dma(lambda e, i=i: e.dma_start(
                    cs_d[i].rearrange("(c w d) -> w c d", w=128, d=D), cs[:, i, :, :]), d_cs)
            SP.wait(t)
            for i in range(2):
                t = SP.dma(lambda e, i=i: e.dma_start(
                    csr[:, i, :], cs_d[i, 0:NP].rearrange("(b p) -> b p", p=128)), d_cs)
            t_cs = t

        t_cs = None

        def turn_counts():
            PE.wait(t_cs, free["PM0"])
            PE.run(lambda e: e.transpose(P["PM0"][:, 0:NB], csr[:, 0, :], idn[0:NB, 0:NB]))
            t = PE.mark(lambda e: e.transpose(P["PM0"][:, 64:64 + NB], csr[:, 1, :], idn[0:NB, 0:NB]))
            t_prep["cT"] = t

        def keep_counts():
            DV.wait(t_prep["cT"])
            t = DV.mark(lambda e: e.tensor_scalar(inv[:, 0, :], P["PM0"][:, 0:NB], 1.0, None, ALU.max))
            t_prep["sw"] = free["PM0"] = DV.mark(lambda e: e.tensor_copy(sw[:, :], P["PM0"][:, 64:64 + NB]))
            DV.wait(t)
            t = DV.mark(lambda e: e.reciprocal(inv[:, 1, :], inv[:, 0, :]))
            DV.wait(t)
            t_prep["inv"] = DV.mark(lambda e: e.tensor_scalar(inv[:, 0, :], inv[:, 1, :], 1.0 / HSCALE, None, ALU.mult))

        t_base = {}

        def add_hi(b):
            DV.wait(t_prep["sw"], *t_quad[b // 4])
            t_base[b] = DV.mark(lambda e: e.scalar_tensor_tensor(
                xs[:, b, :], R[:, b, :], sw[:, b:b + 1], xs[:, b, :], ALU.mult, ALU.add))

        def scales():
            DV.wait(t_w, t_c32)
            for i in range(2):
                t = DV.mark(lambda e, i=i: e.scalar_tensor_tensor(diag, wn[:, i, :], 1.0, wn[:, i, :], ALU.mult,
                                                                  ALU.mult, accum_out=sc[:, i:i + 1]))
                DV.wait(t)
            AC.wait(t)
            t = AC.mark(lambda e: e.activation(sc[:, 0:2], sc[:, 0:2], ACT.Sqrt))
            t2 = AC.mark(lambda e: e.activation(sc[:, 2:3], bcol[:, :], ACT.Abs))
            t_prep["sc"] = (t, t2)

        def powers():
            DV.wait(*t_prep["sc"])
            t = DV.mark(lambda e: e.tensor_tensor(sc[:, 0:1], sc[:, 0:1], sc[:, 1:2], ALU.add))
            DV.wait(t)
            t = DV.mark(lambda e: e.scalar_tensor_tensor(sc[:, 0:1], sc[:, 0:1], 11.5, sc[:, 2:3], ALU.mult, ALU.add))
            DV.wait(t)
            t = DV.mark(lambda e: e.tensor_scalar(sc[:, 0:1], sc[:, 0:1], 1e-30, 1e30, ALU.max, ALU.min))
            DV.wait(t)
            t = DV.mark(lambda e: e.tensor_scalar(sci[:, 0:1], sc[:, 0:1].bitcast(I32), 0x7F800000, None, ALU.bitwise_and))
            DV.wait(t)
            t = DV.mark(lambda e: e.tensor_scalar(sci[:, 1:2], sci[:, 0:1], -1.0, float(254 << 23), ALU.mult, ALU.add))
            t2 = DV.mark(lambda e: e.tensor_scalar(sc[:, 4:5], sci[:, 0:1].bitcast(F32), 2.0 ** -14, None, ALU.mult))
            DV.wait(t, t2)
            t = DV.mark(lambda e: e.tensor_scalar(sc[:, 3:4], sci[:, 1:2].bitcast(F32), 2.0 ** 14, None, ALU.mult))
            DV.wait(t)
            t = DV.mark(lambda e: e.tensor_scalar(diag, idn, sc[:, 3:4], None, ALU.mult))
            t2 = DV.mark(lambda e: e.tensor_scalar(W2L, W2L, sc[:, 4:5], None, ALU.mult))
            t3 = DV.mark(lambda e: e.tensor_scalar(W2R, W2R, sc[:, 4:5], None, ALU.mult))
            PE.wait(t, t_cst, free["PM1"])
            t_prep["sT"] = PE.mark(mm(P["PM1"][:, 0:128], ones[:, :], diag, True, True))
            t_prep["w2"] = (t2, t3)

        def scaled_weights():
            DV.wait(t_prep["sT"])
            t1 = DV.mark(lambda e: e.tensor_tensor(W1L, W1L, P["PM1"][:, 0:128], ALU.mult))
            t2 = DV.mark(lambda e: e.scalar_tensor_tensor(W1R, W1R, 1.0 / HSCALE, P["PM1"][:, 0:128], ALU.mult, ALU.mult))
            t = free["PM1"] = DV.mark(lambda e: e.tensor_tensor(
                brow[:, 0, :], brow[:, 0, :], P["PM1"][0:1, 0:128], ALU.mult))
            PE.wait(t, t1, t2)
            t_prep["bT"] = PE.mark(mm(P["PM1"][:, 0:256], ones[0:1, :], brow[:, :, :].rearrange("o a f -> o (a f)"), True, True))

        def keep_biases():
            DV.wait(t_prep["bT"])
            t_prep["w"] = free["PM1"] = DV.mark(lambda e: e.tensor_copy(
                bb[:, :, :].rearrange("p a f -> p (a f)"), P["PM1"][:, 0:256]))

        pair = [0]
        t_c, t_cst_half, t_ring, t_used = {}, {}, [None] * QN, {}
        d_cb = [dsem(f"d_cb{i}") for i in range(2)]
        t_row, t_made = {}, {}
        quads = [(hh, w, min(w + 4, S.windows(hh))) for hh in range(NH) for w in range(0, S.windows(hh), 4)]
        CB = ("PC0", "PC1", "PV1")

        def built(hh):
            return cb[:, (hh % 2) * CW:(hh % 2) * CW + (NB + 1) * S.width(hh)].rearrange("p (q k) -> p q k", q=NB + 1)

        def count_quad(i):
            hh, a, z = quads[i]
            w0 = HW * hh + a
            n = z - a
            R_ = i % QN
            DV.wait(t_rk[w0 // 128], t_ring[R_], t_cst)
            r_o, k_o = ohr[:, R_, :, 0:n], ohk[:, R_, 0:KEY, 0:n]
            DV.run(lambda e: e.tensor_tensor(r_o, IR[:, :, 0:n], rT[:, w0:w0 + n].unsqueeze(1).to_broadcast([128, 128, n]),
                                             ALU.is_equal))
            t = DV.mark(lambda e: e.tensor_tensor(k_o, IK[:, :, 0:n], kT[:, w0:w0 + n].unsqueeze(1).to_broadcast([128, KEY, n]),
                                                  ALU.is_equal))
            t_made[i] = t

        def count_product(i):
            hh, a, z = quads[i]
            n = z - a
            R_ = i % QN
            cv = built(hh)
            PE.wait(t_made[i])
            for j in range(n):
                bank = CB[pair[0] % 3]
                if j % 2 == 0:
                    PE.wait(free[bank])
                f = mm(P[bank][:, KX * (j % 2):KX * (j % 2) + KX], ohr[:, R_, :, j], ohk[:, R_, :, j], True, True)
                if j % 2 == 0:
                    PE.run(f)
                    continue
                t = PE.mark(f)
                AC.wait(t)
                if hh >= 2:
                    AC.wait(t_cst_half[hh - 2], t_row[hh - 2], t_used.get(hh - 2))
                c0 = D * (a + j - 1)
                o = cv[:, :, c0:c0 + 2 * D].rearrange("p q (w d) -> p w q d", w=2)
                s_ = P[bank][:, 0:2 * KX].rearrange("p (w q d) -> p w q d", w=2, d=D)
                t_c[hh] = free[bank] = AC.mark(lambda e, o=o, s_=s_: e.activation(o, s_, ACT.Copy, saturate=False))
                pair[0] += 1
            t_ring[R_] = t
            if z == S.windows(hh):
                SP.wait(t_c[hh])
                t_cst_half[hh] = SP.dma(lambda e: e.dma_start(
                    c_d[hh, :, 0:NB * S.width(hh)], cb[:, (hh % 2) * CW:(hh % 2) * CW + NB * S.width(hh)]), d_cb[hh % 2])

        def row_check(hh):
            DV.wait(t_c[hh], t_row.get(hh - 1))
            t_row[hh] = DV.mark(lambda e: e.tensor_scalar(junk[:, 0:S.width(hh)], built(hh)[:, NB, :], 15.0, 0.0,
                                                          ALU.is_gt, ALU.add, accum_out=rmax[:, hh:hh + 1]))

        NK = S.bank[-1] + 1
        t_ev, t_X, t_h1, t_Hfree, t_R = {}, {}, {}, [None, None], {}

        def step_blocks(k):
            return list(range(3 * k, NB if k == NK - 1 else min(NB, 3 * k + 3)))

        def step_evac(k, last_tile):
            AC.wait(t_l0[last_tile], t_X.get(k - 1))
            a = AC.mark(lambda e: e.activation(AT[:, k % 2, :], P["PA"][:, :], ACT.Copy))
            b = AC.mark(lambda e: e.activation(BT[:, k % 2, :], P["PB"][:, :], ACT.Copy))
            free["PA"], free["PB"] = a, b
            t_ev[k] = (a, b)

        def step_x(k):
            bl = step_blocks(k)
            PE.wait(*t_ev[k], free["PM0"], t_w)
            for i, b in enumerate(bl):
                o = P["PM0"][:, 128 * i:128 * i + 128]
                at = 128 * b - STEP * k
                ops = [(AT[:, k % 2, at:at + 128], WJ), (BT[:, k % 2, at:at + 128], WE)]
                if i == 0 and k > 0:
                    ops += [(AT[:, (k - 1) % 2, STEP:STEP + 128], WJ), (BT[:, (k - 1) % 2, STEP:STEP + 128], WE)]
                for j, (l, r) in enumerate(ops):
                    f = mm(o, l, r, j == 0, j == len(ops) - 1)
                    if b != bl[-1] or j < len(ops) - 1:
                        PE.run(f)
            t_X[k] = PE.mark(f)

        def step_ln(k):
            bl = step_blocks(k)
            b0, b1, m = bl[0], bl[-1] + 1, len(bl)
            xk = xs[:, b0:b1, :].rearrange("p b f -> p (b f)")
            DV.wait(t_X[k], *[t_base[b] for b in bl])
            t = free["PM0"] = DV.mark(lambda e: e.tensor_tensor(xk, P["PM0"][:, 0:128 * m], xk, ALU.add))
            DV.wait(t)
            for b in bl:
                t = DV.mark(lambda e, b=b: e.bn_stats(st6[:, b, :], xs[:, b, :]))
            DV.wait(t)
            for b in bl:
                t = DV.mark(lambda e, b=b: e.bn_aggr(mv[:, b, :], st6[:, b, :]))
            DV.wait(t)
            t = DV.mark(lambda e: e.tensor_scalar(sd[:, b0:b1], mv[:, b0:b1, 1], 1e-5, None, ALU.add))
            AC.wait(t)
            t_sd[k] = AC.mark(lambda e: e.activation(sd[:, b0:b1], sd[:, b0:b1], ACT.Sqrt))

        t_sd, t_hi1 = {}, {}

        def step_h1(k):
            bl = step_blocks(k)
            b0, b1, m = bl[0], bl[-1] + 1, len(bl)
            DV.wait(t_sd[k])
            t = DV.mark(lambda e: e.reciprocal(rs[:, b0:b1], sd[:, b0:b1]))
            DV.wait(t)
            t = DV.mark(lambda e: e.tensor_scalar(rs[:, b0:b1], rs[:, b0:b1], HSCALE, None, ALU.mult))
            DV.wait(t)
            t = DV.mark(lambda e: e.scalar_tensor_tensor(
                nb_[:, b0:b1], mv[:, b0:b1, 0], -1.0, rs[:, b0:b1], ALU.mult, ALU.mult))
            AC.wait(t, t_Hfree[k % 2], t_prep["w"], t_prep["sw"])
            Hk = H[:, k % 2, 0:128 * m]
            for i, b in enumerate(bl):
                t = AC.mark(lambda e, b=b, i=i: e.activation(H[:, k % 2, 128 * i:128 * i + 128], xs[:, b, :], ACT.Relu,
                                                             bias=nb_[:, b:b + 1], scale=rs[:, b:b + 1]))
            AC.wait(t, t_prep["turn"], t_prep["j"])
            hi = h1[:, 0, b0:b1, :].rearrange("p b f -> p (b f)")
            t_hi1[k] = AC.mark(lambda e: e.activation(hi, Hk, ACT.Copy))

        def step_low(k):
            bl = step_blocks(k)
            b0, b1, m = bl[0], bl[-1] + 1, len(bl)
            Hk = H[:, k % 2, 0:128 * m]
            hi = h1[:, 0, b0:b1, :].rearrange("p b f -> p (b f)")
            lo = h1[:, 1, b0:b1, :].rearrange("p b f -> p (b f)")
            DV.wait(t_hi1[k], t_prep["turn"], t_prep["j"])
            t = DV.mark(lambda e: e.tensor_tensor(lo, Hk, hi, ALU.subtract))
            t_Hfree[k % 2] = t
            for b in bl:
                t_h1[b] = t

        def turn(h, bl, tH, bank, ring):
            m = len(bl)
            PE.wait(tH, free[bank], t_id16)
            for i, b in enumerate(bl):
                o = P[bank][:, 128 * i:128 * i + 128]
                PE.run(mm(o, h[:, 0, b, :], id16[:, :], True, False))
                f = mm(o, h[:, 1, b, :], id16[:, :], False, True)
                if i < m - 1:
                    PE.run(f)
            t = PE.mark(f)
            AC.wait(t, t_ht[ring], t_prep["j"])
            free[bank] = AC.mark(lambda e: e.activation(HT[:, ring, 0:128 * m], P[bank][:, 0:128 * m], ACT.Copy))
            return free[bank]

        def self_term(bl, ring, tT, bank, w, j):
            PE.wait(tT, free[bank], t_prep["w"], t_cst)
            for i, b in enumerate(bl):
                f = mm(P[bank][:, 128 * i:128 * i + 128], HT[:, ring, 128 * i:128 * i + 128], w, True, True)
                if b != bl[-1]:
                    PE.run(f)
            t = PE.mark(f)
            t_ht[ring] = t
            DV.wait(t, t_base.get(bl[-1]) if j == 0 else t_T.get(bl[-1]))
            free[bank] = DV.mark(lambda e: e.tensor_tensor(
                R[:, bl[0]:bl[-1] + 1, :], P[bank][:, 0:128 * len(bl)].rearrange("p (b f) -> p b f", f=128),
                bb[:, j, :].unsqueeze(1).to_broadcast([128, len(bl), 128]), ALU.add))
            for b in bl:
                t_R[j, b] = free[bank]

        t_turn = {}

        def step_turn(k):
            t_turn[k] = turn(h1, step_blocks(k), t_h1[step_blocks(k)[-1]], "PM1", 1)

        def step_r(k):
            self_term(step_blocks(k), 1, t_turn[k], "PM0", W1R, 0)

        t_T = {}
        ring_free = {}
        d_cl = [dsem(f"d_cl{i}") for i in range(8)]
        LAST = len(S.qg) - 1
        big = max(z - a for a, z in S.qg) * HW * D
        per = min(4, CW // big)
        t_agg = {}
        loads = [0]

        def load_part(gi, hh):
            q0, q1 = S.qg[gi]
            wd = S.width(hh)
            s = loads[0] % (2 * per) if gi < LAST else per + loads[0] % per
            loads[0] += 1
            half = s // per
            SP.wait(t_cst_half[hh], ring_free.get(s))
            for h in (NH - 1, NH - 2):
                if h % 2 == half:
                    SP.wait(t_cst_half[h], t_row[h], t_used.get(h))
            o = cb[:, half * CW + (s % per) * big:half * CW + (s % per) * big + (q1 - q0) * wd]
            return s, SP.dma(lambda e: e.dma_start(o, c_d[hh, :, q0 * wd:q1 * wd]), d_cl[s]), o

        def product(bank, h, th, o, q0, a, z, q1, wd, tload):
            if a == q0:
                PE.wait(tload, free[bank])
            for q in range(a, z):
                PE.wait(th[q])
                r = o[:, (q - q0) * wd:(q - q0 + 1) * wd]
                PE.run(mm(P[bank][:, 0:wd], h[:, 0, q, :], r, q == q0, False))
                f = mm(P[bank][:, 0:wd], h[:, 1, q, :], r, False, q == q1 - 1)
                if q < z - 1:
                    PE.run(f)
            return PE.mark(f)

        def conv1_sum(hh, bank, t):
            c = agg[:, HW * D * hh:HW * D * hh + S.width(hh)]
            p = P[bank][:, 0:S.width(hh)]
            if hh not in t_agg:
                AC.wait(t, t_aggfree[0])
                t_agg[hh] = free[bank] = AC.mark(lambda e: e.activation(c, p, ACT.Copy))
            else:
                DV.wait(t, t_agg[hh])
                t_agg[hh] = free[bank] = DV.mark(lambda e: e.tensor_tensor(c, p, c, ALU.add))

        accs = ["PV0"]
        turn_acc = [0]
        owed = []

        def conv1_job(gi, hh, piece, held, done):
            q0, q1 = S.qg[gi]
            wd = S.width(hh)
            out_ = []
            st = {}
            for a in range(q0, q1, piece):
                z = min(q1, a + piece)

                def f(a=a, z=z):
                    if a == q0:
                        st["bank"] = accs[turn_acc[0] % len(accs)]
                        turn_acc[0] += 1
                        for x in list(owed):
                            if x[0] == st["bank"]:
                                owed.remove(x)
                                x[1]()
                    s, tl, o = held
                    t = product(st["bank"], h1, t_h1, o, q0, a, z, q1, wd, tl)
                    if z == q1:
                        if s is None:
                            t_used[hh] = t
                        else:
                            ring_free[s] = t
                        x = (st["bank"], lambda: conv1_sum(hh, st["bank"], t))
                        owed.append(x)

                        def settle():
                            if x in owed:
                                owed.remove(x)
                                x[1]()

                        done(settle)

                out_.append((f, (z - a) * 2 * wd / 2.35e3))
            return out_

        t_aggfree = [None]

        def clear_agg():
            DV.wait(t_h0d, t_qht[NQ - 1])
            t_aggfree[0] = DV.mark(lambda e: e.memset(agg[:, S.n:NP], 0.0)) if NP > S.n else t_qht[NQ - 1]

        def batch(hh):
            a = 0 if hh == 0 else HW * D * hh // 128
            z = NB if hh == NH - 1 else HW * D * (hh + 1) // 128
            return list(range(a, z))

        t_Y, t_hi, t_h2, t_lo = {}, {}, {}, {}
        Tb = AT[:, :, 0:384]

        def node1_y(hh):
            bl = batch(hh)
            PE.wait(t_agg[hh], t_agg.get(hh - 1), t_aggfree[0], free["PM0"], t_prep["w"])
            for i, b in enumerate(bl):
                f = mm(P["PM0"][:, 128 * i:128 * i + 128], agg[:, 128 * b:128 * b + 128], W1L, True, True)
                if b != bl[-1]:
                    PE.run(f)
            t_Y[hh] = PE.mark(f)
            for b in bl:
                t_yb[b] = t_Y[hh]
            DV.wait(t_Y[hh], t_X[NK - 1], t_prep["inv"], t_lo.get(hh - 2), t_hi.get(hh - 2))
            Tk = Tb[:, hh % 2, :]
            for i, b in enumerate(bl):
                DV.wait(t_R[0, b])
                t_T[b] = DV.mark(lambda e, i=i, b=b: e.scalar_tensor_tensor(
                    Tk[:, 128 * i:128 * i + 128], P["PM0"][:, 128 * i:128 * i + 128], inv[:, 0, b:b + 1], R[:, b, :],
                    ALU.mult, ALU.add))
            free["PM0"] = t_T[bl[-1]]
            m = len(bl)
            hi = h2[:, 0, bl[0]:bl[-1] + 1, :].rearrange("p b f -> p (b f)")
            lo = h2[:, 1, bl[0]:bl[-1] + 1, :].rearrange("p b f -> p (b f)")
            AC.wait(t_T[bl[-1]], t_l0[NT - 1])
            t = t_hi[hh] = AC.mark(lambda e: e.activation(hi, Tk[:, 0:128 * m], ACT.Relu))
            DV.wait(t, t_T[bl[-1]])
            t_lo[hh] = DV.mark(lambda e: e.scalar_tensor_tensor(lo, Tk[:, 0:128 * m], 0.0, hi, ALU.max, ALU.subtract))
            for b in bl:
                t_h2[b] = t_lo[hh]

        t_yb = {}
        t_turn2 = {}

        def node1_turn(hh):
            t_turn2[hh] = turn(h2, batch(hh), t_lo[hh], "PM1", hh % 2)

        def node1_r(hh):
            self_term(batch(hh), hh % 2, t_turn2[hh], "PB", W2R, 1)

        d_l2 = [dsem(f"d_l2{i}") for i in range(2)]
        load2, half_free = {}, {}
        t_a2 = {}
        accs2 = ["PC0", "PC1"]

        def load_half(hh):
            if hh >= NH:
                return
            wd = S.width(hh)
            s = hh % 2
            SP.wait(t_cst_half[hh], half_free.get(s))
            for i in range(s * per, s * per + per):
                SP.wait(ring_free.get(i))
            o = cb[:, s * CW:s * CW + NB * wd]
            load2[hh] = (SP.dma(lambda e: e.dma_start(o, c_d[hh, :, 0:NB * wd]), d_l2[s]), o)

        def conv2_half(hh, hooks):
            wd = S.width(hh)
            bank = accs2[hh % 2]
            tload, o = load2[hh]
            cuts = sorted({0, NB} | set(hooks))
            for a, z in zip(cuts, cuts[1:]):
                hooks.get(a, lambda: None)()
                t = product(bank, h2, t_h2, o, 0, a, z, NB, wd, tload)
            half_free[hh % 2] = t
            c = agg[:, HW * D * hh:HW * D * hh + wd]
            last = min(NB - 1, (HW * D * hh + wd - 1) // 128)
            AC.wait(t, t_yb[last])
            t_a2[hh] = free[bank] = AC.mark(lambda e: e.activation(c, P[bank][:, 0:wd], ACT.Copy))

        t_o, t_st = {}, {}
        d_o = [dsem(f"d_o{i}") for i in range(2)]
        ov = out.rearrange("(b p) f -> p b f", p=128)

        def node2_y(hh):
            bl = batch(hh)
            m = len(bl)
            bank = ("PM0", "PA")[hh % 2]
            PE.wait(t_a2[hh], t_a2.get(hh - 1), free[bank], t_prep["w"])
            for i, b in enumerate(bl):
                f = mm(P[bank][:, 128 * i:128 * i + 128], agg[:, 128 * b:128 * b + 128], W2L, True, True)
                if b != bl[-1]:
                    PE.run(f)
            t = PE.mark(f)
            Tk = Tb[:, hh % 2, :]
            E_ = H[:, hh % 2, :]
            DV.wait(t, t_st.get(hh - 2), t_lo[NH - 1], t_lo.get(NH - 2))
            for i, b in enumerate(bl):
                DV.wait(t_R[1, b])
                t = DV.mark(lambda e, i=i, b=b: e.scalar_tensor_tensor(
                    Tk[:, 128 * i:128 * i + 128], P[bank][:, 128 * i:128 * i + 128], inv[:, 1, b:b + 1], R[:, b, :],
                    ALU.mult, ALU.add))
            free[bank] = t
            DV.wait(t)
            s = sm[:, :, 0:m] if hh % 2 == 0 else sm2[:, :, 0:m]
            t = DV.mark(lambda e: e.tensor_reduce(s[:, 0, :], Tk[:, 0:128 * m].rearrange("p (b f) -> p b f", f=128),
                                                  AX.X, ALU.max, negate=True))
            AC.wait(t, *t_Hfree)
            for i in range(m):
                t = AC.mark(lambda e, i=i: e.activation(E_[:, 128 * i:128 * i + 128], Tk[:, 128 * i:128 * i + 128], ACT.Exp,
                                                        bias=s[:, 0, i:i + 1], accum_out=s[:, 1, i:i + 1]))
            AC.wait(t)
            t = AC.mark(lambda e: e.activation(s[:, 2, :], s[:, 1, :], ACT.Ln))
            DV.wait(t)
            t = DV.mark(lambda e: e.tensor_tensor(s[:, 3, :], s[:, 2, :], s[:, 0, :], ALU.subtract))
            DV.wait(t)
            for i, b in enumerate(bl):
                t = DV.mark(lambda e, i=i, b=b: e.scalar_tensor_tensor(
                    Tk[:, 128 * i:128 * i + 128], Tk[:, 128 * i:128 * i + 128], s[:, 3, i:i + 1], xs[:, b, :],
                    ALU.subtract, ALU.add))
            SP.wait(t)
            t_st[hh] = SP.dma(lambda e: e.dma_start(ov[:, bl[0]:bl[-1] + 1, :],
                                                    Tk[:, 0:128 * m].rearrange("p (b f) -> p b f", f=128)), d_o[hh % 2])

        sm2 = sb("sm2", [128, 4, 4])

        def make_flag():
            DV.wait(t_prep["j"], t_drel, *t_row.values())
            a = DV.mark(lambda e: e.tensor_reduce(fl[:, 0:1], rmax[:, :], AX.X, ALU.add))
            b = DV.mark(lambda e: e.tensor_reduce(fl[:, 2:3], cs[:, 0, :, :].rearrange("p c d -> p (c d)"), AX.X, ALU.add))
            c = DV.mark(lambda e: e.tensor_reduce(fl[:, 5:6], drel, AX.X, ALU.max))
            d = DV.mark(lambda e: e.tensor_reduce(fl[:, 6:7], drel, AX.X, ALU.min))
            DV.wait(a, b, c, d)
            b = DV.mark(lambda e: e.tensor_scalar(fl[:, 5:6], fl[:, 5:6], float(OW - 1), None, ALU.is_gt))
            DV.wait(a, b)
            a = DV.mark(lambda e: e.scalar_tensor_tensor(fl[:, 1:2], fl[:, 6:7], 0.0, fl[:, 5:6], ALU.is_lt, ALU.add))
            PE.wait(a, t_cst, free["PM1"])
            t = PE.mark(mm(P["PM1"][0:1, 0:3], ones[:, 0:1], fl[:, 0:3], True, True))
            DV.wait(t)
            t = free["PM1"] = DV.mark(lambda e: e.tensor_copy(flag_f[:, 0:3], P["PM1"][0:1, 0:3]))
            DV.wait(t)
            a = DV.mark(lambda e: e.tensor_scalar(flag_f[:, 3:4], flag_f[:, 2:3], float(S.e), None, ALU.not_equal))
            b = DV.mark(lambda e: e.tensor_tensor(flag_f[:, 0:1], flag_f[:, 0:1], flag_f[:, 1:2], ALU.add))
            DV.wait(a, b)
            t_prep["flag"] = DV.mark(lambda e: e.tensor_tensor(flag[:, :], flag_f[:, 0:1], flag_f[:, 3:4], ALU.add))

        DV.wait(t_nat)
        t_drel = DV.mark(lambda e: e.tensor_tensor(
            drel.rearrange("p (g j) -> p g j", j=4), dst_n[:, :].rearrange("p (g j) -> p g j", j=4),
            baseb.unsqueeze(2).to_broadcast([128, G, 4]), ALU.subtract))
        DV.wait(t_drel, t_c32)
        t_id16 = DV.mark(lambda e: e.tensor_copy(id16[:, :], idn))

        for g in range(EAN):
            load_ea(g)
        PO.wait(t_h0d, t_nat)
        NQ = -(-NB // 4)
        for t in range(4):
            onehot(t)
        quad_turn(0)
        for i in range(QE):
            if i == 1:
                windows_elementwise(0)
            quad_product(i)
            if i + 1 < QE:
                quad_turn(i + 1)

        TILE = 1.03
        clock = {"pe": 0.0, "dv": 0.0, "ac": 0.0}
        n_quad, n_prod = [0], [0]
        done_blocks = [0]
        conv_now = []
        conv_todo = [(gi, hh) for gi in range(LAST) for hh in range(NH)]
        fetched = {}
        half_built = []
        deferred = []

        def soon(f, at):
            deferred.append((at, f))

        def flush(now):
            for x in [x for x in deferred if x[0] <= now]:
                deferred.remove(x)
                x[1]()

        def next_job(now):
            if t_aggfree[0] is None:
                return []
            hn, an = quads[n_prod[0]][0:2] if n_prod[0] < len(quads) else (NH, 0)
            done = lambda f: soon(f, max(now, clock["pe"]) + 1.0)
            for hh in half_built:
                if fetched or hh < hn - (2 if an == 0 else 1):
                    continue
                for gi in range(LAST):
                    if (gi, hh) in conv_todo and S.qg[gi][1] <= done_blocks[0]:
                        q0, q1 = S.qg[gi]
                        wd = S.width(hh)
                        o = cb[:, (hh % 2) * CW + q0 * wd:(hh % 2) * CW + q1 * wd]
                        conv_todo.remove((gi, hh))
                        return conv1_job(gi, hh, 4, (None, t_c[hh], o), done)
            if n_prod[0] == len(quads):
                if len(t_row) < NH:
                    flush(1e9)
                for x in conv_todo[0:4]:
                    if x not in fetched:
                        fetched[x] = load_part(*x)
                for x in conv_todo[0:1]:
                    if S.qg[x[0]][1] <= done_blocks[0]:
                        conv_todo.remove(x)
                        return conv1_job(*x, 4, fetched[x], done)
            return []

        def product_step():
            i = n_prod[0]
            hh = quads[i][0]
            count_product(i)
            n_prod[0] += 1
            clock["pe"] += .43
            clock["ac"] += .95
            if quads[i][2] == S.windows(hh):
                soon(lambda: row_check(hh), clock["ac"] + 1.0)
                half_built.append(hh)

        def work(now, until):
            while True:
                flush(now)
                todo = n_prod[0] < len(quads)
                stop = todo and conv_now and quads[n_prod[0]][1] == 0
                if n_quad[0] < len(quads) and n_quad[0] - n_prod[0] < QN - 1 and clock["dv"] < until \
                        and (HW * quads[n_quad[0]][0] + quads[n_quad[0]][1]) // 128 in t_rk:
                    count_quad(n_quad[0])
                    n_quad[0] += 1
                    clock["dv"] += .95
                    if n_quad[0] - n_prod[0] == QN - 1 and not stop:
                        product_step()
                elif todo and n_quad[0] > n_prod[0] and not stop and max(clock["ac"], clock["pe"]) < until \
                        and (n_quad[0] == len(quads) or n_quad[0] - n_prod[0] >= QN - 1):
                    product_step()
                elif clock["pe"] < until:
                    if not conv_now:
                        conv_now.extend(next_job(now))
                    if not conv_now:
                        break
                    f, p = conv_now.pop(0)
                    f()
                    clock["pe"] += p
                    if not conv_now:
                        clock["dv"] += .4
                else:
                    break
            if n_prod[0] == len(quads):
                accs[:] = ["PV0", "PV1"]
                if "flag" not in t_prep and len(t_row) == NH:
                    make_flag()
                    clock["dv"] += 4

        stage = {}
        ends = {max(g for g in range(G) if S.bank[g] == k): k for k in range(NK)}

        def later(t, f):
            stage.setdefault(t, []).append(f)

        for g, k in ends.items():
            def fin(k=k):
                step_r(k)
                done_blocks[0] = step_blocks(k)[-1] + 1

            t = 4 * g + 3
            later(t + 1, lambda k=k: [add_hi(b) for b in step_blocks(k)])
            for d, f in ((3, step_x), (5, step_ln), (8, step_h1), (11, step_low), (13, step_turn)):
                later(t + d, lambda k=k, f=f: f(k))
            later(t + 16, fin)
        QP = 26
        for i in range(QE, NQ):
            later(QP * (i - QE + 1), lambda i=i: quad_turn(i))
            later(QP * (i - QE + 1) + 3, lambda i=i: quad_product(i))
        later(4, lambda: windows_elementwise(1))
        for w in range(WG):
            later(max(0, 20 * (w - 1)) if WG > 2 else 4 * w, lambda w=w: windows_turn(w))
            later(8 + 3 * w, lambda w=w: counts(w))
        at = 8 + 3 * WG
        for d, f in enumerate((spread_counts, scales, powers, scaled_weights, turn_counts, keep_biases, keep_counts)):
            later(at + 2 * d, f)
        later(QP * (NQ - QE) + 8, clear_agg)
        for t in range(min(NT, GAN)):
            gather(t)
            if t < WG:
                window_weight(t)
        t = 0
        while t < NT or any(x >= t for x in stage):
            now = t * TILE
            for x in clock:
                clock[x] = max(clock[x], now)
            if t % 4 == 0 and t:
                load_ea(t // 4 + EAN - 1)
            for f in stage.get(t, []):
                f()
                for x in clock:
                    clock[x] += .7
            if t < NT:
                onehot(t + 4)
                tile(t)
                if t + GAN < NT:
                    gather(t + GAN)
                clock["pe"] += .34
                clock["dv"] += .23
                if t % 4 == 3 and t // 4 in ends:
                    step_evac(ends[t // 4], t)
                    clock["dv"] += .6
                    clock["ac"] += .5
                work(now, now + TILE)
            else:
                flush(now)
            t += 1
        while n_prod[0] < len(quads) or conv_todo or conv_now:
            now += 1
            for x in clock:
                clock[x] = max(clock[x], now)
            work(now, now + 1)
        flush(1e9)
        work(0, 0)

        held = {hh: load_part(LAST, hh) for hh in range(min(NH, per))}
        for i in range(NH):
            if i == 1:
                load_half(0)
            for f, _ in conv1_job(LAST, i, NB, held[i], lambda f: f()):
                f()
            if i + per < NH:
                held[i + per] = load_part(LAST, i + per)
            if i >= 1:
                node1_y(i - 1)
            if i >= 2:
                node1_turn(i - 2)
            if i >= 3:
                node1_r(i - 3)
        load_half(1)
        node1_y(NH - 1)
        cut = [min(NB - 1, c) for c in (6, 12, 18, 24, 30)]
        todo = [lambda: node1_turn(NH - 2), lambda: node1_r(NH - 3), lambda: node1_turn(NH - 1),
                lambda: node1_r(NH - 2), lambda: node1_r(NH - 1)]
        for hh in range(NH):
            hooks = {}
            if hh == 0:
                for q, f in zip(cut, todo):
                    hooks.setdefault(q, []).append(f)
                hooks = {q: (lambda fs=fs: [f() for f in fs]) for q, fs in hooks.items()}
            else:
                hooks = {min(NB - 1, 8): lambda hh=hh: node2_y(hh - 1)}
            conv2_half(hh, hooks)
            load_half(hh + 2)
        node2_y(NH - 1)
        SP.wait(t_st[NH - 1], t_st.get(NH - 2))

        g1, g2 = xs[:, :, :].rearrange("p b f -> p (b f)"), agg[:, :]
        places = {}
        at = 0
        for n, w in (("C", 129), ("msg", 257), ("rsum", 258), ("eq", 128), ("eqw", 128), ("junk", 128)):
            places[n] = g1[:, at:at + w]
            at += w
        at = 0
        for n, w in (("nA", 258), ("nX", 128), ("nH", 128), ("tT", 512), ("o1", 128)):
            places[n] = g2[:, at:at + w]
            at += w
        places |= {"drow": l0[:, 0:128].bitcast(I32), "col": l0[:, 128:136], "coli": l0[:, 136:140].bitcast(I32),
                   "s1": l0[:, 140:160], "o2": l0[:, 160:288],
                   "h0_d": h0_d, "idn": idn, "bb": bb,
                   "W": {"WI": WI, "WJ": WJ, "WE": WE, "WS": WS, "W1L": W1L, "W1R": W1R, "W2L": W2L, "W2R": W2R}}
        loops = general_path(nc, T, S, out, sem, places, P)
        ends_ = [(q.sem, q.n) for q in (PE, DV, AC, PO)] + [t_st[NH - 1], t_st[NH - 2]]

        def finish(e, q, name):
            q.wait(t_prep["flag"])
            for f in q.ops:
                f(e)
            v = e.value_load(flag[0:1, 0:1], min_val=0, max_val=1 << 20)
            with e.If(v != 0):
                for x, n in ends_:
                    e.wait_ge(x, n)
                for L in loops:
                    if not L.ops[name]:
                        continue
                    if L.rounds == 1:
                        for f in L.ops[name]:
                            f(e, 0)
                        continue
                    with e.Fori(0, L.rounds) as i:
                        for f in L.ops[name]:
                            f(e, i)
            e.end_ifs()

        block = ctx.enter_context(nc.Block())

        @block.sync
        def _(e):
            finish(e, SP, "SP")

        @block.gpsimd
        def _(e):
            finish(e, PO, "PO")

        @block.scalar
        def _(e):
            finish(e, AC, "AC")

        @block.tensor
        def _(e):
            finish(e, PE, "PE")

        @block.vector
        def _(e):
            finish(e, DV, "DV")


def arrays_of(S, x, src, dst, edge_attr_128, edge_weight, L0_gnn_W_msg, L0_gnn_W_self,
              L1_gnn_W1_l, L1_gnn_b1_l, L1_gnn_W1_r, L1_gnn_W2_l, L1_gnn_b2_l, L1_gnn_W2_r):
    import numpy as np

    def rows(a, n, fill=0):
        a = np.asarray(a)
        o = np.full((n,) + a.shape[1:], fill, a.dtype)
        o[:len(a)] = a
        return o

    def natural(a):
        return np.ascontiguousarray(a.reshape(S.g, 128, 4).transpose(1, 0, 2).reshape(128, S.nt))

    A = {"x": rows(x, S.np), "ea": rows(edge_attr_128, S.ep)}
    A["src"], A["dst"], A["ew"] = rows(src, S.ep), rows(dst, S.ep, S.np - 1), rows(edge_weight, S.ep)
    for k in ("src", "dst", "ew"):
        A[k + "_n"] = natural(A[k])
    A["heads"] = np.ascontiguousarray(rows(A["dst"][::64], S.hb * 128, S.np - 1).reshape(S.hb, 128).T)
    Wm = np.asarray(L0_gnn_W_msg)
    A["WI"], A["WJ"], A["WE"] = (np.ascontiguousarray(Wm[128 * i:128 * i + 128]) for i in range(3))
    A["WS"] = np.asarray(L0_gnn_W_self)
    A["W1L"], A["W1R"], A["W2L"], A["W2R"] = (np.ascontiguousarray(np.asarray(w).T)
                                             for w in (L1_gnn_W1_l, L1_gnn_W1_r, L1_gnn_W2_l, L1_gnn_W2_r))
    A["W1Ln"], A["W1Rn"] = np.asarray(L1_gnn_W1_l), np.asarray(L1_gnn_W1_r)
    A["b1"], A["b2"] = np.asarray(L1_gnn_b1_l), np.asarray(L1_gnn_b2_l)
    i128 = np.arange(128)
    c16 = np.concatenate([i128, np.repeat(i128 + 1, 4), np.repeat(np.arange(1, S.key + 1), 4)])
    A["iow"] = np.tile(np.arange(128 * S.wg).astype(np.float16), (128, 1))
    A["c16"] = np.tile(c16.astype(np.float16), (128, 1))
    w5 = D * (i128[:, None] + 128 * np.arange(S.wg)[None, :])
    A["c32"] = np.concatenate([np.eye(128), w5], 1).astype(np.float32)
    A["gen"] = np.concatenate([np.tri(128, k=-1), S.np + i128[:, None]], 1).astype(np.float32)
    A["base"] = np.tile(np.array(S.base, np.float32), (128, 1))
    return A


def kernel(**inputs):
    import numpy as _np
    import concourse.bacc as _bacc
    from concourse import mybir as _mybir
    from concourse.bass_utils import run_bass_kernel_spmd as _run

    S = FULL
    A = arrays_of(S, **{k: _np.asarray(v) for k, v in inputs.items()})
    nc = _bacc.Bacc("TRN2", target_bir_lowering=False, num_devices=1)
    arrays, T = {}, {}
    for name, a in A.items():
        a = _np.ascontiguousarray(a)
        arrays[f"in_{name}_dram"] = a
        T[name] = nc.dram_tensor(f"in_{name}_dram", a.shape, _mybir.dt.from_np(a.dtype), kind="ExternalInput").ap()
    out = nc.dram_tensor("out_0_dram", (S.np, 128), F32, kind="ExternalOutput").ap()
    gnn_kernel(nc, T, S, out)
    r = _run(nc, [arrays], core_ids=[0])
    return r.results[0]["out_0_dram"][:S.n]
```

```python
import concourse.bass as bass
from concourse import mybir
from contextlib import ExitStack

F32 = mybir.dt.float32
F16 = mybir.dt.float16
FP8 = mybir.dt.float8e4
I32 = mybir.dt.int32
ALU = mybir.AluOpType
ACT = mybir.ActivationFunctionType
AX = mybir.AxisListType

D = 5
SL = 128
HW = 64
OW = 96
STRAY = 30
STEP = 384
HSCALE = 4096.0


class Shape:

    def __init__(self, n, e, groups, dense):
        self.n, self.e = n, e
        self.nb = -(-n // 128)
        self.np = self.nb * 128
        self.g = -(-e // 512)
        self.ep = self.g * 512
        self.nt = self.g * 4
        self.nw = n // D
        self.wg = -(-self.nw // 128)
        self.hb = -(-(self.ep // 64) // 128)
        self.nh = -(-self.nw // HW)
        self.key = D * self.nb
        self.kx = self.key + D
        self.qg = groups
        assert n % (2 * D) == 0 and self.ep - e >= 128 and 2 * self.kx <= 512
        self.base, self.wid = [], []
        for g in range(self.g):
            u = min(1.0, (512 * g + 256) / e)
            half = min(OW // 2, round(19 + STRAY * n ** .5 / 79 * max(.2, 2 * (u * (1 - u)) ** .5)))
            mid = min(round((512 * g + 256) * n / e), n)
            lo, hi = max(0, mid - half), min(self.np, mid + half)
            if g == self.g - 1:
                lo, hi = self.np - OW, self.np
            self.base.append(lo)
            self.wid.append(hi - lo)
        self.bank = [b // STEP for b in self.base]
        self.dense = dense
        self.g2 = min(g for g in range(self.g) if self.base[g] + self.wid[g] > 128 * dense)
        self.from2 = 128 * dense - 128
        self.bank2 = {g: (max(self.base[g], self.from2) - self.from2) // STEP for g in range(self.g2, self.g)}
        assert self.base[self.g2] >= self.from2

    def windows(self, hh):
        return min(HW, self.nw - HW * hh)

    def width(self, hh):
        return D * self.windows(hh)


FULL = Shape(6250, 106250, [(0, 6), (6, 15), (15, 24), (24, 33), (33, 39), (39, 45), (45, 49)], 36)


class Queue:

    due = {}

    def __init__(self, sem, cost):
        self.sem, self.n, self.ops, self.seen = sem, 0, [], {}
        self.at, self.cost = 0.0, cost

    def wait(self, *tokens):
        for t in tokens:
            if t is None:
                continue
            sem, v = t
            if self.seen.get(id(sem), 0) < v:
                self.seen[id(sem)] = v
                self.ops.append(lambda e, sem=sem, v=v: e.wait_ge(sem, v))
                self.at = max(self.at, self.due.get((id(sem), v), 0.0) + 0.1)

    def run(self, f, cost=None):
        self.at += cost or self.cost
        self.ops.append(f)

    def mark(self, f, cost=None):
        self.n += 1
        self.at += cost or self.cost
        self.due[id(self.sem), self.n] = self.at
        self.ops.append(lambda e: f(e).then_inc(self.sem, 1))
        return (self.sem, self.n)

    def dma(self, f, ds, cost=2.5):
        ds.n += 16
        self.at += self.cost
        self.due[id(ds.sem), ds.n] = self.at + cost
        self.ops.append(lambda e: f(e).then_inc(ds.sem, 16))
        return (ds.sem, ds.n)


class DmaSem:
    def __init__(self, sem):
        self.sem, self.n = sem, 0


class Steps:

    def __init__(self, rounds):
        self.rounds = rounds
        self.ops = {x: [] for x in ("SP", "PO", "AC", "PE", "DV")}

    def do(self, engine, f, after=None, then=None):
        ops = self.ops[engine]
        if after is not None:
            link, n = after
            ops.append(lambda e, i: e.wait_ge(link, n))
            ops.append(lambda e, i: e.sem_clear(link))
        if then is None:
            ops.append(f)
        else:
            to, by = then
            ops.append(lambda e, i: f(e, i).then_inc(to, by))


def general_path(nc, T, S, out, sem, M, P):
    NB, NP, NT = S.nb, S.np, S.nt
    rows = NP + 128
    acc = [nc.dram_tensor(f"acc{i}_d", [rows, w], F32).ap() for i, w in enumerate((258, 128, 128))]
    x1_d, h1_d, h2_d = (nc.dram_tensor(n, [NP, 128], F32).ap() for n in ("x1_d", "h1_d", "h2g_d"))
    links = ("go", "to_po", "to_dv", "gathered", "eq_pe", "sums", "dv_po", "dv_pe", "dv_sp", "dv_ac", "dv", "po_dma",
             "ac_dv", "ac_sp", "ac", "pe", "stored")
    (go, to_po, to_dv, gathered, eq_pe, sums, dv_po, dv_pe, dv_sp, dv_ac, dv, po_dma,
     ac_dv, ac_sp, ac, pe, stored) = (sem("g_" + n) for n in links)
    src_r, dst_r, ew_r = (T[k].rearrange("(n o) -> n o", o=1) for k in ("src", "dst", "ew"))
    dst_c = T["dst"].rearrange("(o n) -> o n", o=1)
    C, msg, rsum, eq, eqw, junk, drow = M["C"], M["msg"], M["rsum"], M["eq"], M["eqw"], M["junk"], M["drow"]
    col, coli = M["col"], M["coli"]
    low, dummy = C[:, 0:128], C[:, 128:129]
    ds = bass.ds
    loops = []

    L = Steps(1)
    L.do("SP", lambda e, i: e.dma_start(C, T["gen"]), then=(to_dv, 16))
    L.do("DV", lambda e, i: e.memset(rsum, 0.0), (to_dv, 16), (dv, 1))
    L.do("DV", lambda e, i: e.memset(msg[:, 256:257], 1.0), (dv, 1), (dv_sp, 1))
    for n, a in enumerate(acc):
        w = a.shape[1]
        L.do("SP", lambda e, i, a=a, w=w: e.dma_start(
            a.rearrange("(b p) f -> p b f", p=128), rsum[:, 0:w].unsqueeze(1).to_broadcast([128, rows // 128, w])),
            (dv_sp, 1) if n == 0 else None, (stored, 16))
    L.do("SP", lambda e, i: e.sem_inc(go, 1), (stored, 48))
    loops.append(L)

    def settled(L, then):
        L.do("PO", lambda e, i: e.wait_ge(po_dma, 16))
        L.do("PO", lambda e, i: e.dma_reset(range(po_dma.num, po_dma.num + 1)))
        L.do("PO", lambda e, i: e.sem_clear(po_dma))
        L.do("PO", lambda e, i: e.sem_inc(then, 1))

    def edges(table, a, first):
        w = 258 if first else 128
        L = Steps(NT)
        tile = lambda v, i: v[ds(i * 128, 128), :]
        L.do("SP", lambda e, i: e.dma_start(coli[:, 0:1], tile(src_r, i)), (go, 1), (to_po, 16))
        L.do("SP", lambda e, i: e.dma_start(coli[:, 1:2], tile(dst_r, i)), None, (to_po, 16))
        L.do("SP", lambda e, i: e.dma_start(col[:, 0:1], tile(ew_r, i)), None, (to_po, 16))
        L.do("SP", lambda e, i: e.dma_start(drow, dst_c[:, ds(i * 128, 128)].to_broadcast([128, 128])), None, (to_po, 16))
        if first:
            L.do("SP", lambda e, i: e.dma_start(msg[:, 128:256], tile(T["ea"], i)), None, (to_po, 16))
        L.do("PO", lambda e, i: e.indirect_dma_start(msg[:, 0:128], None, table, bass.IndirectOffsetOnAxis(coli[:, 0:1], 0)),
             (to_po, 80 if first else 64), (po_dma, 16))
        settled(L, gathered)
        L.do("DV", lambda e, i: e.tensor_copy(col[:, 1:2], coli[:, 1:2]), (gathered, 1), (dv, 1))
        L.do("DV", lambda e, i: e.tensor_scalar(eq, drow, col[:, 1:2], 0.0, ALU.is_equal, ALU.add,
                                                accum_out=rsum[:, 257:258]), (dv, 1), (dv, 1))
        L.do("DV", lambda e, i: e.scalar_tensor_tensor(junk, drow, col[:, 1:2], low, ALU.is_equal, ALU.mult,
                                                       accum_out=col[:, 2:3]), (dv, 1), (dv, 1))
        L.do("DV", lambda e, i: e.tensor_tensor(col[:, 3:4], dummy, col[:, 1:2], ALU.subtract), (dv, 1), (dv, 1))
        L.do("DV", lambda e, i: e.scalar_tensor_tensor(col[:, 4:5], col[:, 2:3], 0.5, col[:, 3:4], ALU.is_gt, ALU.mult),
             (dv, 1), (dv, 1))
        L.do("DV", lambda e, i: e.tensor_tensor(coli[:, 2:3], col[:, 4:5], col[:, 1:2], ALU.add), (dv, 1),
             (dv, 1) if first else (eq_pe, 1))
        if first:
            L.do("DV", lambda e, i: e.tensor_scalar(eqw, eq, col[:, 0:1], None, ALU.mult), (dv, 1), (eq_pe, 1))
            L.do("PE", lambda e, i: e.matmul(P["PA"][:, 0:257], eqw, msg[:, 0:257], start=True, stop=True), (eq_pe, 1), (sums, 1))
            L.do("DV", lambda e, i: e.tensor_copy(rsum[:, 0:257], P["PA"][:, 0:257]), (sums, 1), (dv_po, 1))
        else:
            L.do("PE", lambda e, i: e.matmul(P["PA"][:, 0:128], eq, msg[:, 0:128], start=True, stop=True), (eq_pe, 1), (sums, 1))
            L.do("DV", lambda e, i: e.tensor_copy(rsum[:, 0:128], P["PA"][:, 0:128]), (sums, 1), (dv_po, 1))
        L.do("PO", lambda e, i: e.indirect_dma_start(a, bass.IndirectOffsetOnAxis(coli[:, 2:3], 0), rsum[:, 0:w], None,
                                                     compute_op=ALU.add), (dv_po, 1), (po_dma, 16))
        settled(L, go)
        loops.append(L)

    nA, nX, nH, tT, o1, o2, s1 = M["nA"], M["nX"], M["nH"], M["tT"], M["o1"], M["o2"], M["s1"]
    W, bb, idn = M["W"], M["bb"], M["idn"]
    blk = lambda v, i: v[ds(i * 128, 128), :]

    def turned(L, parts, weights, then):
        m = len(parts)
        for j, v in enumerate(parts):
            L.do("PE", lambda e, i, j=j, v=v: e.transpose(P["PA"][:, 128 * j:128 * j + 128], v, idn),
                 (dv_pe, 1) if j == 0 else None, (pe, 1) if j == m - 1 else None)
        L.do("DV", lambda e, i: e.tensor_copy(tT[:, 0:128 * m], P["PA"][:, 0:128 * m]), (pe, 1), (dv_pe, 1))
        for j, w in enumerate(weights):
            L.do("PE", lambda e, i, j=j, w=w: e.matmul(P["PB"][:, 0:128], tT[:, 128 * j:128 * j + 128], w,
                                                       start=j == 0, stop=j == m - 1),
                 (dv_pe, 1) if j == 0 else None, then if j == m - 1 else None)

    edges(M["h0_d"], acc[0], True)
    L = Steps(NB)
    L.do("SP", lambda e, i: e.dma_start(nA, blk(acc[0], i)), (go, 1), (to_dv, 16))
    L.do("SP", lambda e, i: e.dma_start(nX, blk(T["x"], i)), None, (to_dv, 16))
    L.do("SP", lambda e, i: e.dma_start(nH, blk(M["h0_d"], i)), None, (to_dv, 16))
    L.do("DV", lambda e, i: e.tensor_scalar(o1, nH, nA[:, 256:257], None, ALU.mult), (to_dv, 48), (dv_pe, 1))
    turned(L, (nA[:, 0:128], nA[:, 128:256], o1, nH), (W["WJ"], W["WE"], W["WI"], W["WS"]), (sums, 1))
    L.do("DV", lambda e, i: e.tensor_tensor(o1, P["PB"][:, 0:128], nX, ALU.add), (sums, 1), (dv, 1))
    L.do("DV", lambda e, i: e.bn_stats(s1[:, 0:6], o1), (dv, 1), (dv, 1))
    L.do("DV", lambda e, i: e.bn_aggr(s1[:, 6:8], s1[:, 0:6]), (dv, 1), (dv, 1))
    L.do("DV", lambda e, i: e.tensor_scalar(s1[:, 8:9], s1[:, 7:8], 1e-5, None, ALU.add), (dv, 1), (dv_ac, 1))
    L.do("AC", lambda e, i: e.activation(s1[:, 9:10], s1[:, 8:9], ACT.Sqrt), (dv_ac, 1), (ac_dv, 1))
    L.do("DV", lambda e, i: e.reciprocal(s1[:, 10:11], s1[:, 9:10]), (ac_dv, 1), (dv, 1))
    L.do("DV", lambda e, i: e.tensor_scalar(s1[:, 11:12], s1[:, 10:11], HSCALE, None, ALU.mult), (dv, 1), (dv, 1))
    L.do("DV", lambda e, i: e.scalar_tensor_tensor(s1[:, 12:13], s1[:, 6:7], -1.0, s1[:, 11:12], ALU.mult, ALU.mult),
         (dv, 1), (dv_ac, 1))
    L.do("AC", lambda e, i: e.activation(o2, o1, ACT.Relu, bias=s1[:, 12:13], scale=s1[:, 11:12]), (dv_ac, 1), (ac_sp, 1))
    L.do("SP", lambda e, i: e.dma_start(blk(x1_d, i), o1), (ac_sp, 1), (stored, 16))
    L.do("SP", lambda e, i: e.dma_start(blk(h1_d, i), o2), None, (stored, 16))
    L.do("SP", lambda e, i: e.sem_inc(go, 1), (stored, 32))
    loops.append(L)

    def conv(a, h_d, wl, wr, by, bias):
        L = Steps(NB)
        L.do("SP", lambda e, i: e.dma_start(nA[:, 0:128], blk(a, i)), (go, 1), (to_dv, 16))
        L.do("SP", lambda e, i: e.dma_start(nA[:, 256:258], acc[0][ds(i * 128, 128), 256:258]), None, (to_dv, 16))
        L.do("SP", lambda e, i: e.dma_start(nX, blk(x1_d, i)), None, (to_dv, 16))
        L.do("SP", lambda e, i: e.dma_start(nH, blk(h_d, i)), None, (to_dv, 16))
        L.do("DV", lambda e, i: e.tensor_scalar(s1[:, 0:1], nA[:, 257:258], 1.0, None, ALU.max), (to_dv, 64), (dv, 1))
        L.do("DV", lambda e, i: e.reciprocal(s1[:, 1:2], s1[:, 0:1]), (dv, 1), (dv, 1))
        L.do("DV", lambda e, i: e.tensor_scalar(o2, nA[:, 0:128], s1[:, 1:2], by, ALU.mult, ALU.mult), (dv, 1), (dv_pe, 1))
        turned(L, (o2, nH), (wl, wr), (sums, 1))
        L.do("DV", lambda e, i: e.tensor_tensor(o1, P["PB"][:, 0:128], bias, ALU.add), (sums, 1), (dv, 1))
        loops.append(L)
        return L

    edges(h1_d, acc[1], False)
    L = conv(acc[1], h1_d, W["W1L"], W["W1R"], 1.0 / HSCALE, bb[:, 0, :])
    L.do("DV", lambda e, i: e.tensor_scalar(o2, o1, 0.0, None, ALU.max), (dv, 1), (dv_sp, 1))
    L.do("SP", lambda e, i: e.dma_start(blk(h2_d, i), o2), (dv_sp, 1), (stored, 16))
    L.do("SP", lambda e, i: e.sem_inc(go, 1), (stored, 16))

    edges(h2_d, acc[2], False)
    L = conv(acc[2], h2_d, W["W2L"], W["W2R"], 1.0, bb[:, 1, :])
    L.do("DV", lambda e, i: e.tensor_reduce(s1[:, 2:3], o1, AX.X, ALU.max, negate=True), (dv, 1), (dv_ac, 1))
    L.do("AC", lambda e, i: e.activation(o2, o1, ACT.Exp, bias=s1[:, 2:3], accum_out=s1[:, 3:4]), (dv_ac, 1), (ac, 1))
    L.do("AC", lambda e, i: e.activation(s1[:, 4:5], s1[:, 3:4], ACT.Ln), (ac, 1), (ac_dv, 1))
    L.do("DV", lambda e, i: e.tensor_tensor(s1[:, 5:6], s1[:, 4:5], s1[:, 2:3], ALU.subtract), (ac_dv, 1), (dv, 1))
    L.do("DV", lambda e, i: e.scalar_tensor_tensor(o2, o1, s1[:, 5:6], nX, ALU.subtract, ALU.add), (dv, 1), (dv_sp, 1))
    L.do("SP", lambda e, i: e.dma_start(blk(out, i), o2), (dv_sp, 1), (stored, 16))
    L.do("SP", lambda e, i: e.sem_inc(go, 1), (stored, 16))
    L = Steps(1)
    L.do("SP", lambda e, i: e.wait_ge(go, 1))
    loops.append(L)
    return loops


def gnn_kernel(nc, T, S, out):
    NB, NP, G, NT, WG, HB = S.nb, S.np, S.g, S.nt, S.wg, S.hb
    KEY, KX, NH, NW = S.key, S.kx, S.nh, S.nw
    ctx = ExitStack()
    with ctx:
        def sb(name, shape, dt=F32):
            return ctx.enter_context(nc.sbuf_tensor(name, shape, dt))

        def sem(name):
            return ctx.enter_context(nc.semaphore(name))

        def dsem(name):
            return DmaSem(sem(name))

        h0_d = nc.dram_tensor("h0_d", [NP, 128], F32).ap()
        h2_d = nc.dram_tensor("h2_d", [NP, 256], F16).ap()
        cs_d = nc.dram_tensor("cs_d", [2, WG * 128 * D], F32).ap()
        c_d = nc.dram_tensor("c_d", [NH, 128, NB * HW * D], FP8).ap()

        xs = sb("xs", [128, NB, 128])
        agg = sb("agg", [128, NP])
        h0 = agg[:, :].rearrange("p (b f) -> p b f", f=128)
        R = sb("R", [128, NB, 128])
        h1r = sb("h1r", [128, NB * 128])
        h1 = h1r[:, :].bitcast(F16).rearrange("p (a b f) -> p a b f", a=2, f=128)
        l0 = sb("l0", [128, max(NB * 128, 5120 + 96 * 12)])
        h2 = l0[:, 0:NB * 128].bitcast(F16).rearrange("p (b a f) -> p a b f", a=2, f=128)
        EAN, GAN, OHN, QN = 6, 16, 12, 3
        ea = l0[:, 0:3072].rearrange("p (n j f) -> p n j f", n=EAN, j=4)
        ga = l0[:, 3072:5120].rearrange("p (n f) -> p n f", n=GAN)
        oh = l0[:, 5120:5120 + OW * OHN].rearrange("p (n f) -> p n f", n=OHN)
        CW = (NB + 1) * HW * D
        cbr = sb("cbr", [128, CW // 2])
        cb = cbr[:, :].bitcast(FP8)
        win = h1r[:, :] if NB >= 3 * WG else sb("win", [128, 3 * 128 * WG])[:, :]
        wsrc = win[:, 0:128 * WG].bitcast(I32)
        wdst = win[:, 128 * WG:256 * WG].bitcast(I32)
        wew = win[:, 256 * WG:384 * WG]
        src_n = sb("src_s", [128, NT], I32)
        dst_n = sb("dst_s", [128, NT], I32)
        drel = dst_n[:, :].bitcast(F32)
        ew_n = sb("ew_s", [128, NT])
        c16 = sb("c16_s", [128, 128 + 128 * 4 + KEY * 4], F16)
        iota = c16[:, 0:OW]
        IR = c16[:, 128:640].rearrange("p (r w) -> p r w", w=4)
        IK = c16[:, 640:640 + 4 * KEY].rearrange("p (r w) -> p r w", w=4)
        early = R[:, :, :].rearrange("p b f -> p (b f)")
        early = early[:, NB * 128 - 128 * WG - 2 * G:]
        baseb = early[:, 128 * WG:128 * WG + G]
        lastb = early[:, 128 * WG + G:128 * WG + 2 * G]
        QE = min(-(-NB // 4), 5)
        WH = 128 * ((WG + 1) // 2)
        if NB * 128 - 128 * WG - 2 * G - 512 * QE >= 3 * WH:
            tmp = R[:, :, :].rearrange("p b f -> p (b f)")[:, 512 * QE:512 * QE + 3 * WH]
        else:
            tmp = sb("tmp", [128, 3 * WH])
        tmp = tmp.rearrange("p (n k) -> p n k", n=3)
        iow = early[:, 0:64 * WG].bitcast(F16)
        d64 = early[:, 64 * WG:128 * WG].bitcast(I32).rearrange("p (w s) -> p w s", s=64)
        c32 = sb("c32_s", [128, 128 + WG])
        idn = c32[:, 0:128]
        w5 = c32[:, 128:128 + WG]
        id16 = sb("id16", [128, 128], F16)
        ones16 = sb("ones16", [128, 1], F16)
        zero16 = sb("zero16", [128, 128], F16)
        any16 = c16[:, 128:640]
        ones = sb("ones", [128, 128])
        heads = sb("heads_s", [128, HB], I32)
        hs = sb("hs", [128, HB])
        rT = sb("rT", [128, 128 * WG], F16)
        kT = sb("kT", [128, 128 * WG], F16)
        ohr = sb("ohr", [128, QN, 128, 4], F16)
        ohk = sb("ohk", [128, QN, KX, 4], F16)
        AT = sb("AT", [128, 2, 512])
        BT = sb("BT", [128, 2, 512])
        W = sb("W", [128, 8, 128])
        WI, WJ, WE, WS, W1L, W1R, W2L, W2R = (W[:, i, :] for i in range(8))
        bcol = sb("bcol", [128, 1])
        brow = sb("brow", [1, 2, 128])
        bb = sb("bb", [128, 2, 128])
        H = sb("H", [128, 2, 384])
        wn = H[:, 0, 0:256].rearrange("p (a f) -> p a f", a=2)
        diag = H[:, 1, 0:128]
        HT = sb("HT", [128, 2, 512])
        cmp = HT[:, :, :].bitcast(F16).rearrange("p a k -> p (a k)")
        cmp = (cmp, AT[:, :, :].rearrange("p a k -> p (a k)").bitcast(F16))
        st6 = sb("st6", [128, NB, 6])
        mv = sb("mv", [128, NB, 2])
        sd = sb("sd", [128, NB])
        rs = sb("rs", [128, NB])
        nb_ = sb("nb_", [128, NB])
        kk = sb("kk", [128, WG])
        idx1 = sb("idx1", [128, WG], I32)
        idx2 = sb("idx2", [128, WG], I32)
        c64 = sb("c64", [128, WG])
        cs = sb("cs", [128, 2, WG, D])
        csr = H[0:NB, 1, 128:384].rearrange("p (a f) -> p a f", a=2)
        inv = sb("inv", [128, 2, NB])
        sw = sb("sw", [128, NB])
        sc = sb("sc", [128, 8])
        sci = sb("sci", [128, 2], I32)
        fl = sb("fl", [128, 8])
        flag_f = sb("flag_f", [1, 4])
        flag = sb("flag", [1, 1], I32)
        sm = sb("sm", [128, 4, 4])
        rmax = sb("rmax", [128, NH])
        junk = sb("junk", [128, HW * D], F16)

        names = ["PA", "PB", "PC0", "PC1", "PV0", "PV1", "PM0", "PM1"]
        P = {n: ctx.enter_context(nc.psum_tensor(n, [128, 512], F32)) for n in names}
        free = dict.fromkeys(names)

        Queue.due = {}
        PE, DV, AC, PO, SP = (Queue(sem("s_" + n), c) for n, c in (
            ("pe", .23), ("dv", .2), ("ac", .42), ("po", 1.04), ("sp", .06)))

        def mm(o, l, r, start, stop):
            return lambda e: e.matmul(o, l, r, start=start, stop=stop, skip_group_check=True)

        LATER = (None, 0)
        held, tasks = set(), []

        SPAN = .25

        def start(g, favour):
            tasks.append([favour, g, next(g)])

        def begin(x):
            q, needs, takes = x[2]
            if held.intersection(takes):
                return 1e9
            ts = needs()
            if LATER in ts:
                return 1e9
            return max([q.at, *(t if type(t) is float else Queue.due.get((id(t[0]), t[1]), 0.0) for t in ts if t)])

        def run_tasks():
            while tasks:
                at = [(begin(x), -x[0], n) for n, x in enumerate(tasks)]
                first = min(at)
                assert first[0] < 1e8, [y[1].__name__ for y in tasks]
                q = tasks[first[2]][2][0]
                x = tasks[min((-tasks[n][0], b, n) for b, _, n in at if b < first[0] + SPAN and tasks[n][2][0] is q)[2]]
                held.update(x[2][2])
                try:
                    x[2] = next(x[1])
                except StopIteration:
                    tasks.remove(x)

        def finish_now(g):
            for _, needs, takes in g:
                assert LATER not in needs() and not held.intersection(takes)
                held.update(takes)

        d_a, d_c, d_nat, d_w = dsem("d_a"), dsem("d_c"), dsem("d_nat"), dsem("d_w")
        SP.dma(lambda e: e.dma_start(heads[:, :], T["heads"]), d_a)
        t_head = SP.dma(lambda e: e.dma_start(iow, T["iow"]), d_a)
        XP = 7
        pieces = [(b, min(NB, b + XP)) for b in range(0, NB, XP)]
        xv = T["x"].rearrange("(b p) f -> p b f", p=128)
        t_x = []
        for i, (b0, b1) in enumerate(pieces):
            t_x.append(SP.dma(lambda e, b0=b0, b1=b1: e.dma_start(xs[:, b0:b1, :], xv[:, b0:b1, :]), dsem(f"d_x{i}"), 4 + 2.3 * i))
        SP.dma(lambda e: e.dma_start(c32[:, :], T["c32"]), d_c)
        t_c32 = SP.dma(lambda e: e.dma_start(c16[:, :], T["c16"]), d_c)
        AC.dma(lambda e: e.dma_start(dst_n[:, :], T["dst_n"]), d_nat)
        AC.dma(lambda e: e.dma_start(early[:, 128 * WG:128 * WG + 2 * G], T["base"]), d_nat)
        AC.dma(lambda e: e.dma_start(ew_n[:, :], T["ew_n"]), d_nat)
        t_nat = AC.dma(lambda e: e.dma_start(src_n[:, :], T["src_n"]), d_nat)
        for i, w in enumerate(["WI", "WJ", "WE", "WS", "W1L", "W1R", "W2L", "W2R"]):
            AC.dma(lambda e, i=i, w=w: e.dma_start(W[:, i, :], T[w]), d_w)
        AC.dma(lambda e: e.dma_start(wn[:, 0, :], T["W1Ln"]), d_w)
        AC.dma(lambda e: e.dma_start(wn[:, 1, :], T["W1Rn"]), d_w)
        AC.dma(lambda e: e.dma_start(bcol[:, :], T["b1"].rearrange("(p o) -> p o", o=1)), d_w)
        AC.dma(lambda e: e.dma_start(brow[:, 0, :], T["b1"].rearrange("(o p) -> o p", o=1)), d_w)
        t_w = AC.dma(lambda e: e.dma_start(brow[:, 1, :], T["b2"].rearrange("(o p) -> o p", o=1)), d_w)

        PO.run(lambda e: e.memset(ones16[:, :], 1.0))
        PO.run(lambda e: e.memset(zero16[:, :], 0.0))
        PO.run(lambda e: e.memset(cs[:, :, :, :], 0.0))
        PO.run(lambda e: e.memset(fl[:, :], 0.0))
        PO.run(lambda e: e.memset(ohk[:, :, KEY + 1:KX, :], 0.0))
        PO.run(lambda e: e.memset(ohk[:, :, KEY:KEY + 1, :], 1.0))
        t_cst = PO.mark(lambda e: e.memset(ones[:, :], 1.0))

        DV.wait(t_head)
        t = DV.mark(lambda e: e.tensor_scalar(hs[:, :], heads[:, :], 0.5, 1.0 / D, ALU.add, ALU.mult))
        DV.wait(t)
        PE.wait(t_cst, t_head)
        PE.run(mm(P["PV0"][:, 0:WG], zero16[:, :], iow[:, 0:WG], True, False))
        t_pe = [None, None]
        for i in range(HB):
            DV.wait(t_pe[i % 2])
            c = cmp[i % 2][:, 0:128 * WG]
            t = DV.mark(lambda e, i=i, c=c: e.tensor_scalar(c, iow, hs[:, i:i + 1], None, ALU.is_gt), .465)
            PE.wait(t)
            for w in range(WG):
                f = mm(P["PV0"][:, w:w + 1], c[:, 128 * w:128 * w + 128], ones16[:, :], False, i == HB - 1)
                if w < WG - 1:
                    PE.run(f, .027)
            t_pe[i % 2] = PE.mark(f, .027)
        DV.wait(t_pe[(HB - 1) % 2])
        t = DV.mark(lambda e: e.tensor_scalar(kk[:, :], P["PV0"][:, 0:WG], -1.0, 0.0, ALU.add, ALU.max))
        free["PV0"] = t
        DV.wait(t)
        t_i1 = DV.mark(lambda e: e.tensor_scalar(idx1[:, :], kk[:, :], 64.0, None, ALU.mult))

        dst_r = T["dst"].rearrange("(n o) -> n o", o=1)
        src_r = T["src"].rearrange("(n o) -> n o", o=1)
        ew_r = T["ew"].rearrange("(n o) -> n o", o=1)

        def fetch(dst, tab, idx, w, ds):
            return PO.dma(lambda e: e.indirect_dma_start(dst, None, tab, bass.IndirectOffsetOnAxis(idx[:, w:w + 1], 0)), ds)

        d_h = dsem("d_h")
        PO.wait(t_i1)
        for w in range(WG):
            t_d64 = fetch(d64[:, w, :], dst_r, idx1, w, d_h)

        def window_starts():
            nonlocal t_c64
            DV.wait(t_d64, t_c32)
            for w in range(WG):
                t = DV.mark(lambda e, w=w: e.tensor_scalar(d64[:, w, :], d64[:, w, :], w5[:, w:w + 1], 0.0,
                                                           ALU.is_lt, ALU.add, accum_out=c64[:, w:w + 1]))
            DV.wait(t)
            t = t_c64 = DV.mark(lambda e: e.scalar_tensor_tensor(kk[:, :], kk[:, :], 64.0, c64[:, :], ALU.mult, ALU.add))
            DV.wait(t)
            t_i2 = DV.mark(lambda e: e.tensor_scalar(idx2[:, :], kk[:, :], float(S.ep - SL), None, ALU.min))
            PO.wait(t_i2)
            for w in range(WG):
                fetch(wsrc[:, 128 * w:128 * w + 128], src_r, idx2, w, d_win[0 if w < (WG + 1) // 2 else 1])
                t_win[w] = fetch(wdst[:, 128 * w:128 * w + 128], dst_r, idx2, w, d_win[0 if w < (WG + 1) // 2 else 1])

        t_c64, t_win, t_ww = None, {}, {}
        d_win, d_ww = [dsem("d_win0"), dsem("d_win1")], [dsem(f"d_ww{i}") for i in range(3)]

        def window_weight(w):
            t_ww[w] = fetch(wew[:, 128 * w:128 * w + 128], ew_r, idx2, w, d_ww[w % 3])

        d_h0 = dsem("d_h0")
        t_h0 = []
        for i, (b0, b1) in enumerate(pieces):
            DV.wait(t_x[i])
            for b in range(b0, b1):
                t = DV.mark(lambda e, b=b: e.bn_stats(st6[:, b, :], xs[:, b, :]))
            DV.wait(t)
            for b in range(b0, b1):
                t = DV.mark(lambda e, b=b: e.bn_aggr(mv[:, b, :], st6[:, b, :]), .075)
            DV.wait(t)
            t = DV.mark(lambda e, b0=b0, b1=b1: e.tensor_scalar(sd[:, b0:b1], mv[:, b0:b1, 1], 1e-5, None, ALU.add), .07)
            AC.wait(t)
            t = AC.mark(lambda e, b0=b0, b1=b1: e.activation(sd[:, b0:b1], sd[:, b0:b1], ACT.Sqrt), .1)
            DV.wait(t)
            t = DV.mark(lambda e, b0=b0, b1=b1: e.reciprocal(rs[:, b0:b1], sd[:, b0:b1]), .1)
            DV.wait(t)
            t = DV.mark(lambda e, b0=b0, b1=b1: e.scalar_tensor_tensor(
                nb_[:, b0:b1], mv[:, b0:b1, 0], -1.0, rs[:, b0:b1], ALU.mult, ALU.mult), .08)
            AC.wait(t, t_x[i])
            for b in range(b0, b1):
                t = AC.mark(lambda e, b=b: e.activation(h0[:, b, :], xs[:, b, :], ACT.Relu,
                                                        bias=nb_[:, b:b + 1], scale=rs[:, b:b + 1]), .39)
            t_h0.append(t)
            SP.wait(t)
            t_h0d = SP.dma(lambda e, b0=b0, b1=b1: e.dma_start(
                h0_d.rearrange("(b p) f -> p b f", p=128)[:, b0:b1, :], h0[:, b0:b1, :]), d_h0)
            if i == min(3, len(pieces) - 1):
                window_starts()

        ea_v = T["ea"].rearrange("(g p j) f -> g p j f", p=128, j=4)
        d_ea = [dsem(f"d_ea{i}") for i in range(EAN)]
        d_ga = [dsem(f"d_ga{i}") for i in range(GAN)]
        t_ea, t_ga, t_oh, t_l0 = {}, {}, {}, {}

        def load_ea(g):
            if g >= G:
                return
            if g >= EAN:
                SP.wait(t_l0[4 * (g - EAN) + 3])
            t_ea[g] = SP.dma(lambda e: e.dma_start(ea[:, g % EAN, :, :], ea_v[g]), d_ea[g % EAN])

        def gather(t):
            if t >= GAN:
                PO.wait(t_l0[t - GAN])
            t_ga[t] = PO.dma(lambda e: e.indirect_dma_start(
                ga[:, t % GAN, :], None, h0_d, bass.IndirectOffsetOnAxis(src_n[:, t:t + 1], 0)), d_ga[t % GAN])

        def onehot(t):
            if t >= NT:
                return
            if t >= OHN:
                DV.wait(t_l0[t - OHN])
            t_oh[t] = DV.mark(lambda e: e.tensor_scalar(
                oh[:, t % OHN, 0:S.wid[t // 4]], iota[:, 0:S.wid[t // 4]], drel[:, t:t + 1], ew_n[:, t:t + 1], ALU.is_equal, ALU.mult), .24)

        def tile(t):
            g = t // 4
            k = S.bank[g]
            if t == 0 or (t % 4 == 0 and S.bank[g - 1] != k):
                PE.wait(free["PA"])
                PE.run(mm(P["PA"][:, :], zero16[:, :], any16, True, False))
                PE.wait(free["PB"])
                PE.run(mm(P["PB"][:, :], zero16[:, :], any16, True, False))
            at = S.base[g] - STEP * k
            last = t == NT - 1 or (t % 4 == 3 and S.bank[g + 1] != k)
            PE.wait(t_ga[t], t_oh[t])
            w = S.wid[g]
            PE.run(mm(P["PA"][:, at:at + w], ga[:, t % GAN, :], oh[:, t % OHN, 0:w], False, last), .03 + w / 600)
            PE.wait(t_ea[g])
            t_l0[t] = PE.mark(mm(P["PB"][:, at:at + w], ea[:, g % EAN, t % 4, :], oh[:, t % OHN, 0:w], False, last), .03 + w / 600)

        t_quad, t_ht, t_qht = {}, [None, None], {}

        def quad(i):
            b0, b1 = 4 * i, min(NB, 4 * i + 4)
            m = b1 - b0
            yield PE, lambda: [t_c32, t_h0[(b1 - 1) // XP], free["PM1"]], ["PM1", "HT0"]
            PE.wait(t_c32, t_h0[(b1 - 1) // XP], free["PM1"])
            for j in range(m):
                f = lambda e, j=j: e.transpose(P["PM1"][:, 128 * j:128 * j + 128], h0[:, b0 + j, :], idn)
                if j < m - 1:
                    PE.run(f, .14)
            t = PE.mark(f, .14)
            yield AC, lambda: [t, t_ht[0]], []
            AC.wait(t, t_ht[0], t_pe[0], t_pe[1])
            free["PM1"] = t_qht[i] = AC.mark(lambda e: e.activation(HT[:, 0, 0:128 * m], P["PM1"][:, 0:128 * m], ACT.Copy))
            held.discard("PM1")
            yield PE, lambda: [t_qht[i], t_w, free["PM0"], free["PV0"]], ["PM0", "PV0"]
            PE.wait(t_qht[i], t_w, free["PM0"], free["PV0"])
            for bank, w in (("PM0", WS), ("PV0", WI)):
                for j in range(m):
                    f = mm(P[bank][:, 128 * j:128 * j + 128], HT[:, 0, 128 * j:128 * j + 128], w, True, True)
                    if bank == "PM0" or j < m - 1:
                        PE.run(f, .26)
            t2 = PE.mark(f, .26)
            t_ht[0] = t2
            held.discard("HT0")
            x4 = xs[:, b0:b1, :].rearrange("p b f -> p (b f)")
            yield DV, lambda: [t2], []
            DV.wait(t2, t_h0[(b1 - 1) // XP])
            t_q0 = free["PM0"] = DV.mark(lambda e: e.tensor_tensor(x4, P["PM0"][:, 0:128 * m], x4, ALU.add), .6)
            held.discard("PM0")
            yield AC, lambda: [t2] + ([t_prep.get(("rk", 1), LATER), t_prep.get("over", [LATER])[0]] if i >= QE else []), []
            AC.wait(t2, t_c64, t_drel, t_prep["rk", 1] if i >= QE else None, t_prep["over"][0] if i >= QE else None)
            free["PV0"] = AC.mark(lambda e: e.activation(R[:, b0:b1, :].rearrange("p b f -> p (b f)"),
                                                         P["PV0"][:, 0:128 * m], ACT.Copy), .48)
            held.discard("PV0")
            t_quad[i] = (t_q0, free["PV0"])

        V = 128 * WG
        t_prep = {}

        parts = [(0, (WG + 1) // 2), ((WG + 1) // 2, WG)]
        r16, k16 = {}, {}

        def windows_elementwise(part):
            wa, wz = parts[part]
            c = slice(128 * wa, 128 * wz)
            n = 128 * (wz - wa)
            fT, v_ = tmp[:, 0, 0:n], tmp[:, 1, 0:n]
            ri = tmp[:, 2, 0:n].bitcast(I32)
            d_ = wdst.bitcast(F32)[:, c]
            s_ = wsrc[:, c]
            DV.wait(t_win[wz - 1], t_c32, t_prep.get(("rk", 0)))
            t = DV.mark(lambda e: e.tensor_scalar(ri, s_, 127, None, ALU.bitwise_and), .41)
            t2 = DV.mark(lambda e: e.tensor_tensor(
                d_.rearrange("p (c s) -> p c s", s=128), wdst[:, c].rearrange("p (c s) -> p c s", s=128),
                w5[:, wa:wz].unsqueeze(2).to_broadcast([128, wz - wa, 128]), ALU.subtract), .74)
            DV.wait(t)
            t3 = DV.mark(lambda e: e.tensor_tensor(fT, s_, ri, ALU.subtract), .74)
            DV.wait(t2)
            t4 = DV.mark(lambda e: e.tensor_scalar(v_, d_, 0.0, None, ALU.is_ge), .41)
            DV.wait(t4)
            t4 = DV.mark(lambda e: e.scalar_tensor_tensor(v_, d_, float(D), v_, ALU.is_lt, ALU.mult), .74)
            DV.wait(t3)
            t3 = DV.mark(lambda e: e.scalar_tensor_tensor(fT, fT, D / 128.0, d_, ALU.mult, ALU.add), .74)
            DV.wait(t3, t4)
            k_, r_ = s_.bitcast(F16)[:, 0:n], s_.bitcast(F16)[:, n:2 * n]
            DV.mark(lambda e: e.tensor_scalar(k_, fT, 1.0, None, ALU.add), .41)
            t5 = DV.mark(lambda e: e.scalar_tensor_tensor(r_, ri, 1.0, v_, ALU.add, ALU.mult), .74)
            t_prep["rk", part] = t5
            for w in range(wa, wz):
                k16[w] = k_[:, 128 * (w - wa):128 * (w - wa) + 128]
                r16[w] = r_[:, 128 * (w - wa):128 * (w - wa) + 128]

        t_rk = {}

        def windows_turn(w):
            bank = "PM1"
            yield PE, lambda: [t_prep.get(("rk", 0 if w < parts[0][1] else 1), LATER), free[bank]], [bank]
            PE.wait(t_prep["rk", 0 if w < parts[0][1] else 1], free[bank], t_id16)
            v = P[bank][:, :].bitcast(F16)
            PE.run(lambda e: e.transpose(v[:, 0:128], r16[w], id16[:, :]), .06)
            t = PE.mark(lambda e: e.transpose(v[:, 128:256], k16[w], id16[:, :]), .06)
            t_prep["turn"] = t
            yield AC, lambda: [t], []
            AC.wait(t)
            AC.run(lambda e: e.activation(rT[:, 128 * w:128 * w + 128], v[:, 0:128], ACT.Copy), .2)
            t2 = AC.mark(lambda e: e.activation(kT[:, 128 * w:128 * w + 128], v[:, 128:256], ACT.Copy), .2)
            free[bank] = t_rk[w] = t2
            held.discard(bank)

        def counts(w):
            pw = min(128, NW - 128 * w)
            d_ = wdst.bitcast(F32)[0:pw, 128 * w:128 * w + 128]
            j0, j1 = (HT[0:pw, 1, 128 * i:128 * i + 128] for i in (0, 1))
            DV.wait(t_cst, t_ww[w], t_prep.get("j"), *t_pe)
            for i in range(D):
                t = DV.mark(lambda e, i=i: e.tensor_scalar(j0, d_, float(i), 0.0, ALU.is_equal, ALU.add,
                                                           accum_out=cs[0:pw, 0, w, i:i + 1]))
                t2 = DV.mark(lambda e, i=i: e.scalar_tensor_tensor(j1, d_, float(i), wew[0:pw, 128 * w:128 * w + 128],
                                                                   ALU.is_equal, ALU.mult,
                                                                   accum_out=cs[0:pw, 1, w, i:i + 1]))
                DV.wait(t, t2)
            t_prep["j"] = t2

        d_cs = dsem("d_cs")

        def spread_counts():
            SP.wait(t_prep["j"])
            for i in range(2):
                t = SP.dma(lambda e, i=i: e.dma_start(
                    cs_d[i].rearrange("(c w d) -> w c d", w=128, d=D), cs[:, i, :, :]), d_cs)
            return t

        def gather_counts(t):
            nonlocal t_cs
            SP.wait(t)
            for i in range(2):
                t = SP.dma(lambda e, i=i: e.dma_start(
                    csr[:, i, :], cs_d[i, 0:NP].rearrange("(b p) -> b p", p=128)), d_cs)
            t_cs = t

        t_cs = None

        def turn_counts():
            PE.wait(t_cs, free["PM0"])
            PE.run(lambda e: e.transpose(P["PM0"][:, 0:NB], csr[:, 0, :], idn[0:NB, 0:NB]))
            t = PE.mark(lambda e: e.transpose(P["PM0"][:, 64:64 + NB], csr[:, 1, :], idn[0:NB, 0:NB]))
            t_prep["cT"] = t

        def keep_counts():
            DV.wait(t_prep["cT"])
            t = DV.mark(lambda e: e.tensor_scalar(inv[:, 0, :], P["PM0"][:, 0:NB], 1.0, None, ALU.max))
            t_prep["sw"] = free["PM0"] = DV.mark(lambda e: e.tensor_copy(sw[:, :], P["PM0"][:, 64:64 + NB]))
            DV.wait(t)
            t = DV.mark(lambda e: e.reciprocal(inv[:, 1, :], inv[:, 0, :]))
            DV.wait(t)
            t_prep["inv"] = DV.mark(lambda e: e.tensor_scalar(inv[:, 0, :], inv[:, 1, :], 1.0 / HSCALE, None, ALU.mult))

        t_base = {}

        def add_hi(b):
            DV.wait(t_prep["sw"], *t_quad[b // 4])
            t_base[b] = DV.mark(lambda e: e.scalar_tensor_tensor(
                xs[:, b, :], R[:, b, :], sw[:, b:b + 1], xs[:, b, :], ALU.mult, ALU.add), .26)

        def scales():
            DV.wait(t_w, t_c32)
            for i in range(2):
                t = DV.mark(lambda e, i=i: e.scalar_tensor_tensor(diag, wn[:, i, :], 1.0, wn[:, i, :], ALU.mult,
                                                                  ALU.mult, accum_out=sc[:, i:i + 1]))
                DV.wait(t)
            AC.wait(t)
            t = AC.mark(lambda e: e.activation(sc[:, 0:2], sc[:, 0:2], ACT.Sqrt))
            t2 = AC.mark(lambda e: e.activation(sc[:, 2:3], bcol[:, :], ACT.Abs))
            t_prep["sc"] = (t, t2)

        def powers():
            DV.wait(*t_prep["sc"])
            t = DV.mark(lambda e: e.tensor_tensor(sc[:, 0:1], sc[:, 0:1], sc[:, 1:2], ALU.add))
            DV.wait(t)
            t = DV.mark(lambda e: e.scalar_tensor_tensor(sc[:, 0:1], sc[:, 0:1], 11.5, sc[:, 2:3], ALU.mult, ALU.add))
            DV.wait(t)
            t = DV.mark(lambda e: e.tensor_scalar(sc[:, 0:1], sc[:, 0:1], 1e-30, 1e30, ALU.max, ALU.min))
            DV.wait(t)
            t = DV.mark(lambda e: e.tensor_scalar(sci[:, 0:1], sc[:, 0:1].bitcast(I32), 0x7F800000, None, ALU.bitwise_and))
            DV.wait(t)
            t = DV.mark(lambda e: e.tensor_scalar(sci[:, 1:2], sci[:, 0:1], -1.0, float(254 << 23), ALU.mult, ALU.add))
            t2 = DV.mark(lambda e: e.tensor_scalar(sc[:, 4:5], sci[:, 0:1].bitcast(F32), 2.0 ** -14, None, ALU.mult))
            DV.wait(t, t2)
            t = DV.mark(lambda e: e.tensor_scalar(sc[:, 3:4], sci[:, 1:2].bitcast(F32), 2.0 ** 14, None, ALU.mult))
            DV.wait(t)
            t = DV.mark(lambda e: e.tensor_scalar(diag, idn, sc[:, 3:4], None, ALU.mult))
            t2 = DV.mark(lambda e: e.tensor_scalar(W2L, W2L, sc[:, 4:5], None, ALU.mult))
            t3 = DV.mark(lambda e: e.tensor_scalar(W2R, W2R, sc[:, 4:5], None, ALU.mult))
            t_prep["w2"] = (t2, t3)
            return t

        def powers_turned(t):
            PE.wait(t, t_cst, free["PM1"])
            t_prep["sT"] = PE.mark(mm(P["PM1"][:, 0:128], ones[:, :], diag, True, True))

        def scaled_weights():
            DV.wait(t_prep["sT"])
            t1 = DV.mark(lambda e: e.tensor_tensor(W1L, W1L, P["PM1"][:, 0:128], ALU.mult))
            t2 = DV.mark(lambda e: e.scalar_tensor_tensor(W1R, W1R, 1.0 / HSCALE, P["PM1"][:, 0:128], ALU.mult, ALU.mult))
            t = free["PM1"] = DV.mark(lambda e: e.tensor_tensor(
                brow[:, 0, :], brow[:, 0, :], P["PM1"][0:1, 0:128], ALU.mult))
            t_prep["w1"] = (t1, t2)
            return t

        def bias_rows(t):
            PE.wait(t, *t_prep["w1"])
            t_prep["bT"] = PE.mark(mm(P["PM1"][:, 0:256], ones[0:1, :], brow[:, :, :].rearrange("o a f -> o (a f)"), True, True))

        def keep_biases():
            DV.wait(t_prep["bT"])
            t_prep["w"] = free["PM1"] = DV.mark(lambda e: e.tensor_copy(
                bb[:, :, :].rearrange("p a f -> p (a f)"), P["PM1"][:, 0:256]))

        n_prod, half_built = [(0, 0, 0)], []
        t_c, t_cst_half, t_ring, t_used = {}, {}, {}, {}
        d_cb = [dsem(f"d_cb{i}") for i in range(2)]
        t_row, t_made = {}, {}
        quads = [(hh, w, min(w + 4, S.windows(hh))) for hh in range(NH) for w in range(0, S.windows(hh), 4)]
        CB = ("PC0", "PC1", "PV1")

        def built(hh):
            return cb[:, (hh % 2) * CW:(hh % 2) * CW + (NB + 1) * S.width(hh)].rearrange("p (q k) -> p q k", q=NB + 1)

        def count_quad(i):
            hh, a, z = quads[i]
            w0 = HW * hh + a
            n = z - a
            R_ = i % QN
            DV.wait(t_rk[w0 // 128], t_ring.get(i - QN), t_cst)
            r_o, k_o = ohr[:, R_, :, 0:n], ohk[:, R_, 0:KEY, 0:n]
            DV.run(lambda e: e.tensor_tensor(
                r_o, IR[:, :, 0:n], rT[:, w0:w0 + n].unsqueeze(1).to_broadcast([128, 128, n]), ALU.is_equal), .335)
            t_made[i] = DV.mark(lambda e: e.tensor_tensor(
                k_o, IK[:, :, 0:n], kT[:, w0:w0 + n].unsqueeze(1).to_broadcast([128, KEY, n]), ALU.is_equal), .58)

        def count_quads():
            for i, (hh, a, z) in enumerate(quads):
                yield DV, lambda: [t_rk.get((HW * hh + a) // 128, LATER), t_ring.get(i - QN, LATER) if i >= QN else None], []
                count_quad(i)

        def keep_counts_of(hh, w, bank, t):
            AC.wait(t)
            if hh >= 2:
                AC.wait(t_cst_half[hh - 2], t_row[hh - 2], t_used.get(hh - 2))
            o = built(hh)[:, :, D * w:D * w + 2 * D].rearrange("p q (w d) -> p w q d", w=2)
            s_ = P[bank][:, 0:2 * KX].rearrange("p (w q d) -> p w q d", w=2, d=D)
            t_c[hh] = free[bank] = AC.mark(lambda e: e.activation(o, s_, ACT.Copy, saturate=False), .47)
            held.discard(bank)

        def store_half(hh):
            SP.wait(t_c[hh])
            t_cst_half[hh] = SP.dma(lambda e: e.dma_start(
                c_d[hh, :, 0:NB * S.width(hh)], cb[:, (hh % 2) * CW:(hh % 2) * CW + NB * S.width(hh)]), d_cb[hh % 2], 6.0)
            half_built.append(hh)

        def count_products():
            turn_ = 0
            for i, (hh, a, z) in enumerate(quads):
                n = z - a
                R_ = i % QN
                for j in range(0, n, 2):
                    bank = CB[turn_ % 3]
                    turn_ += 1
                    new = a == 0 and j == 0
                    yield (PE, lambda: [t_made.get(i, LATER), free[bank],
                                        t_row.get(hh - 2, LATER) if new and hh >= 2 else None],
                           [bank] + ([f"C{hh % 2}"] if new else []))
                    if new:
                        held.discard(f"C{hh % 2}")
                    n_prod[0] = (hh, a, j + 2)
                    PE.wait(t_made[i], free[bank])
                    PE.run(mm(P[bank][:, 0:KX], ohr[:, R_, :, j], ohk[:, R_, :, j], True, True), .105)
                    t = PE.mark(mm(P[bank][:, KX:2 * KX], ohr[:, R_, :, j + 1], ohk[:, R_, :, j + 1], True, True), .105)
                    yield AC, lambda: [t], []
                    keep_counts_of(hh, a + j, bank, t)
                t_ring[i] = t
                if z == S.windows(hh):
                    store_half(hh)
                    start(row_check(hh), .5)
            n_prod[0] = (NH, 0, 0)

        def row_check(hh):
            yield DV, lambda: [t_c[hh]], []
            DV.wait(t_c[hh], t_row.get(hh - 1))
            t_row[hh] = DV.mark(lambda e: e.tensor_scalar(junk[:, 0:S.width(hh)], built(hh)[:, NB, :], 15.0, 0.0,
                                                          ALU.is_gt, ALU.add, accum_out=rmax[:, hh:hh + 1]), .4)

        NK = S.bank[-1] + 1
        t_ev, t_X, t_h1, t_Hfree, t_R = {}, {}, {}, [None, None], {}

        def step_blocks(k):
            return list(range(3 * k, NB if k == NK - 1 else min(NB, 3 * k + 3)))

        def step_evac(k, last_tile):
            assert k == 0 or k - 1 in t_X
            AC.wait(t_l0[last_tile], t_X.get(k - 1), t_prep["over"][0])
            a = AC.mark(lambda e: e.activation(AT[:, k % 2, :], P["PA"][:, :], ACT.Copy))
            b = AC.mark(lambda e: e.activation(BT[:, k % 2, :], P["PB"][:, :], ACT.Copy))
            free["PA"], free["PB"] = a, b
            t_ev[k] = (a, b)

        def turn(h, bl, tH, bank, ring):
            m = len(bl)
            yield PE, lambda: [tH, free[bank]], [bank, f"HT{ring}"]
            PE.wait(tH, free[bank], t_id16)
            for i, b in enumerate(bl):
                o = P[bank][:, 128 * i:128 * i + 128]
                PE.run(mm(o, h[:, 0, b, :], id16[:, :], True, False), .06)
                f = mm(o, h[:, 1, b, :], id16[:, :], False, True)
                if i < m - 1:
                    PE.run(f, .06)
            t = PE.mark(f, .06)
            yield AC, lambda: [t, t_ht[ring]], []
            AC.wait(t, t_ht[ring], t_prep["j"])
            t_turned[ring] = free[bank] = AC.mark(lambda e: e.activation(HT[:, ring, 0:128 * m], P[bank][:, 0:128 * m], ACT.Copy))
            held.discard(bank)

        def self_term(bl, ring, bank, w, j):
            yield PE, lambda: [t_turned[ring], free[bank], t_prep.get("w", LATER)], [bank]
            PE.wait(t_turned[ring], free[bank], t_prep["w"], t_cst)
            for i, b in enumerate(bl):
                f = mm(P[bank][:, 128 * i:128 * i + 128], HT[:, ring, 128 * i:128 * i + 128], w, True, True)
                if b != bl[-1]:
                    PE.run(f)
            t = PE.mark(f)
            t_ht[ring] = t
            held.discard(f"HT{ring}")
            tb = t_base.get(bl[-1]) if j == 0 else t_T.get(bl[-1])
            yield DV, lambda: [t], []
            DV.wait(t, tb)
            free[bank] = DV.mark(lambda e: e.tensor_tensor(
                R[:, bl[0]:bl[-1] + 1, :], P[bank][:, 0:128 * len(bl)].rearrange("p (b f) -> p b f", f=128),
                bb[:, j, :].unsqueeze(1).to_broadcast([128, len(bl), 128]), ALU.add), .47)
            held.discard(bank)
            for b in bl:
                t_R[j, b] = free[bank]

        t_turned = {}

        def step(k):
            bl = step_blocks(k)
            b0, b1, m = bl[0], bl[-1] + 1, len(bl)
            yield DV, lambda: [t_prep.get("sw", LATER), *[t for b in bl for t in t_quad.get(b // 4, [LATER])]], []
            for b in bl:
                add_hi(b)
            yield PE, lambda: [*t_ev[k], free["PM0"]], ["PM0"]
            PE.wait(*t_ev[k], free["PM0"], t_w)
            for i, b in enumerate(bl):
                o = P["PM0"][:, 128 * i:128 * i + 128]
                at = 128 * b - STEP * k
                ops = [(AT[:, k % 2, at:at + 128], WJ), (BT[:, k % 2, at:at + 128], WE)]
                if i == 0 and k > 0:
                    ops += [(AT[:, (k - 1) % 2, STEP:STEP + 128], WJ), (BT[:, (k - 1) % 2, STEP:STEP + 128], WE)]
                for j, (l, r) in enumerate(ops):
                    f = mm(o, l, r, j == 0, j == len(ops) - 1)
                    if b != bl[-1] or j < len(ops) - 1:
                        PE.run(f)
            t_X[k] = PE.mark(f)
            xk = xs[:, b0:b1, :].rearrange("p b f -> p (b f)")
            yield DV, lambda: [t_X[k], *[t_base.get(b, LATER) for b in bl]], []
            DV.wait(t_X[k], *[t_base[b] for b in bl])
            t = free["PM0"] = DV.mark(lambda e: e.tensor_tensor(xk, P["PM0"][:, 0:128 * m], xk, ALU.add), .47)
            held.discard("PM0")
            DV.wait(t)
            for b in bl:
                t = DV.mark(lambda e, b=b: e.bn_stats(st6[:, b, :], xs[:, b, :]))
            DV.wait(t)
            for b in bl:
                t = DV.mark(lambda e, b=b: e.bn_aggr(mv[:, b, :], st6[:, b, :]), .08)
            DV.wait(t)
            t1 = DV.mark(lambda e: e.tensor_scalar(sd[:, b0:b1], mv[:, b0:b1, 1], 1e-5, None, ALU.add), .08)
            yield AC, lambda: [t1], []
            AC.wait(t1)
            t2 = AC.mark(lambda e: e.activation(sd[:, b0:b1], sd[:, b0:b1], ACT.Sqrt), .1)
            yield DV, lambda: [t2], []
            DV.wait(t2)
            t = DV.mark(lambda e: e.reciprocal(rs[:, b0:b1], sd[:, b0:b1]), .11)
            DV.wait(t)
            t = DV.mark(lambda e: e.tensor_scalar(rs[:, b0:b1], rs[:, b0:b1], HSCALE, None, ALU.mult), .08)
            DV.wait(t)
            t3 = DV.mark(lambda e: e.scalar_tensor_tensor(
                nb_[:, b0:b1], mv[:, b0:b1, 0], -1.0, rs[:, b0:b1], ALU.mult, ALU.mult), .08)
            yield AC, lambda: [t3, t_Hfree[k % 2], t_prep.get("w", LATER), t_prep.get("sw", LATER)], []
            AC.wait(t3, t_Hfree[k % 2], t_prep["w"], t_prep["sw"])
            Hk = H[:, k % 2, 0:128 * m]
            for i, b in enumerate(bl):
                t = AC.mark(lambda e, b=b, i=i: e.activation(H[:, k % 2, 128 * i:128 * i + 128], xs[:, b, :], ACT.Relu,
                                                             bias=nb_[:, b:b + 1], scale=rs[:, b:b + 1]), .39)
            if b1 > XB:
                yield AC, lambda: [], [f"S{2 * per}", f"S{2 * per + 1}"]
                held.difference_update((f"S{2 * per}", f"S{2 * per + 1}"))
                for i in (0, 1):
                    AC.wait(ring_free.get(2 * per + i))
                    DV.wait(ring_free.get(2 * per + i))
            AC.wait(t, t_prep["turn"], t_prep["j"])
            hi = h1[:, 0, b0:b1, :].rearrange("p b f -> p (b f)")
            lo = h1[:, 1, b0:b1, :].rearrange("p b f -> p (b f)")
            t4 = AC.mark(lambda e: e.activation(hi, Hk, ACT.Copy))
            yield DV, lambda: [t4], []
            DV.wait(t4, t_prep["turn"], t_prep["j"])
            t = DV.mark(lambda e: e.tensor_tensor(lo, Hk, hi, ALU.subtract), .47)
            t_Hfree[k % 2] = t
            for b in bl:
                t_h1[b] = t
            done_blocks[0] = bl[-1] + 1
            yield from turn(h1, bl, t, "PM1", 1)
            yield from self_term(bl, 1, "PM0", W1R, 0)

        t_T = {}
        ring_free = {}
        d_cl = [dsem(f"d_cl{i}") for i in range(10)]
        LAST = len(S.qg) - 1
        big = max(z - a for a, z in S.qg) * HW * D
        per = min(4, CW // big)
        XB = NB - -(-big // 256)
        spare = [h1r[:, :].bitcast(FP8)[:, 256 * (NB * a + XB):256 * (NB * a + NB)] for a in (0, 1)]
        t_agg = {}

        def load_part(gi, hh, s):
            q0, q1 = S.qg[gi]
            wd = S.width(hh)
            half = s // per
            SP.wait(t_cst_half[hh], ring_free.get(s))
            for h in (NH - 1, NH - 2):
                if h % 2 == half:
                    SP.wait(t_cst_half[h], t_row[h], t_used.get(h))
            o = cb[:, half * CW + (s % per) * big:half * CW + (s % per) * big + (q1 - q0) * wd]
            return s, SP.dma(lambda e: e.dma_start(o, c_d[hh, :, q0 * wd:q1 * wd]), d_cl[s]), o

        def product(bank, h, th, o, q0, a, z, q1, wd, tload, n=None):
            n = n or wd
            if a == q0:
                PE.wait(tload, free[bank])
            for q in range(a, z):
                PE.wait(th[q])
                r = o[:, (q - q0) * wd:(q - q0) * wd + n]
                PE.run(mm(P[bank][:, 0:n], h[:, 0, q, :], r, q == q0, False), n / 2.35e3)
                f = mm(P[bank][:, 0:n], h[:, 1, q, :], r, False, q == q1 - 1)
                if q < z - 1:
                    PE.run(f, n / 2.35e3)
            return PE.mark(f, n / 2.35e3)

        accs = ["PV0"]
        t_aggfree = [None]
        done_blocks = [0]
        conv_todo = [(gi, hh) for gi in range(LAST + 1) for hh in range(NH)]

        def conv1_choice():
            if t_aggfree[0] is None:
                return None
            if not loading[0]:
                for hh in half_built:
                    if hh + 2 > n_prod[0][0]:
                        for gi in range(LAST):
                            if (gi, hh) in conv_todo and S.qg[gi][1] <= done_blocks[0]:
                                q0, q1 = (q * S.width(hh) for q in S.qg[gi])
                                return gi, hh, None, t_c[hh], cb[:, (hh % 2) * CW + q0:(hh % 2) * CW + q1]
            for x in conv_todo:
                if x in fetched and S.qg[x[0]][1] <= done_blocks[0]:
                    return (*x, *fetched[x])
            return None

        def conv1_stream():
            jobs = 0
            while conv_todo:
                bank = accs[jobs % len(accs)]
                jobs += 1
                pick = [None]

                def needs():
                    pick[0] = conv1_choice()
                    if pick[0] is None or (pick[0][2] is None and f"C{pick[0][1] % 2}" in held):
                        return [LATER]
                    return [pick[0][3], free[bank]]

                yield PE, needs, [bank]
                gi, hh, s, tl, o = pick[0]
                conv_todo.remove((gi, hh))
                if s is None:
                    held.add(f"C{hh % 2}")
                q0, q1 = S.qg[gi]
                for a in range(q0, q1, PIECE):
                    z = min(q1, a + PIECE)
                    if a > q0:
                        yield PE, lambda: [], []
                    t = product(bank, h1, t_h1, o, q0, a, z, q1, S.width(hh), tl)
                if s is None:
                    t_used[hh] = t
                    held.discard(f"C{hh % 2}")
                else:
                    ring_free[s] = t
                    held.discard(f"S{s}")
                if not conv_todo:
                    last_conv1[0] = t
                start(conv1_sum(hh, bank, t), .5)

        def early_loader():
            n = 0
            while not loading[0]:
                pick = [None]

                def needs():
                    pick[0] = None
                    for x in conv_todo:
                        if x[0] < LAST and S.qg[x[0]][1] <= done_blocks[0] and x not in fetched and x[1] + 2 <= n_prod[0][0]:
                            pick[0] = x
                            break
                    late = loading[0] or done_blocks[0] + 2 * 3 > XB
                    return [] if late else [LATER] if pick[0] is None else [t_cst_half[pick[0][1]]]

                yield SP, needs, [f"S{2 * per + n % 2}"]
                s = 2 * per + n % 2
                if pick[0] is None or loading[0] or done_blocks[0] + 2 * 3 > XB:
                    held.discard(f"S{s}")
                    return
                n += 1
                gi, hh = pick[0]
                q0, q1 = S.qg[gi]
                wd = S.width(hh)
                o = spare[s - 2 * per][:, 0:(q1 - q0) * wd]
                SP.wait(t_cst_half[hh], ring_free.get(s), t_prep["turn"], t_prep["j"])
                fetched[pick[0]] = s, load_now(o, hh, q0 * wd, q1 * wd, d_cl[s]), o

        def load_now(o, hh, a, z, ds):
            return SP.dma(lambda e: e.dma_start(o, c_d[hh, :, a:z]), ds, 4.0)

        def loader():
            yield SP, lambda: [LATER if n_prod[0][0] < NH else None, *[t_row.get(h, LATER) for h in range(NH)]], ["C0", "C1"]
            held.difference_update(("C0", "C1"))
            accs[:] = ["PV0", "PV1"]
            loading[0] = True
            n = 0
            todo = [x for x in conv_todo if x not in fetched]
            for i, x in enumerate(todo):
                if x[0] < LAST:
                    s = n % (2 * per)
                elif x[1] == 0:
                    n = 0
                if x[0] == LAST:
                    s = per + n % per
                    if n == per:
                        yield SP, lambda: [], [f"S{j}" for j in range(per)]
                        yield from load_half(0)
                n += 1
                yield SP, lambda: [], [f"S{s}"]
                fetched[x] = load_part(*x, s)
            if NH <= per:
                yield SP, lambda: [], [f"S{j}" for j in range(per)]
                yield from load_half(0)
            yield SP, lambda: [], [f"S{j}" for j in range(per, 2 * per)]
            for hh in range(1, NH):
                if HW * D * hh < 128 * S.dense:
                    yield from load_half(hh)

        fetched, loading = {}, [False]
        def conv1_sum(hh, bank, t):
            wd = S.width(hh)
            c = agg[:, HW * D * hh:HW * D * hh + wd]
            p = P[bank][:, 0:wd]
            first = hh not in sums_begun
            sums_begun.add(hh)
            if first:
                yield AC, lambda: [t], []
                AC.wait(t, t_aggfree[0])
                t_agg[hh] = free[bank] = AC.mark(lambda e: e.activation(c, p, ACT.Copy), .35)
            else:
                yield DV, lambda: [t, t_agg.get(hh, LATER)], [f"A{hh}"]
                DV.wait(t, t_agg[hh])
                t_agg[hh] = free[bank] = DV.mark(lambda e: e.tensor_tensor(c, p, c, ALU.add), .4)
                held.discard(f"A{hh}")
            held.discard(bank)
            sums_left[hh] -= 1
            if not sums_left[hh]:
                t_sum[hh] = t_agg[hh]

        t_sum, sums_left = {}, [len(S.qg)] * NH
        PIECE = 4
        sums_begun = set()

        def clear_agg():
            DV.wait(t_h0d, t_qht[NQ - 1])
            t_aggfree[0] = DV.mark(lambda e: e.memset(agg[:, S.n:NP], 0.0)) if NP > S.n else t_qht[NQ - 1]

        def batch(hh):
            a = 0 if hh == 0 else HW * D * hh // 128
            z = NB if hh == NH - 1 else HW * D * (hh + 1) // 128
            return list(range(a, z))

        t_Y, t_hi, t_h2, t_lo, t_h2d = {}, {}, {}, {}, {}
        d_h2 = dsem("d_h2")
        Tb = AT[:, :, 0:384]

        def node1(hh):
            bl = batch(hh)
            m = len(bl)
            yield PE, lambda: [t_sum.get(hh, LATER), t_sum.get(max(0, hh - 1), LATER), t_aggfree[0], free["PM0"]], ["PM0", f"T{hh % 2}"]
            PE.wait(t_sum[hh], t_sum.get(hh - 1), t_aggfree[0], free["PM0"], t_prep["w"])
            for i, b in enumerate(bl):
                f = mm(P["PM0"][:, 128 * i:128 * i + 128], agg[:, 128 * b:128 * b + 128], W1L, True, True)
                if b != bl[-1]:
                    PE.run(f)
            t_Y[hh] = PE.mark(f)
            for b in bl:
                t_yb[b] = t_Y[hh]
            yield DV, lambda: [t_Y[hh], *[t_R.get((0, b), LATER) for b in bl]], []
            DV.wait(t_Y[hh], t_X[NK - 1], t_prep["inv"], t_lo.get(hh - 2), t_hi.get(hh - 2))
            Tk = Tb[:, hh % 2, :]
            for i, b in enumerate(bl):
                DV.wait(t_R[0, b])
                t_T[b] = DV.mark(lambda e, i=i, b=b: e.scalar_tensor_tensor(
                    Tk[:, 128 * i:128 * i + 128], P["PM0"][:, 128 * i:128 * i + 128], inv[:, 0, b:b + 1], R[:, b, :],
                    ALU.mult, ALU.add), .27)
            free["PM0"] = t_T[bl[-1]]
            held.discard("PM0")
            hi, lo = (h2[:, a, bl[0]:bl[-1] + 1, :] for a in (0, 1))
            T3 = Tk[:, 0:128 * m].rearrange("p (b f) -> p b f", f=128)
            yield AC, lambda: [t_T[bl[-1]], t_l0[NT - 1]], []
            AC.wait(t_T[bl[-1]], t_l0[NT - 1])
            t = t_hi[hh] = AC.mark(lambda e: e.activation(hi, T3, ACT.Relu))
            yield DV, lambda: [t], []
            DV.wait(t, t_T[bl[-1]])
            t_lo[hh] = DV.mark(lambda e: e.scalar_tensor_tensor(lo, T3, 0.0, hi, ALU.max, ALU.subtract), .47)
            held.discard(f"T{hh % 2}")
            SP.wait(t_lo[hh])
            t_h2d[hh] = SP.dma(lambda e: e.dma_start(
                h2_d.rearrange("(b p) f -> p b f", p=128)[:, bl[0]:bl[-1] + 1, :],
                l0[:, 128 * bl[0]:128 * bl[-1] + 128].bitcast(F16).rearrange("p (b f) -> p b f", f=256)), d_h2)
            for b in bl:
                t_h2[b] = t_lo[hh]
            yield from turn(h2, bl, t_lo[hh], "PM1", hh % 2)
            yield from self_term(bl, hh % 2, "PB", W2R, 1)

        t_yb = {}

        d_l2 = [dsem(f"d_l2{i}") for i in range(2)]
        load2, half_free = {}, {}
        t_a2 = {}
        accs2 = ["PC0", "PC1"]

        def load_half(hh):
            wd = S.width(hh)
            s = hh % 2
            if hh >= 2:
                yield SP, lambda: [half_free.get(hh - 2, LATER)], []
                SP.wait(half_free[hh - 2])
            SP.wait(t_cst_half[hh])
            for i in range(s * per, s * per + per):
                SP.wait(ring_free.get(i))
            for h in (NH - 1, NH - 2):
                if h % 2 == s:
                    SP.wait(t_cst_half[h], t_row[h], t_used.get(h))
            o = cb[:, s * CW:s * CW + NB * wd]
            load2[hh] = (SP.dma(lambda e: e.dma_start(o, c_d[hh, :, 0:NB * wd]), d_l2[s], 8.0 if hh < 2 else 5.0), o)

        def conv2_half(hh):
            wd = S.width(hh)
            need_wd = min(wd, 128 * S.dense - HW * D * hh)
            bank = accs2[hh % 2]
            for a in range(0, NB, PIECE):
                z = min(NB, a + PIECE)
                need = lambda: [t_h2.get(q, LATER) for q in range(a, z)]
                if a == 0:
                    yield PE, lambda: [load2[hh][0] if hh in load2 else LATER, free[bank]] + need(), [bank]
                else:
                    yield PE, need, []
                t = product(bank, h2, t_h2, load2[hh][1], 0, a, z, NB, wd, load2[hh][0], need_wd)
            half_free[hh] = t
            c = agg[:, HW * D * hh:HW * D * hh + need_wd]
            last = min(NB - 1, (HW * D * hh + need_wd - 1) // 128)
            start(conv2_out(hh, bank, t, c, need_wd, last), .5)

        def conv2_out(hh, bank, t, c, wd, last):
            yield AC, lambda: [t, t_yb.get(last, LATER)], []
            AC.wait(t, t_yb[last])
            t_a2[hh] = free[bank] = AC.mark(lambda e: e.activation(c, P[bank][:, 0:wd], ACT.Copy), .35)
            held.discard(bank)

        t_o, t_st = {}, {}
        d_o = [dsem(f"d_o{i}") for i in range(2)]
        ov = out.rearrange("(b p) f -> p b f", p=128)

        GA2 = min(16, NB * 128 // (128 + OW // 2))
        ga2 = h1r[:, 0:128 * GA2].bitcast(F16).rearrange("p (n f) -> p n f", n=GA2)
        oh2 = h1r[:, 128 * GA2:128 * GA2 + OW * GA2 // 2].bitcast(F16).rearrange("p (n f) -> p n f", n=GA2)
        d_g2 = [dsem(f"d_g2{i}") for i in range(GA2)]
        t_g2, t_oh2, t_m2 = {}, {}, {}
        T2 = 4 * S.g2
        N2 = max(S.bank2.values()) + 1
        last_conv1 = [None]

        def gathers2():
            yield PO, lambda: [t_h2d.get(hh, LATER) for hh in range(NH)] + [last_conv1[0] or LATER], []
            PO.wait(t_h2d[NH - 1], last_conv1[0])
            for t in range(T2, NT):
                if t - T2 >= GA2:
                    yield PO, lambda: [t_m2.get(t - GA2, LATER)], []
                gather2(t)

        def gather2(t):
            PO.wait(t_m2.get(t - GA2))
            t_g2[t] = PO.dma(lambda e: e.indirect_dma_start(
                ga2[:, t % GA2, :], None, h2_d, bass.IndirectOffsetOnAxis(src_n[:, t:t + 1], 0)), d_g2[t % GA2])

        def onehots2():
            yield DV, lambda: [last_conv1[0] or LATER], []
            DV.wait(last_conv1[0])
            for t in range(T2, NT):
                yield DV, lambda: [t_m2.get(t - GA2, LATER) if t - T2 >= GA2 else None], []
                onehot2(t)

        def onehot2(t):
            DV.wait(t_m2.get(t - GA2))
            w = S.wid[t // 4]
            t_oh2[t] = DV.mark(lambda e: e.tensor_scalar(
                oh2[:, t % GA2, 0:w], iota[:, 0:w], drel[:, t:t + 1], None, ALU.is_equal), .154)

        def tiles2():
            for t in range(T2, NT):
                g = t // 4
                j = S.bank2[g]
                bank = ("PV0", "PV1")[j % 2]
                new = t == T2 or (t % 4 == 0 and S.bank2[g - 1] != j)
                last = t == NT - 1 or (t % 4 == 3 and S.bank2[g + 1] != j)
                yield PE, lambda: [t_g2.get(t, LATER), t_oh2.get(t, LATER), free[bank]], [bank] if new else []
                if new:
                    PE.wait(free[bank], last_conv1[0])
                    PE.run(mm(P[bank][:, :], zero16[:, :], any16, True, False))
                at = S.base[g] - S.from2 - STEP * j
                w = S.wid[g]
                PE.wait(t_g2[t], t_oh2[t])
                PE.run(mm(P[bank][:, at:at + w], ga2[:, t % GA2, 0:128], oh2[:, t % GA2, 0:w], False, False), .056)
                t_m2[t] = PE.mark(mm(P[bank][:, at:at + w], ga2[:, t % GA2, 128:256], oh2[:, t % GA2, 0:w], False, last), .056)
                if last:
                    start(sums2(j, bank, t_m2[t]), .5)

        def sums2(j, bank, t):
            c0 = S.from2 + STEP * j
            c1 = min(NP, c0 + 512)
            yield AC, lambda: [t, t_yb.get(c1 // 128 - 1, LATER)], []
            AC.wait(t, t_yb[c1 // 128 - 1])
            a = t
            if c1 - c0 > 128:
                a = free[bank] = AC.mark(lambda e: e.activation(agg[:, c0 + 128:c1], P[bank][:, 128:c1 - c0], ACT.Copy), .45)
            if j:
                yield DV, lambda: [t, a, t_a2.get(("e", j - 1), LATER)], []
                DV.wait(t, a, t_a2["e", j - 1])
                a = free[bank] = DV.mark(lambda e: e.tensor_tensor(
                    agg[:, c0:c0 + 128], P[bank][:, 0:128], agg[:, c0:c0 + 128], ALU.add))
            t_a2["e", j] = a
            held.discard(bank)

        def batch2():
            out_ = []
            for hh in range(NH):
                bl = [b for b in batch(hh) if b < S.dense and HW * D * hh < 128 * S.dense]
                if HW * D * hh < 128 * S.dense <= HW * D * (hh + 1):
                    bl = [b for b in range(batch(hh)[0], S.dense)]
                if bl:
                    out_.append((bl, [hh, max(0, hh - 1)]))
            for j in range(N2):
                b0 = S.dense if j == 0 else (S.from2 + STEP * j) // 128
                b1 = NB if j == N2 - 1 else (S.from2 + STEP * j + STEP) // 128
                out_.append((list(range(b0, b1)), [("e", j)]))
            assert sorted(b for bl, _ in out_ for b in bl) == list(range(NB))
            return out_

        def node2(hh, bl, sums):
            m = len(bl)
            bank = ("PM0", "PA")[hh % 2]
            yield PE, lambda: [*[t_a2.get(x, LATER) for x in sums], free[bank]], [bank, f"T{hh % 2}"]
            PE.wait(*[t_a2[x] for x in sums], free[bank], t_prep["w"])
            for i, b in enumerate(bl):
                f = mm(P[bank][:, 128 * i:128 * i + 128], agg[:, 128 * b:128 * b + 128], W2L, True, True)
                if b != bl[-1]:
                    PE.run(f)
            t1 = PE.mark(f)
            Tk = Tb[:, hh % 2, :]
            E_ = H[:, hh % 2, :]
            yield DV, lambda: [t1, t_st.get(hh % 2), *[t_R.get((1, b), LATER) for b in bl]], []
            DV.wait(t1, t_st.get(hh % 2), t_lo[NH - 1], t_lo.get(NH - 2))
            for i, b in enumerate(bl):
                DV.wait(t_R[1, b])
                t = DV.mark(lambda e, i=i, b=b: e.scalar_tensor_tensor(
                    Tk[:, 128 * i:128 * i + 128], P[bank][:, 128 * i:128 * i + 128], inv[:, 1, b:b + 1], R[:, b, :],
                    ALU.mult, ALU.add), .27)
            free[bank] = t
            held.discard(bank)
            DV.wait(t)
            s = sm[:, :, 0:m] if hh % 2 == 0 else sm2[:, :, 0:m]
            t2 = DV.mark(lambda e: e.tensor_reduce(s[:, 0, :], Tk[:, 0:128 * m].rearrange("p (b f) -> p b f", f=128),
                                                   AX.X, ALU.max, negate=True), .47)
            yield AC, lambda: [t2], []
            AC.wait(t2, *t_Hfree)
            for i in range(m):
                t = AC.mark(lambda e, i=i: e.activation(E_[:, 128 * i:128 * i + 128], Tk[:, 128 * i:128 * i + 128], ACT.Exp,
                                                        bias=s[:, 0, i:i + 1], accum_out=s[:, 1, i:i + 1]), .75 if i == 0 else .3)
            AC.wait(t)
            t3 = AC.mark(lambda e: e.activation(s[:, 2, :], s[:, 1, :], ACT.Ln), 1.4)
            yield DV, lambda: [t3], []
            DV.wait(t3)
            t = DV.mark(lambda e: e.tensor_tensor(s[:, 3, :], s[:, 2, :], s[:, 0, :], ALU.subtract), .08)
            DV.wait(t)
            for i, b in enumerate(bl):
                t = DV.mark(lambda e, i=i, b=b: e.scalar_tensor_tensor(
                    Tk[:, 128 * i:128 * i + 128], Tk[:, 128 * i:128 * i + 128], s[:, 3, i:i + 1], xs[:, b, :],
                    ALU.subtract, ALU.add), .27)
            SP.wait(t)
            t_st[hh % 2] = SP.dma(lambda e: e.dma_start(ov[:, bl[0]:bl[-1] + 1, :],
                                                    Tk[:, 0:128 * m].rearrange("p (b f) -> p b f", f=128)), d_o[hh % 2])
            held.discard(f"T{hh % 2}")

        sm2 = sb("sm2", [128, 4, 4])

        def make_flag():
            yield DV, lambda: [t_prep.get("inv", LATER), *[t_row.get(h, LATER) for h in range(NH)]], []
            DV.wait(t_prep["j"], t_drel, *t_row.values())
            a = DV.mark(lambda e: e.tensor_reduce(fl[:, 0:1], rmax[:, :], AX.X, ALU.add))
            b = DV.mark(lambda e: e.tensor_reduce(fl[:, 2:3], cs[:, 0, :, :].rearrange("p c d -> p (c d)"), AX.X, ALU.add))
            DV.wait(a, b, *t_prep["over"])
            b = DV.mark(lambda e: e.tensor_scalar(fl[:, 5:6], fl[:, 5:6], 0.0, None, ALU.is_gt))
            DV.wait(a, b)
            t1 = DV.mark(lambda e: e.scalar_tensor_tensor(fl[:, 1:2], fl[:, 6:7], 0.0, fl[:, 5:6], ALU.is_lt, ALU.add))
            yield PE, lambda: [t1, free["PM1"]], ["PM1"]
            PE.wait(t1, t_cst, free["PM1"])
            t2 = PE.mark(mm(P["PM1"][0:1, 0:3], ones[:, 0:1], fl[:, 0:3], True, True))
            yield DV, lambda: [t2], []
            DV.wait(t2)
            t = free["PM1"] = DV.mark(lambda e: e.tensor_copy(flag_f[:, 0:3], P["PM1"][0:1, 0:3]))
            held.discard("PM1")
            DV.wait(t)
            a = DV.mark(lambda e: e.tensor_scalar(flag_f[:, 3:4], flag_f[:, 2:3], float(S.e), None, ALU.not_equal))
            b = DV.mark(lambda e: e.tensor_tensor(flag_f[:, 0:1], flag_f[:, 0:1], flag_f[:, 1:2], ALU.add))
            DV.wait(a, b)
            t_prep["flag"] = DV.mark(lambda e: e.tensor_tensor(flag[:, :], flag_f[:, 0:1], flag_f[:, 3:4], ALU.add))

        DV.wait(t_nat)
        t_drel = DV.mark(lambda e: e.tensor_tensor(
            drel.rearrange("p (g j) -> p g j", j=4), dst_n[:, :].rearrange("p (g j) -> p g j", j=4),
            baseb.unsqueeze(2).to_broadcast([128, G, 4]), ALU.subtract), .94)
        DV.wait(t_drel, t_c32)
        t_id16 = DV.mark(lambda e: e.tensor_copy(id16[:, :], idn))

        for g in range(EAN):
            load_ea(g)
        PO.wait(t_h0d, t_nat)
        NQ = -(-NB // 4)
        def reach():
            yield DV, lambda: [t_drel], []
            past = AT[:, :, :].rearrange("p a k -> p (a k)")[:, 0:NT]
            DV.wait(t_drel, *t_pe)
            t = DV.mark(lambda e: e.tensor_tensor(
                past.rearrange("p (g j) -> p g j", j=4), drel.rearrange("p (g j) -> p g j", j=4),
                lastb.unsqueeze(2).to_broadcast([128, G, 4]), ALU.subtract), .94)
            DV.wait(t, t_cst)
            c = DV.mark(lambda e: e.tensor_reduce(fl[:, 5:6], past, AX.X, ALU.max), .94)
            d = DV.mark(lambda e: e.tensor_reduce(fl[:, 6:7], drel, AX.X, ALU.min), .94)
            t_prep["over"] = (c, d)

        def quads_of_blocks():
            began = PE.at
            for i in range(NQ):
                yield PE, lambda: [began + QGAP * (i - QE)], []
                yield from quad(i)
            clear_agg()

        def windows():
            for part, (wa, wz) in enumerate(parts):
                yield DV, lambda: [t_win[wz - 1], t_prep.get(("rk", part - 1), LATER) if part else None], []
                windows_elementwise(part)
                for w in range(wa, wz):
                    yield from windows_turn(w)

        def window_counts():
            began = DV.at
            for w in range(WG):
                yield DV, lambda: [t_ww[w], began + GAP * w,
                                   t_prep.get(("rk", 0 if w < parts[0][1] else 1), LATER)], []
                counts(w)
            yield SP, lambda: [t_prep["j"] if len(t_rk) == WG else LATER], []
            t = spread_counts()
            yield SP, lambda: [t], []
            gather_counts(t)
            yield PE, lambda: [t_cs, free["PM0"]], ["PM0"]
            turn_counts()
            yield DV, lambda: [t_prep["cT"]], []
            keep_counts()
            held.discard("PM0")

        def scaling():
            yield DV, lambda: [t_w, t_c32], []
            scales()
            yield DV, lambda: [*t_prep["sc"]], []
            t = powers()
            yield PE, lambda: [t, free["PM1"]], ["PM1"]
            powers_turned(t)
            yield DV, lambda: [t_prep["sT"]], []
            t = scaled_weights()
            yield PE, lambda: [t], []
            bias_rows(t)
            yield DV, lambda: [t_prep["bT"]], []
            keep_biases()
            held.discard("PM1")

        NQ = -(-NB // 4)
        LEAD, GAP, QGAP = 6, 7.0, 12.0
        ends = {max(g for g in range(G) if S.bank[g] == k): k for k in range(NK)}
        for t in range(LEAD):
            onehot(t)
        for t in range(min(NT, GAN)):
            gather(t)
            if t < WG:
                window_weight(t)
        def tiles():
            for t in range(NT):
                yield PE, lambda: [t_ga.get(t, LATER), t_oh.get(t, LATER), t_ea.get(t // 4, LATER)], []
                tile(t)
                if t % 4 == 3 and t // 4 in ends:
                    k = ends[t // 4]
                    yield AC, lambda: [t_l0[t], t_X.get(k - 1, LATER) if k else None, t_prep.get("over", [LATER])[0]], []
                    step_evac(k, t)
                    start(step(k), 1.0)

        def onehots():
            for t in range(LEAD, NT):
                yield DV, lambda: [t_l0.get(t - OHN, LATER) if t >= OHN else None], []
                onehot(t)

        def gathers():
            for t in range(GAN, NT):
                yield PO, lambda: [t_l0.get(t - GAN, LATER)], []
                gather(t)

        def edge_loads():
            for g in range(EAN, G):
                yield SP, lambda: [t_l0.get(4 * (g - EAN) + 3, LATER)], []
                load_ea(g)

        for favour, g in ((3.0, tiles), (3.0, onehots), (3.0, gathers), (3.0, edge_loads), (.5, reach), (.5, quads_of_blocks), (.5, windows), (.3, window_counts),
                          (.5, scaling), (.4, count_products), (.2, count_quads), (0, conv1_stream), (0, loader), (0, early_loader),
                          (0, make_flag)):
            start(g(), favour)
        for hh in range(NH):
            start(node1(hh), .8 - .01 * hh)
            if HW * D * hh < 128 * S.dense:
                start(conv2_half(hh), -.01 * hh)
        for n, (bl, sums) in enumerate(batch2()):
            start(node2(n, bl, sums), .4)
        for favour, g in ((2.0, gathers2), (2.0, onehots2), (2.0, tiles2)):
            start(g(), favour)
        run_tasks()
        SP.wait(*t_st.values())

        g1, g2 = xs[:, :, :].rearrange("p b f -> p (b f)"), agg[:, :]
        places = {}
        at = 0
        for n, w in (("C", 129), ("msg", 257), ("rsum", 258), ("eq", 128), ("eqw", 128), ("junk", 128)):
            places[n] = g1[:, at:at + w]
            at += w
        at = 0
        for n, w in (("nA", 258), ("nX", 128), ("nH", 128), ("tT", 512), ("o1", 128)):
            places[n] = g2[:, at:at + w]
            at += w
        places |= {"drow": l0[:, 0:128].bitcast(I32), "col": l0[:, 128:136], "coli": l0[:, 136:140].bitcast(I32),
                   "s1": l0[:, 140:160], "o2": l0[:, 160:288],
                   "h0_d": h0_d, "idn": idn, "bb": bb,
                   "W": {"WI": WI, "WJ": WJ, "WE": WE, "WS": WS, "W1L": W1L, "W1R": W1R, "W2L": W2L, "W2R": W2R}}
        loops = general_path(nc, T, S, out, sem, places, P)
        ends_ = [(q.sem, q.n) for q in (PE, DV, AC, PO)] + [t_st[0], t_st[1]]

        def finish(e, q, name):
            q.wait(t_prep["flag"])
            for f in q.ops:
                f(e)
            v = e.value_load(flag[0:1, 0:1], min_val=0, max_val=1 << 20)
            with e.If(v != 0):
                for x, n in ends_:
                    e.wait_ge(x, n)
                for L in loops:
                    if not L.ops[name]:
                        continue
                    if L.rounds == 1:
                        for f in L.ops[name]:
                            f(e, 0)
                        continue
                    with e.Fori(0, L.rounds) as i:
                        for f in L.ops[name]:
                            f(e, i)
            e.end_ifs()

        block = ctx.enter_context(nc.Block())

        @block.sync
        def _(e):
            finish(e, SP, "SP")

        @block.gpsimd
        def _(e):
            finish(e, PO, "PO")

        @block.scalar
        def _(e):
            finish(e, AC, "AC")

        @block.tensor
        def _(e):
            finish(e, PE, "PE")

        @block.vector
        def _(e):
            finish(e, DV, "DV")


def arrays_of(S, x, src, dst, edge_attr_128, edge_weight, L0_gnn_W_msg, L0_gnn_W_self,
              L1_gnn_W1_l, L1_gnn_b1_l, L1_gnn_W1_r, L1_gnn_W2_l, L1_gnn_b2_l, L1_gnn_W2_r):
    import numpy as np

    def rows(a, n, fill=0):
        a = np.asarray(a)
        o = np.full((n,) + a.shape[1:], fill, a.dtype)
        o[:len(a)] = a
        return o

    def natural(a):
        return np.ascontiguousarray(a.reshape(S.g, 128, 4).transpose(1, 0, 2).reshape(128, S.nt))

    A = {"x": rows(x, S.np), "ea": rows(edge_attr_128, S.ep)}
    A["src"], A["dst"], A["ew"] = rows(src, S.ep), rows(dst, S.ep, S.np - 1), rows(edge_weight, S.ep)
    for k in ("src", "dst", "ew"):
        A[k + "_n"] = natural(A[k])
    A["heads"] = np.ascontiguousarray(rows(A["dst"][::64], S.hb * 128, S.np - 1).reshape(S.hb, 128).T)
    Wm = np.asarray(L0_gnn_W_msg)
    A["WI"], A["WJ"], A["WE"] = (np.ascontiguousarray(Wm[128 * i:128 * i + 128]) for i in range(3))
    A["WS"] = np.asarray(L0_gnn_W_self)
    A["W1L"], A["W1R"], A["W2L"], A["W2R"] = (np.ascontiguousarray(np.asarray(w).T)
                                             for w in (L1_gnn_W1_l, L1_gnn_W1_r, L1_gnn_W2_l, L1_gnn_W2_r))
    A["W1Ln"], A["W1Rn"] = np.asarray(L1_gnn_W1_l), np.asarray(L1_gnn_W1_r)
    A["b1"], A["b2"] = np.asarray(L1_gnn_b1_l), np.asarray(L1_gnn_b2_l)
    i128 = np.arange(128)
    c16 = np.concatenate([i128, np.repeat(i128 + 1, 4), np.repeat(np.arange(1, S.key + 1), 4)])
    A["iow"] = np.tile(np.arange(128 * S.wg).astype(np.float16), (128, 1))
    A["c16"] = np.tile(c16.astype(np.float16), (128, 1))
    w5 = D * (i128[:, None] + 128 * np.arange(S.wg)[None, :])
    A["c32"] = np.concatenate([np.eye(128), w5], 1).astype(np.float32)
    A["gen"] = np.concatenate([np.tri(128, k=-1), S.np + i128[:, None]], 1).astype(np.float32)
    A["base"] = np.tile(np.array(S.base + [w - 1 for w in S.wid], np.float32), (128, 1))
    return A


def kernel(**inputs):
    import numpy as _np
    import concourse.bacc as _bacc
    from concourse import mybir as _mybir
    from concourse.bass_utils import run_bass_kernel_spmd as _run

    S = FULL
    A = arrays_of(S, **{k: _np.asarray(v) for k, v in inputs.items()})
    nc = _bacc.Bacc("TRN2", target_bir_lowering=False, num_devices=1)
    arrays, T = {}, {}
    for name, a in A.items():
        a = _np.ascontiguousarray(a)
        arrays[f"in_{name}_dram"] = a
        T[name] = nc.dram_tensor(f"in_{name}_dram", a.shape, _mybir.dt.from_np(a.dtype), kind="ExternalInput").ap()
    out = nc.dram_tensor("out_0_dram", (S.np, 128), F32, kind="ExternalOutput").ap()
    gnn_kernel(nc, T, S, out)
    r = _run(nc, [arrays], core_ids=[0])
    return r.results[0]["out_0_dram"][:S.n]
```

```python
import concourse.bass as bass
from concourse import mybir
from contextlib import ExitStack

F32 = mybir.dt.float32
F16 = mybir.dt.float16
FP8 = mybir.dt.float8e4
I32 = mybir.dt.int32
ALU = mybir.AluOpType
ACT = mybir.ActivationFunctionType
AX = mybir.AxisListType

X0, XP = 4, 8
HI_BY, LO_BY = "AAAAADD", "PPPPPDD"
FETCH = 1.0
PELAG = 0.0
MIXF = 4.5
EA_AT = 3
SF = .01
WSF = 2.75
AHEAD = 2
D = 5
SL = 128
HW = 64
OW = 76
STRAY = 30
STEP = 384
HSCALE = 4096.0
WSCALE = 256.0
ESCALE = 64.0
WMAX = 65504.0 / WSCALE


class Shape:

    def __init__(self, n, e, groups, cut, starts):
        self.n, self.e = n, e
        self.nb = -(-n // 128)
        self.np = self.nb * 128
        self.g = -(-e // 512)
        self.ep = self.g * 512
        self.nt = self.g * 4
        self.nw = n // D
        self.wg = -(-self.nw // 128)
        self.hb = -(-(self.ep // 64) // 128)
        self.nh = -(-self.nw // HW)
        self.key = D * self.nb
        self.kx = self.key + D
        self.qg = groups
        assert n % (2 * D) == 0 and self.ep - e >= 128 and 2 * self.kx <= 512
        self.base, self.wid = [], []
        for g in range(self.g):
            u = min(1.0, (512 * g + 256) / e)
            half = min(OW // 2, round(8 + STRAY * n ** .5 / 79 * max(.2, 2 * (u * (1 - u)) ** .5)))
            self.wid.append(2 * half if g < self.g - 1 else OW)
            for j in range(4):
                mid = min(round((512 * g + 128 * j + 64) * n / e), n)
                lo = max(0, min(mid - half, self.np - 2 * half))
                self.base.append(lo if g < self.g - 1 else self.np - OW)
        self.starts, self.nk = starts + [self.np], len(starts)
        self.bank = [max(k for k in range(self.nk) if starts[k] <= self.base[4 * g]) for g in range(self.g)]
        assert all(x % 128 == 0 for x in starts) and all(z - a <= STEP for a, z in zip(starts, self.starts[1:]))
        assert all(self.base[4 * g + 3] + self.wid[g] <= self.starts[self.bank[g] + 1] + (128 if self.bank[g] < self.nk - 1 else 0)
                   for g in range(self.g))
        self.late = tuple(range(self.nb - 4, self.nb))
        assert starts[-4:] == [128 * b for b in self.late] and groups[-1][1] == self.late[0]
        self.cut = cut
        self.g2 = min(g for g in range(self.g) if self.base[4 * g + 3] + self.wid[g] > cut)
        self.from2 = cut - 128
        self.bank2 = {g: (max(self.base[4 * g], self.from2) - self.from2) // STEP for g in range(self.g2, self.g)}
        assert self.base[4 * self.g2] >= self.from2

    def windows(self, hh):
        return min(HW, self.nw - HW * hh)

    def width(self, hh):
        return D * self.windows(hh)


FULL = Shape(6250, 106250, [(0, 6), (6, 12), (12, 18), (18, 24), (24, 30), (30, 33), (33, 39), (39, 42), (42, 43), (43, 45)],
             4668, [*range(0, 5760, 384), 5504, 5760, 5888, 6016, 6144])


class Queue:

    due = {}

    def __init__(self, sem, cost, lag=0.0):
        self.sem, self.n, self.ops, self.seen = sem, 0, [], {}
        self.at, self.cost, self.lag = 0.0, cost, lag

    def wait(self, *tokens):
        for t in tokens:
            if t is None:
                continue
            sem, v = t
            if self.seen.get(id(sem), 0) < v:
                self.seen[id(sem)] = v
                self.ops.append(lambda e, sem=sem, v=v: e.wait_ge(sem, v))
                self.at = max(self.at, self.due.get((id(sem), v), 0.0) + 0.1)

    def run(self, f, cost=None):
        self.at += cost or self.cost
        self.ops.append(f)

    def mark(self, f, cost=None):
        self.n += 1
        self.at += cost or self.cost
        self.due[id(self.sem), self.n] = self.at + self.lag
        self.ops.append(lambda e: f(e).then_inc(self.sem, 1))
        return (self.sem, self.n)

    def dma(self, f, ds, cost=2.5):
        ds.n += 16
        self.at += self.cost
        self.due[id(ds.sem), ds.n] = self.at + cost
        self.ops.append(lambda e: f(e).then_inc(ds.sem, 16))
        return (ds.sem, ds.n)


class DmaSem:
    def __init__(self, sem):
        self.sem, self.n = sem, 0


class Steps:

    def __init__(self, rounds):
        self.rounds = rounds
        self.ops = {x: [] for x in ("SP", "PO", "AC", "PE", "DV")}

    def do(self, engine, f, after=None, then=None):
        ops = self.ops[engine]
        if after is not None:
            link, n = after
            ops.append(lambda e, i: e.wait_ge(link, n))
            ops.append(lambda e, i: e.sem_clear(link))
        if then is None:
            ops.append(f)
        else:
            to, by = then
            ops.append(lambda e, i: f(e, i).then_inc(to, by))


def general_path(nc, T, S, out, sem, M, P):
    NB, NP, NT = S.nb, S.np, S.nt
    rows = NP + 128
    acc = [nc.dram_tensor(f"acc{i}_d", [rows, w], F32).ap() for i, w in enumerate((258, 128, 128))]
    x1_d, h0_d, h1_d, h2_d = (nc.dram_tensor(n, [NP, 128], F32).ap() for n in ("x1_d", "h0g_d", "h1_d", "h2g_d"))
    links = ("go", "to_po", "to_dv", "gathered", "eq_pe", "sums", "dv_po", "dv_pe", "dv_sp", "dv_ac", "dv", "po_dma",
             "ac_dv", "ac_sp", "ac", "pe", "stored")
    (go, to_po, to_dv, gathered, eq_pe, sums, dv_po, dv_pe, dv_sp, dv_ac, dv, po_dma,
     ac_dv, ac_sp, ac, pe, stored) = (sem("g_" + n) for n in links)
    src_r, dst_r, ew_r = (T[k].rearrange("(n o) -> n o", o=1) for k in ("src", "dst", "ew"))
    dst_c = T["dst"].rearrange("(o n) -> o n", o=1)
    C, msg, rsum, eq, eqw, junk, drow = M["C"], M["msg"], M["rsum"], M["eq"], M["eqw"], M["junk"], M["drow"]
    col, coli = M["col"], M["coli"]
    low, dummy = C[:, 0:128], C[:, 128:129]
    ds = bass.ds
    loops = []

    L = Steps(1)
    L.do("SP", lambda e, i: e.dma_start(C, T["gen"]), then=(to_dv, 16))
    L.do("SP", lambda e, i: e.dma_start(M["Wall"][:, 0:4, :], T["W"][:, 0:4, :]), then=(to_dv, 16))
    L.do("DV", lambda e, i: e.memset(rsum, 0.0), (to_dv, 32), (dv, 1))
    L.do("DV", lambda e, i: e.memset(msg[:, 256:257], 1.0), (dv, 1), (dv_sp, 1))
    for n, a in enumerate(acc):
        w = a.shape[1]
        L.do("SP", lambda e, i, a=a, w=w: e.dma_start(
            a.rearrange("(b p) f -> p b f", p=128), rsum[:, 0:w].unsqueeze(1).to_broadcast([128, rows // 128, w])),
            (dv_sp, 1) if n == 0 else None, (stored, 16))
    L.do("SP", lambda e, i: e.sem_inc(go, 1), (stored, 48))
    loops.append(L)

    def settled(L, then):
        L.do("PO", lambda e, i: e.wait_ge(po_dma, 16))
        L.do("PO", lambda e, i: e.dma_reset(range(po_dma.num, po_dma.num + 1)))
        L.do("PO", lambda e, i: e.sem_clear(po_dma))
        L.do("PO", lambda e, i: e.sem_inc(then, 1))

    def edges(table, a, first):
        w = 258 if first else 128
        L = Steps(NT)
        tile = lambda v, i: v[ds(i * 128, 128), :]
        L.do("SP", lambda e, i: e.dma_start(coli[:, 0:1], tile(src_r, i)), (go, 1), (to_po, 16))
        L.do("SP", lambda e, i: e.dma_start(coli[:, 1:2], tile(dst_r, i)), None, (to_po, 16))
        L.do("SP", lambda e, i: e.dma_start(col[:, 0:1], tile(ew_r, i)), None, (to_po, 16))
        L.do("SP", lambda e, i: e.dma_start(drow, dst_c[:, ds(i * 128, 128)].to_broadcast([128, 128])), None, (to_po, 16))
        if first:
            L.do("SP", lambda e, i: e.dma_start(msg[:, 128:256], tile(T["ea"], i)), None, (to_po, 16))
        L.do("PO", lambda e, i: e.indirect_dma_start(msg[:, 0:128], None, table, bass.IndirectOffsetOnAxis(coli[:, 0:1], 0)),
             (to_po, 80 if first else 64), (po_dma, 16))
        settled(L, gathered)
        L.do("DV", lambda e, i: e.tensor_copy(col[:, 1:2], coli[:, 1:2]), (gathered, 1), (dv, 1))
        L.do("DV", lambda e, i: e.tensor_scalar(eq, drow, col[:, 1:2], 0.0, ALU.is_equal, ALU.add,
                                                accum_out=rsum[:, 257:258]), (dv, 1), (dv, 1))
        L.do("DV", lambda e, i: e.scalar_tensor_tensor(junk, drow, col[:, 1:2], low, ALU.is_equal, ALU.mult,
                                                       accum_out=col[:, 2:3]), (dv, 1), (dv, 1))
        L.do("DV", lambda e, i: e.tensor_tensor(col[:, 3:4], dummy, col[:, 1:2], ALU.subtract), (dv, 1), (dv, 1))
        L.do("DV", lambda e, i: e.scalar_tensor_tensor(col[:, 4:5], col[:, 2:3], 0.5, col[:, 3:4], ALU.is_gt, ALU.mult),
             (dv, 1), (dv, 1))
        L.do("DV", lambda e, i: e.tensor_tensor(coli[:, 2:3], col[:, 4:5], col[:, 1:2], ALU.add), (dv, 1),
             (dv, 1) if first else (eq_pe, 1))
        if first:
            L.do("DV", lambda e, i: e.tensor_scalar(eqw, eq, col[:, 0:1], None, ALU.mult), (dv, 1), (eq_pe, 1))
            L.do("PE", lambda e, i: e.matmul(P["PA"][:, 0:257], eqw, msg[:, 0:257], start=True, stop=True), (eq_pe, 1), (sums, 1))
            L.do("DV", lambda e, i: e.tensor_copy(rsum[:, 0:257], P["PA"][:, 0:257]), (sums, 1), (dv_po, 1))
        else:
            L.do("PE", lambda e, i: e.matmul(P["PA"][:, 0:128], eq, msg[:, 0:128], start=True, stop=True), (eq_pe, 1), (sums, 1))
            L.do("DV", lambda e, i: e.tensor_copy(rsum[:, 0:128], P["PA"][:, 0:128]), (sums, 1), (dv_po, 1))
        L.do("PO", lambda e, i: e.indirect_dma_start(a, bass.IndirectOffsetOnAxis(coli[:, 2:3], 0), rsum[:, 0:w], None,
                                                     compute_op=ALU.add), (dv_po, 1), (po_dma, 16))
        settled(L, go)
        loops.append(L)

    nA, nX, nH, tT, o1, o2, s1 = M["nA"], M["nX"], M["nH"], M["tT"], M["o1"], M["o2"], M["s1"]
    W, bb, idn = M["W"], M["bb"], M["idn"]
    blk = lambda v, i: v[ds(i * 128, 128), :]

    def turned(L, parts, weights, then):
        m = len(parts)
        for j, v in enumerate(parts):
            L.do("PE", lambda e, i, j=j, v=v: e.transpose(P["PA"][:, 128 * j:128 * j + 128], v, idn),
                 (dv_pe, 1) if j == 0 else None, (pe, 1) if j == m - 1 else None)
        L.do("DV", lambda e, i: e.tensor_copy(tT[:, 0:128 * m], P["PA"][:, 0:128 * m]), (pe, 1), (dv_pe, 1))
        for j, w in enumerate(weights):
            L.do("PE", lambda e, i, j=j, w=w: e.matmul(P["PB"][:, 0:128], tT[:, 128 * j:128 * j + 128], w,
                                                       start=j == 0, stop=j == m - 1),
                 (dv_pe, 1) if j == 0 else None, then if j == m - 1 else None)

    def normed(L, v, o, by, then):
        L.do("DV", lambda e, i: e.bn_stats(s1[:, 0:6], v), (dv, 1), (dv, 1))
        L.do("DV", lambda e, i: e.bn_aggr(s1[:, 6:8], s1[:, 0:6]), (dv, 1), (dv, 1))
        L.do("DV", lambda e, i: e.tensor_scalar(s1[:, 8:9], s1[:, 7:8], 1e-5, None, ALU.add), (dv, 1), (dv_ac, 1))
        L.do("AC", lambda e, i: e.activation(s1[:, 9:10], s1[:, 8:9], ACT.Sqrt), (dv_ac, 1), (ac_dv, 1))
        L.do("DV", lambda e, i: e.reciprocal(s1[:, 10:11], s1[:, 9:10]), (ac_dv, 1), (dv, 1))
        L.do("DV", lambda e, i: e.tensor_scalar(s1[:, 11:12], s1[:, 10:11], by, None, ALU.mult), (dv, 1), (dv, 1))
        L.do("DV", lambda e, i: e.scalar_tensor_tensor(s1[:, 12:13], s1[:, 6:7], -1.0, s1[:, 11:12], ALU.mult, ALU.mult),
             (dv, 1), (dv_ac, 1))
        L.do("AC", lambda e, i: e.activation(o, v, ACT.Relu, bias=s1[:, 12:13], scale=s1[:, 11:12]), (dv_ac, 1), then)

    L = Steps(NB)
    L.do("SP", lambda e, i: e.dma_start(nX, blk(T["x"], i)), (go, 1), (to_dv, 16))
    L.do("DV", lambda e, i: e.sem_inc(dv, 1), (to_dv, 16))
    normed(L, nX, o2, 1.0, (ac_sp, 1))
    L.do("SP", lambda e, i: e.dma_start(blk(h0_d, i), o2), (ac_sp, 1), (stored, 16))
    L.do("SP", lambda e, i: e.sem_inc(go, 1), (stored, 16))
    loops.append(L)

    edges(h0_d, acc[0], True)
    L = Steps(NB)
    L.do("SP", lambda e, i: e.dma_start(nA, blk(acc[0], i)), (go, 1), (to_dv, 16))
    L.do("SP", lambda e, i: e.dma_start(nX, blk(T["x"], i)), None, (to_dv, 16))
    L.do("SP", lambda e, i: e.dma_start(nH, blk(h0_d, i)), None, (to_dv, 16))
    L.do("DV", lambda e, i: e.tensor_scalar(o1, nH, nA[:, 256:257], None, ALU.mult), (to_dv, 48), (dv_pe, 1))
    turned(L, (nA[:, 0:128], nA[:, 128:256], o1, nH), (W["WJ"], W["WE"], W["WI"], W["WS"]), (sums, 1))
    L.do("DV", lambda e, i: e.tensor_tensor(o1, P["PB"][:, 0:128], nX, ALU.add), (sums, 1), (dv, 1))
    normed(L, o1, o2, HSCALE, (ac_sp, 1))
    L.do("SP", lambda e, i: e.dma_start(blk(x1_d, i), o1), (ac_sp, 1), (stored, 16))
    L.do("SP", lambda e, i: e.dma_start(blk(h1_d, i), o2), None, (stored, 16))
    L.do("SP", lambda e, i: e.sem_inc(go, 1), (stored, 32))
    loops.append(L)

    def conv(a, h_d, wl, wr, by, bias):
        L = Steps(NB)
        L.do("SP", lambda e, i: e.dma_start(nA[:, 0:128], blk(a, i)), (go, 1), (to_dv, 16))
        L.do("SP", lambda e, i: e.dma_start(nA[:, 256:258], acc[0][ds(i * 128, 128), 256:258]), None, (to_dv, 16))
        L.do("SP", lambda e, i: e.dma_start(nX, blk(x1_d, i)), None, (to_dv, 16))
        L.do("SP", lambda e, i: e.dma_start(nH, blk(h_d, i)), None, (to_dv, 16))
        L.do("DV", lambda e, i: e.tensor_scalar(s1[:, 0:1], nA[:, 257:258], 1.0, None, ALU.max), (to_dv, 64), (dv, 1))
        L.do("DV", lambda e, i: e.reciprocal(s1[:, 1:2], s1[:, 0:1]), (dv, 1), (dv, 1))
        L.do("DV", lambda e, i: e.tensor_scalar(o2, nA[:, 0:128], s1[:, 1:2], by, ALU.mult, ALU.mult), (dv, 1), (dv_pe, 1))
        turned(L, (o2, nH), (wl, wr), (sums, 1))
        L.do("DV", lambda e, i: e.tensor_tensor(o1, P["PB"][:, 0:128], bias, ALU.add), (sums, 1), (dv, 1))
        loops.append(L)
        return L

    edges(h1_d, acc[1], False)
    L = conv(acc[1], h1_d, W["W1L"], W["W1R"], 1.0, bb[:, 0, :])
    L.do("DV", lambda e, i: e.tensor_scalar(o2, o1, 0.0, None, ALU.max), (dv, 1), (dv_sp, 1))
    L.do("SP", lambda e, i: e.dma_start(blk(h2_d, i), o2), (dv_sp, 1), (stored, 16))
    L.do("SP", lambda e, i: e.sem_inc(go, 1), (stored, 16))

    edges(h2_d, acc[2], False)
    L = conv(acc[2], h2_d, W["W2L"], W["W2R"], 1.0, bb[:, 1, :])
    L.do("DV", lambda e, i: e.tensor_reduce(s1[:, 2:3], o1, AX.X, ALU.max, negate=True), (dv, 1), (dv_ac, 1))
    L.do("AC", lambda e, i: e.activation(o2, o1, ACT.Exp, bias=s1[:, 2:3], accum_out=s1[:, 3:4]), (dv_ac, 1), (ac, 1))
    L.do("AC", lambda e, i: e.activation(s1[:, 4:5], s1[:, 3:4], ACT.Ln), (ac, 1), (ac_dv, 1))
    L.do("DV", lambda e, i: e.tensor_tensor(s1[:, 5:6], s1[:, 4:5], s1[:, 2:3], ALU.subtract), (ac_dv, 1), (dv, 1))
    L.do("DV", lambda e, i: e.scalar_tensor_tensor(o2, o1, s1[:, 5:6], nX, ALU.subtract, ALU.add), (dv, 1), (dv_sp, 1))
    L.do("SP", lambda e, i: e.dma_start(blk(out, i), o2), (dv_sp, 1), (stored, 16))
    L.do("SP", lambda e, i: e.sem_inc(go, 1), (stored, 16))
    L = Steps(1)
    L.do("SP", lambda e, i: e.wait_ge(go, 1))
    loops.append(L)
    return loops


def gnn_kernel(nc, T, S, out):
    NB, NP, G, NT, WG, HB = S.nb, S.np, S.g, S.nt, S.wg, S.hb
    KEY, KX, NH, NW = S.key, S.kx, S.nh, S.nw
    ctx = ExitStack()
    with ctx:
        def sb(name, shape, dt=F32):
            return ctx.enter_context(nc.sbuf_tensor(name, shape, dt))

        def sem(name):
            return ctx.enter_context(nc.semaphore(name))

        def dsem(name):
            return DmaSem(sem(name))

        h0_d = nc.dram_tensor("h0_d", [NP, 256], F16).ap()
        h2_d = nc.dram_tensor("h2_d", [NP, 256], F16).ap()
        sdw_d = nc.dram_tensor("sdw_d", [HB * 128 * 64, 3], I32).ap()
        cs_d = nc.dram_tensor("cs_d", [2, WG * 128 * D], F32).ap()
        c_d = nc.dram_tensor("c_d", [NH, 128, NB * HW * D], FP8).ap()

        xs = sb("xs", [128, NB, 128])
        agg = sb("agg", [128, NP])
        h0b = agg[:, :].bitcast(F16).rearrange("p (b f) -> p b f", f=256)
        h0 = agg[:, :].bitcast(F16).rearrange("p (b a f) -> p a b f", a=2, f=128)
        R = sb("R", [128, NB, 128])
        h1r = sb("h1r", [128, NB * 128])
        h1 = h1r[:, :].bitcast(F16).rearrange("p (a b f) -> p a b f", a=2, f=128)
        EAN, ESN, GAN, OHN, QN = 3, 3, 16, 3, 3
        L0W = EAN * 512 + ESN * 512 + GAN * 128 + OHN * OW * 4
        l0 = sb("l0", [128, max(NB * 128, L0W)])
        h2 = l0[:, 0:NB * 128].bitcast(F16).rearrange("p (b a f) -> p a b f", a=2, f=128)
        at = 0
        ea = l0[:, at:at + EAN * 512].rearrange("p (n f) -> p n f", n=EAN)
        at += EAN * 512
        es = l0[:, at:at + ESN * 512].bitcast(F16).rearrange("p (n a f) -> p n a f", n=ESN, a=2)
        at += ESN * 512
        ga = l0[:, at:at + GAN * 128].bitcast(F16).rearrange("p (n f) -> p n f", n=GAN)
        at += GAN * 128
        oh = l0[:, at:at + OHN * OW * 4].bitcast(F16).rearrange("p (n a c j) -> p n a c j", n=OHN, a=2, j=4)
        eq = sb("eq", [128, 2, OW, 4], F16)
        CW = (NB + 1) * HW * D
        cbr = sb("cbr", [128, CW // 2])
        cb = cbr[:, :].bitcast(FP8)
        win = h1r[:, :] if NB >= 3 * WG else sb("win", [128, 3 * 128 * WG])[:, :]
        win3 = win[:, 0:384 * WG].rearrange("p (k a) -> p k a", a=3)
        wsrc, wdst = (win3[:, :, i].bitcast(I32) for i in (0, 1))
        wdf, wew = win3[:, :, 1], win3[:, :, 2]
        wkr = win[:, 0:384 * WG].bitcast(F16).rearrange("p (k a) -> p a k", a=6)
        src_n = sb("src_s", [128, NT], I32)
        drel = sb("drel", [128, NT], F16)
        w16 = sb("w16", [128, G, 2, 4], F16)
        spare0 = cbr[:, 0:NB * 128].rearrange("p (b f) -> p b f", f=128)
        raw = cbr[:, NB * 128:NB * 128 + 2 * NT] if NB * 128 + 2 * NT <= CW // 2 else sb("raw", [128, 2 * NT])[:, :]
        dst_n, ew_n = raw[:, 0:NT].bitcast(I32), raw[:, NT:2 * NT]
        c16 = sb("c16_s", [128, 4 * max(KEY, 128)], F16)
        IK = c16[:, :].rearrange("p (r w) -> p r w", w=4)
        early = R[:, :, :].rearrange("p b f -> p (b f)")
        early = early[:, NB * 128 - 128 * WG - G:]
        lastb = early[:, 128 * WG:128 * WG + G]
        QE = min(-(-NB // 4), 5)
        WH = 128 * ((WG + 1) // 2)
        if NB * 128 - 128 * WG - G - 512 * QE >= 3 * WH:
            tmp = R[:, :, :].rearrange("p b f -> p (b f)")[:, 512 * QE:512 * QE + 3 * WH]
        else:
            tmp = sb("tmp", [128, 3 * WH])
        tmp = tmp.rearrange("p (n k) -> p n k", n=3)
        iow = early[:, 0:64 * WG].bitcast(F16)
        d64 = early[:, 64 * WG:128 * WG].rearrange("p (w s) -> p w s", s=64)
        assert 192 * HB <= 512 * QE and 128 * HB + NT + G <= ESN * 512 + GAN * 128 and 64 * HB <= 1024
        flat = l0[:, EAN * 512:EAN * 512 + 128 * HB].bitcast(I32).rearrange("p (a k) -> p a k", a=2)
        rowb = l0[0:1, EAN * 512 + 128 * HB:EAN * 512 + 128 * HB + NT + G]
        mixed = R[:, :, :].rearrange("p b f -> p (b f)")[:, 0:192 * HB].bitcast(I32)
        c32 = sb("c32_s", [128, 128 + WG])
        idn = c32[:, 0:128]
        w5 = c32[:, 128:128 + WG]
        id16 = sb("id16", [128, 128], F16)
        ones16 = sb("ones16", [128, 128], F16)
        zero16 = sb("zero16", [128, 128], F16)
        any16 = c16[:, 0:512]
        ones = sb("ones", [128, 128])
        heads = sb("heads_s", [128, HB], I32)
        hs = sb("hs", [128, HB])
        rk = sb("rk", [128, QN * 512 + QN * 4 * KX + 256 * WG], F16)[:, :]
        ohr = rk[:, 0:QN * 512].rearrange("p (n r w) -> p n r w", n=QN, w=4)
        ohk = rk[:, QN * 512:QN * 512 + QN * 4 * KX].rearrange("p (n k w) -> p n k w", n=QN, w=4)
        rT, kT = (rk[:, QN * 512 + QN * 4 * KX + 128 * WG * i:][:, 0:128 * WG] for i in (0, 1))
        TAIL = NH * HW * D
        tails = [cb.rearrange("p (q k) -> p q k", q=2)[:, :, CW - TAIL:], rk.bitcast(FP8)[:, 0:2 * TAIL].rearrange("p (q k) -> p q k", q=2)]
        AT = sb("AT", [128, 2, 512])
        BT = sb("BT", [128, 2, 512])
        blocks = BT[:, :, :].rearrange("p a k -> p (a k)")[:, 0:64 * HB].bitcast(I32).rearrange("p (i s) -> p i s", s=64)
        rest = h1r[:, 384 * WG:NB * 128] if NB >= 3 * WG else sb("rest", [128, 97 * HB + 1])[:, :]
        before = rest[:, 0:64 * HB].bitcast(I32).rearrange("p (i s) -> p i s", s=64)
        dif = rest[:, 64 * HB:64 * HB + (65 * HB + 1) // 2].bitcast(F16)[:, 0:65 * HB].rearrange("p (i s) -> p i s", s=65)
        W = sb("W", [128, 8, 128])
        WI, WS, WJ, WE, W1L, W1R, W2L, W2R = (W[:, i, :] for i in range(8))
        bcol = sb("bcol", [128, 1])
        brow = sb("brow", [1, 2, 128])
        bb = sb("bb", [128, 2, 128])
        H = sb("H", [128, 2, 384])
        wn = H[:, 0, 0:256].rearrange("p (a f) -> p a f", a=2)
        diag = H[:, 1, 0:128]
        HT = sb("HT", [128, 2, 512])
        cmp = [v.rearrange("p a k -> p (a k)").bitcast(F16)[:, 384 * i:384 * i + 384] for v in (HT[:, :, :], AT[:, :, :]) for i in range(5)]
        st6 = sb("st6", [128, NB, 6])
        mv = sb("mv", [128, NB, 2])
        sd = sb("sd", [128, NB])
        rs = sb("rs", [128, NB])
        nb_ = sb("nb_", [128, NB])
        kk = sb("kk", [128, WG])
        idx2 = sb("idx2", [128, WG], I32)
        c64 = sb("c64", [128, WG])
        cs = sb("cs", [128, 2, WG, D])
        csr = H[0:NB, 1, 128:384].rearrange("p (a f) -> p a f", a=2)
        inv = sb("inv", [128, 2, NB])
        sw = sb("sw", [128, NB])
        sc = sb("sc", [128, 8])
        sci = sb("sci", [128, 2], I32)
        fl = sb("fl", [128, 12])
        flag_f = sb("flag_f", [1, 8])
        flag = sb("flag", [1, 1], I32)
        sm = sb("sm", [128, 4, 4])
        rmax = sb("rmax", [128, NH])
        junk = sb("junk", [128, HW * D], F16)

        names = ["PA", "PB", "PC0", "PC1", "PV0", "PV1", "PM0", "PM1"]
        P = {n: ctx.enter_context(nc.psum_tensor(n, [128, 512], F32)) for n in names}
        free = dict.fromkeys(names)

        Queue.due = {}
        PE, DV, AC, PO, SP = (Queue(sem("s_" + n), *c) for n, *c in (
            ("pe", .23, PELAG), ("dv", .2), ("ac", .42), ("po", 1.04), ("sp", .06)))

        def mm(o, l, r, start, stop):
            return lambda e: e.matmul(o, l, r, start=start, stop=stop, skip_group_check=True)

        LATER = (None, 0)
        held, tasks = set(), []

        SPAN = .15

        def start(g, favour):
            tasks.append([favour, g, next(g)])

        def begin(x):
            q, needs, takes = x[2]
            if held.intersection(takes):
                return 1e9
            ts = needs()
            if LATER in ts:
                return 1e9
            return max([q.at, *(t if type(t) is float else Queue.due.get((id(t[0]), t[1]), 0.0) for t in ts if t)])

        def later(t, by):
            return Queue.due.get((id(t[0]), t[1]), 0.0) + by if t and t != LATER else t

        def run_tasks():
            while tasks:
                at = [(begin(x), -x[0], n) for n, x in enumerate(tasks)]
                first = min(at)
                assert first[0] < 1e8, [y[1].__name__ for y in tasks]
                q = tasks[first[2]][2][0]
                x = tasks[min((-tasks[n][0], b, n) for b, _, n in at if b < first[0] + SPAN and tasks[n][2][0] is q)[2]]
                held.update(x[2][2])
                try:
                    x[2] = next(x[1])
                except StopIteration:
                    tasks.remove(x)

        def finish_now(g):
            for _, needs, takes in g:
                assert LATER not in needs() and not held.intersection(takes)
                held.update(takes)

        d_a, d_c, d_nat, d_w, d_row = dsem("d_a"), dsem("d_c"), dsem("d_nat"), dsem("d_w"), dsem("d_row")
        d_blk, d_flat = dsem("d_blk"), dsem("d_flat")
        bus = [2.0]

        def transfer(o, i, ds, kb):
            bus[0] = max(bus[0], SP.at + 1.2) + kb / 360
            return SP.dma(lambda e: e.dma_start(o, i), ds, bus[0] + 1.0 - SP.at)

        pieces = [(0, min(NB, X0))] + [(b, min(NB, b + XP)) for b in range(X0, NB, XP)]
        piece_of = [next(i for i, (a, z) in enumerate(pieces) if a <= b < z) for b in range(NB)]
        NP_ = len(pieces)
        xv = T["x"].rearrange("(b p) f -> p b f", p=128)
        t_x = {}

        def load_x(i):
            if i < NP_:
                b0, b1 = pieces[i]
                t_x[i] = transfer(xs[:, b0:b1, :], xv[:, b0:b1, :], dsem(f"d_x{i}"), 64 * (b1 - b0))

        t_head = transfer(heads[:, :], T["heads"], d_a, 8)
        load_x(0)
        load_x(1)
        transfer(blocks, T["blocks"], d_blk, HB * 32)
        t_blk = transfer(before, T["before"], d_blk, HB * 32)
        t_c32 = transfer(c32[:, :], T["c32"], d_c, 70)
        transfer(flat[:, 0, :], T["src_b"], d_flat, HB * 32)
        load_x(2)
        t_flat = transfer(flat[:, 1, :].bitcast(F32), T["ew_b"], d_flat, HB * 32)
        for i in range(3, NP_):
            load_x(i)
        t_rows = transfer(rowb, T["rows"], d_row, 4)
        for o, i, kb in ((W[:, :, :], T["W"], 520), (wn[:, :, :], T["Wn"], 130), (bcol[:, :], T["b"][0].rearrange("(p o) -> p o", o=1), 1),
                         (brow[:, :, :], T["b"].unsqueeze(0), 1)):
            t_w = transfer(o, i, d_w, kb)

        t_iota = PO.mark(lambda e: e.iota(iow, pattern=[[1, 128 * WG]], base=0, channel_multiplier=0,
                                          allow_small_or_imprecise_dtypes=True), 2.9)
        for o, by in ((zero16[:, :], 0.0), (ones16[:, :], 1.0), (dif[:, :, 64:65], 1.0), (cs[:, :, :, :], 0.0), (fl[:, :], 0.0),
                      (ohk[:, :, KEY + 1:KX, :], 0.0), (ohk[:, :, KEY:KEY + 1, :], 1.0)):
            PO.run(lambda e, o=o, by=by: e.memset(o, by), .06)
        t_cst = PO.mark(lambda e: e.memset(ones[:, :], 1.0), .15)
        DV.wait(t_iota)
        t_IK = DV.mark(lambda e: e.tensor_scalar(IK, iow[:, 0:c16.shape[1] // 4].unsqueeze(2).to_broadcast([128, c16.shape[1] // 4, 4]),
                                                 1.0, None, ALU.add), .6)
        AC.wait(t_cst)
        AC.run(lambda e: e.activation(sc[:, 7:8], ones[:, 0:1], ACT.Sqrt), 1.5)

        def mix():
            nonlocal t_mix, t_sdw, t_nat
            m3 = mixed.rearrange("p (k a) -> p k a", a=3)
            for i, v, ready in ((1, blocks.rearrange("p i s -> p (i s)"), t_blk), (0, flat[:, 0, :], t_flat), (2, flat[:, 1, :], t_flat)):
                yield PO, lambda: [ready], []
                PO.wait(ready)
                t_mix = PO.mark(lambda e, i=i, v=v: e.tensor_copy(m3[:, :, i], v), 2.9)
            SP.wait(t_mix)
            t_sdw = transfer(sdw_d.rearrange("(i p s) a -> p i (s a)", p=128, s=64), mixed.rearrange("p (i k) -> p i k", k=192),
                             dsem("d_sdw"), HB * 96)
            transfer(dst_n, T["dst_n"], d_nat, NT / 2)
            transfer(ew_n, T["ew_n"], d_nat, NT / 2)
            t_nat = transfer(src_n[:, :], T["src_n"], d_nat, NT / 2)

        ea_v = T["ea"].rearrange("(g j p) f -> g p j f", p=128, j=4)
        d_ea = [dsem(f"d_ea{i}") for i in range(EAN)]
        t_ea, t_sp = {}, {}

        def load_ea(g):
            if g >= EAN:
                SP.wait(t_sp[g - EAN])
            t_ea[g] = transfer(ea[:, g % EAN, :].rearrange("p (j f) -> p j f", j=4), ea_v[g], d_ea[g % EAN], 256)

        d_h0 = dsem("d_h0")
        t_h0, t_h0d, t_mix, t_sdw, t_nat, t_pe, t_relu = {}, None, None, None, None, [None, None], {}

        def h0_stats(i):
            b0, b1 = pieces[i]
            yield DV, lambda: [t_x[i], t_relu.get(i - AHEAD, LATER) if i >= AHEAD else None], []
            DV.wait(t_x[i])
            for b in range(b0, b1):
                if b > b0:
                    yield DV, lambda: [], []
                t = DV.mark(lambda e, b=b: e.bn_stats(st6[:, b, :], xs[:, b, :]), .203)
            DV.wait(t)
            for b in range(b0, b1):
                t = DV.mark(lambda e, b=b: e.bn_aggr(mv[:, b, :], st6[:, b, :]), .075)
            DV.wait(t)
            t = DV.mark(lambda e: e.tensor_scalar(sd[:, b0:b1], mv[:, b0:b1, 1], 1e-5, HSCALE ** -2, ALU.add, ALU.mult), .1)
            start(h0_scale(i, t), 5)

        def h0_scale(i, t):
            b0, b1 = pieces[i]
            yield AC, lambda: [t], []
            AC.wait(t)
            t = AC.mark(lambda e: e.activation(sd[:, b0:b1], sd[:, b0:b1], ACT.Sqrt), .1)
            yield DV, lambda: [t], []
            DV.wait(t)
            t = DV.mark(lambda e: e.reciprocal(rs[:, b0:b1], sd[:, b0:b1]), .12)
            DV.wait(t)
            t = DV.mark(lambda e: e.scalar_tensor_tensor(
                nb_[:, b0:b1], mv[:, b0:b1, 0], -1.0, rs[:, b0:b1], ALU.mult, ALU.mult), .1)
            start(h0_piece(i, t), 4 - .1 * i)

        def h0_piece(i, t):
            nonlocal t_h0d
            b0, b1 = pieces[i]
            for b in range(b0, b1):
                yield AC, lambda: [t], []
                AC.wait(t)
                t1 = AC.mark(lambda e, b=b: e.activation(spare0[:, b, :], xs[:, b, :], ACT.Relu,
                                                         bias=nb_[:, b:b + 1], scale=rs[:, b:b + 1]), .387)
                t_relu[i] = t1
            name = HI_BY[min(i, len(HI_BY) - 1)]
            q, cost = {"A": (AC, .2 + .092 * (b1 - b0)), "D": (DV, .07 + .067 * (b1 - b0)), "P": (PO, .1 + .26 * (b1 - b0))}[name]
            yield q, lambda: [t1], []
            q.wait(t1)
            if name == "A":
                t2 = AC.mark(lambda e: e.activation(h0[:, 0, b0:b1, :], spare0[:, b0:b1, :], ACT.Copy), cost)
            else:
                t2 = q.mark(lambda e: e.tensor_copy(h0[:, 0, b0:b1, :], spare0[:, b0:b1, :]), cost)
            name = LO_BY[min(i, len(LO_BY) - 1)]
            q, cost = {"D": (DV, .07 + .133 * (b1 - b0)), "P": (PO, .05 + .256 * (b1 - b0))}[name]
            yield q, lambda: [t2], []
            q.wait(t2, t1)
            t_h0[i] = q.mark(lambda e: e.tensor_tensor(
                h0[:, 1, b0:b1, :], spare0[:, b0:b1, :], h0[:, 0, b0:b1, :], ALU.subtract), cost)
            if i == max(0, NP_ - EA_AT):
                for g in range(EAN):
                    load_ea(g)
            SP.wait(t_h0[i])
            t_h0d = transfer(h0_d.rearrange("(b p) f -> p b f", p=128)[:, b0:b1, :], h0b[:, b0:b1, :], d_h0, 64 * (b1 - b0))

        t_drel = t_w16 = t_wsc = t_id16 = t_last = None

        def edge_places():
            nonlocal t_drel, t_last
            cut = NT // 2
            yield PE, lambda: [t_rows, t_cst], []
            PE.wait(t_rows, t_cst)
            for bank, a, z in (("PM0", 0, cut), ("PM1", cut, NT), ("PC0", NT, NT + G)):
                t = PE.mark(mm(P[bank][:, 0:z - a], ones[0:1, :], rowb[:, a:z], True, True), (z - a) / 300)
            yield DV, lambda: [t, t_nat or LATER, t_i2 or LATER], []
            DV.wait(t, t_nat)
            for bank, a, z in (("PM0", 0, cut), ("PM1", cut, NT)):
                t_drel = free[bank] = DV.mark(lambda e, bank=bank, a=a, z=z: e.tensor_tensor(
                    drel[:, a:z], dst_n[:, a:z], P[bank][:, 0:z - a], ALU.subtract), .5)
            t_last = free["PC0"] = DV.mark(lambda e: e.tensor_copy(lastb, P["PC0"][:, 0:G]), .3)

        def edge_weights():
            nonlocal t_w16, t_id16
            ew4 = AT[:, :, :].rearrange("p a k -> p (a k)")[:, 0:NT].rearrange("p (g j) -> p g j", j=4)
            yield DV, lambda: [t_nat or LATER, t_starts[0] or LATER], []
            DV.wait(t_nat, t_starts[0], t_c32)
            t = DV.mark(lambda e: e.tensor_scalar(ew4, ew_n.rearrange("p (g j) -> p g j", j=4), -WMAX, WMAX, ALU.max, ALU.min), .5)
            t_id16 = DV.mark(lambda e: e.tensor_copy(id16[:, :], idn), .14)
            yield AC, lambda: [t], []
            AC.wait(t)
            t2 = AC.mark(lambda e: e.activation(w16[:, :, 0, :], ew4, ACT.Copy, scale=WSCALE), .8)
            yield DV, lambda: [t2], []
            DV.wait(t2, t)
            t_w16 = DV.mark(lambda e: e.scalar_tensor_tensor(w16[:, :, 1, :], ew4, WSCALE, w16[:, :, 0, :], ALU.mult, ALU.subtract), .94)

        t_win, t_c64, t_starts, t_i2 = {}, None, [None], None
        d_win = [dsem("d_win0"), dsem("d_win1")]

        def window_starts():
            nonlocal t_c64, t_i2
            yield DV, lambda: [t_head, t_cst], []
            DV.wait(t_head, t_cst)
            t_hs = DV.mark(lambda e: e.tensor_scalar(hs[:, :], heads[:, :], 0.5, 1.0 / D, ALU.add, ALU.mult), .08)
            yield DV, lambda: [t_blk], []
            DV.wait(t_blk)
            t_dif = DV.mark(lambda e: e.tensor_tensor(dif[:, :, 0:64], blocks, before, ALU.subtract), .94)
            t_cmp = {}
            half = -(-WG // 2)
            banks = [("PV0", 0, half), ("PV1", half, WG)]
            PE.wait(t_cst, t_dif)
            for bank, a, z in banks:
                PE.run(mm(P[bank][:, 0:65 * (z - a)], zero16[:, :], iow[:, 0:65 * (z - a)], True, False))
            for i in range(HB):
                tiles_ = range(64 * i, min(NT, 64 * i + 64))
                lo = min(S.base[t] for t in tiles_)
                hi = max(S.base[t] + S.wid[t // 4] for t in tiles_) if 64 * i + 64 <= NT else NP
                some = [w for w in range(WG) if D * (128 * w + 127) > lo and D * 128 * w <= hi]
                c, t_free = cmp[i % len(cmp)], t_cmp.get(i - len(cmp))
                if some:
                    a, z = some[0], some[-1] + 1
                    assert z - a <= 3
                    yield DV, lambda: [t_hs, t_free], []
                    DV.wait(t_hs, t_free)
                    t = DV.mark(lambda e, i=i, c=c, a=a, z=z: e.tensor_scalar(
                        c[:, 0:128 * (z - a)], iow[:, 128 * a:128 * z], hs[:, i:i + 1], None, ALU.is_gt), .06 + .033 * (z - a))
                    PE.wait(t)
                else:
                    z = next((w for w in range(WG) if D * 128 * w > hi), WG)
                    a = z
                for bank, wa, wz in banks:
                    for w in range(max(a, wa), wz):
                        PE.run(mm(P[bank][:, 65 * (w - wa):65 * (w - wa) + 65],
                                  c[:, 128 * (w - a):128 * (w - a) + 128] if w < z else ones16[:, :], dif[:, i, :], False, False), .054)
                t_cmp[i] = PE.mark(mm(P["PV0"][:, 0:65], zero16[:, :], dif[:, i, :], False, i == HB - 1), .054)
            t_pe[0] = t_pe[1] = PE.mark(mm(P["PV1"][:, 0:65], zero16[:, :], dif[:, 0, :], False, True), .054)
            yield DV, lambda: [t_pe[0], t_c32], []
            DV.wait(t_pe[0], t_c32)
            for bank, a, z in banks:
                v = P[bank][:, 0:65 * (z - a)].rearrange("p (w s) -> p w s", s=65)
                DV.mark(lambda e, v=v, a=a, z=z: e.tensor_scalar(kk[:, a:z].unsqueeze(2), v[:, :, 64:65], -1.0, 0.0, ALU.add, ALU.max), .08)
                t = free[bank] = DV.mark(lambda e, v=v, a=a, z=z: e.tensor_tensor(
                    d64[:, a:z, :], v[:, :, 0:64], w5[:, a:z].unsqueeze(2).to_broadcast([128, z - a, 64]), ALU.is_lt), .4)
            DV.wait(t)
            t = DV.mark(lambda e: e.tensor_reduce(c64[:, :], d64, AX.X, ALU.add), .73)
            DV.wait(t)
            t = t_c64 = DV.mark(lambda e: e.scalar_tensor_tensor(kk[:, :], kk[:, :], 64.0, c64[:, :], ALU.mult, ALU.add), .08)
            DV.wait(t)
            t_starts[0] = t_i2 = DV.mark(lambda e: e.tensor_scalar(idx2[:, :], kk[:, :], float(S.ep - SL), None, ALU.min), .08)

        def fetch_windows():
            for w in range(WG):
                yield PO, lambda: [t_i2 or LATER, t_sdw or LATER], []
                PO.wait(t_i2, t_sdw)
                t_win[w] = PO.dma(lambda e, w=w: e.indirect_dma_start(
                    win[:, 384 * w:384 * w + 384].bitcast(I32), None, sdw_d, bass.IndirectOffsetOnAxis(idx2[:, w:w + 1], 0)),
                    d_win[0 if w < (WG + 1) // 2 else 1])

        start(window_starts(), WSF)
        start(mix(), MIXF)
        for i in range(NP_):
            start(h0_stats(i), 3 - SF * i)
        def undo_powers():
            nonlocal t_wsc
            for v, by in ((W[:, 0:2, :], 1 / HSCALE), (WJ, 1 / HSCALE / WSCALE), (WE, 1 / ESCALE / WSCALE)):
                yield AC, lambda: [t_w, t_i2 or LATER], []
                AC.wait(t_w)
                t_wsc = AC.mark(lambda e, v=v, by=by: e.activation(v, v, ACT.Copy, scale=by), .23)

        start(undo_powers(), .7)
        start(edge_places(), .8)
        start(edge_weights(), .8)
        start(fetch_windows(), FETCH)
        run_tasks()

        d_ga = [dsem(f"d_ga{i}") for i in range(GAN)]
        t_eh, t_ga, t_oh, t_l0 = {}, {}, {}, {}
        PRODUCTS = ((0, 0), (0, 1), (1, 0), (1, 1))

        def split_hi(g):
            AC.wait(t_ea[g], t_mix, t_l0[4 * (g - ESN) + 3] if g >= ESN else None)
            t_eh[g] = AC.mark(lambda e: e.activation(es[:, g % ESN, 0, :], ea[:, g % EAN, :], ACT.Copy, scale=ESCALE, saturate=False), .52)

        def split_lo(g):
            DV.wait(t_eh[g])
            if g == 0:
                DV.mark(lambda e: e.tensor_reduce(fl[:, 9:10], ea[:, 0, :], AX.X, ALU.max), .6)
            t_sp[g] = DV.mark(lambda e: e.scalar_tensor_tensor(
                es[:, g % ESN, 1, :], ea[:, g % EAN, :], ESCALE, es[:, g % ESN, 0, :], ALU.mult, ALU.subtract), .61)

        def gather(t):
            if t >= GAN:
                PO.wait(t_l0[t - GAN])
            t_ga[t] = PO.dma(lambda e: e.indirect_dma_start(
                ga[:, t % GAN, :], None, h0_d, bass.IndirectOffsetOnAxis(src_n[:, t:t + 1], 0)), d_ga[t % GAN])

        def equal(o, g):
            w = S.wid[g]
            return DV.mark(lambda e: e.tensor_tensor(
                o, IK[:, 0:w, :], drel[:, 4 * g:4 * g + 4].unsqueeze(1).to_broadcast([128, w, 4]), ALU.is_equal), .07 + w / 480)

        def onehot(g):
            w = S.wid[g]
            DV.wait(t_w16, t_IK, t_l0[4 * (g - OHN) + 3] if g >= OHN else None)
            DV.wait(t_oh.get(g - 2))
            t = equal(eq[:, g % 2, 0:w, :], g)
            DV.wait(t)
            t_oh[g] = DV.mark(lambda e: e.tensor_tensor(
                oh[:, g % OHN, :, 0:w, :], eq[:, g % 2, 0:w, :].unsqueeze(1).to_broadcast([128, 2, w, 4]),
                w16[:, g, :, :].unsqueeze(2).to_broadcast([128, 2, w, 4]), ALU.mult), .07 + w / 240)

        def tile(t):
            g, j = t // 4, t % 4
            k = S.bank[g]
            if t == 0 or (j == 0 and S.bank[g - 1] != k):
                PE.wait(free["PA"])
                PE.run(mm(P["PA"][:, 0:span[k]], zero16[:, :], any16[:, 0:span[k]], True, False))
                PE.wait(free["PB"])
                PE.run(mm(P["PB"][:, 0:span[k]], zero16[:, :], any16[:, 0:span[k]], True, False))
            at = S.base[t] - S.starts[k]
            last = t == NT - 1 or (j == 3 and S.bank[g + 1] != k)
            w = S.wid[g]
            hi, lo = (oh[:, g % OHN, a, 0:w, j] for a in (0, 1))
            PE.wait(t_oh[g])
            for bank, v, ready in (("PA", (ga[:, t % GAN, 0:128], ga[:, t % GAN, 128:256]), t_ga[t]),
                                   ("PB", tuple(es[:, g % ESN, a, 128 * j:128 * j + 128] for a in (0, 1)), t_sp[g])):
                PE.wait(ready)
                o = P[bank][:, at:at + w]
                for n, (l, r) in enumerate(PRODUCTS):
                    f = mm(o, v[l], (hi, lo)[r], False, last and n == len(PRODUCTS) - 1)
                    if bank == "PA" or n < len(PRODUCTS) - 1:
                        PE.run(f, w / 2.1e3)
            t_l0[t] = PE.mark(f, w / 2.1e3)

        t_quad, t_ht, t_qht = {}, [None, None], {}

        def quad(i):
            b0, b1 = 4 * i, min(NB, 4 * i + 4)
            m = b1 - b0
            yield PE, lambda: [t_id16, t_h0[piece_of[b1 - 1]], free["PM1"]], ["PM1", "HT0"]
            PE.wait(t_id16, t_h0[piece_of[b1 - 1]], free["PM1"])
            for j in range(m):
                o = P["PM1"][:, 128 * j:128 * j + 128]
                PE.run(mm(o, h0[:, 0, b0 + j, :], id16[:, :], True, False), .06)
                f = mm(o, h0[:, 1, b0 + j, :], id16[:, :], False, True)
                if j < m - 1:
                    PE.run(f, .06)
            t = PE.mark(f, .06)
            yield AC, lambda: [t, t_ht[0]], []
            AC.wait(t, t_ht[0], t_pe[0], t_pe[1])
            free["PM1"] = t_qht[i] = AC.mark(lambda e: e.activation(HT[:, 0, 0:128 * m], P["PM1"][:, 0:128 * m], ACT.Copy))
            held.discard("PM1")
            yield PE, lambda: [t_qht[i], t_wsc, free["PM0"], free["PV0"]], ["PM0", "PV0"]
            PE.wait(t_qht[i], t_wsc, free["PM0"], free["PV0"])
            for bank, w in (("PM0", WS), ("PV0", WI)):
                for j in range(m):
                    f = mm(P[bank][:, 128 * j:128 * j + 128], HT[:, 0, 128 * j:128 * j + 128], w, True, True)
                    if bank == "PM0" or j < m - 1:
                        PE.run(f, .26)
            t2 = PE.mark(f, .26)
            t_ht[0] = t2
            held.discard("HT0")
            x4 = xs[:, b0:b1, :].rearrange("p b f -> p (b f)")
            yield DV, lambda: [t2], []
            DV.wait(t2, t_h0[piece_of[b1 - 1]])
            t_q0 = free["PM0"] = DV.mark(lambda e: e.tensor_tensor(x4, P["PM0"][:, 0:128 * m], x4, ALU.add), .6)
            held.discard("PM0")
            yield AC, lambda: [t2] + ([t_prep.get(("rk", 1), LATER), t_prep.get("over", [LATER])[0]] if i >= QE else []), []
            AC.wait(t2, t_c64, t_drel, t_sdw, t_prep["rk", 1] if i >= QE else None, t_prep["over"][0] if i >= QE else None)
            free["PV0"] = AC.mark(lambda e: e.activation(R[:, b0:b1, :].rearrange("p b f -> p (b f)"),
                                                         P["PV0"][:, 0:128 * m], ACT.Copy), .48)
            held.discard("PV0")
            t_quad[i] = (t_q0, free["PV0"])

        V = 128 * WG
        t_prep = {}

        parts = [(0, (WG + 1) // 2), ((WG + 1) // 2, WG)]
        r16, k16 = {}, {}

        def windows_elementwise(part):
            wa, wz = parts[part]
            c = slice(128 * wa, 128 * wz)
            n = 128 * (wz - wa)
            fT, v_ = tmp[:, 0, 0:n], tmp[:, 1, 0:n]
            ri = tmp[:, 2, 0:n].bitcast(I32)
            d_ = wdf[:, c]
            s_ = wsrc[:, c]
            DV.wait(t_win[wz - 1], t_c32, t_prep.get(("rk", 0)))
            t = DV.mark(lambda e: e.tensor_scalar(ri, s_, 127, None, ALU.bitwise_and), .41)
            t2 = DV.mark(lambda e: e.tensor_tensor(
                d_.rearrange("p (c s) -> p c s", s=128), wdst[:, c].rearrange("p (c s) -> p c s", s=128),
                w5[:, wa:wz].unsqueeze(2).to_broadcast([128, wz - wa, 128]), ALU.subtract), .74)
            DV.wait(t)
            t3 = DV.mark(lambda e: e.tensor_tensor(fT, s_, ri, ALU.subtract), .74)
            DV.wait(t2)
            t4 = DV.mark(lambda e: e.tensor_scalar(v_, d_, 0.0, None, ALU.is_ge), .41)
            DV.wait(t4)
            t4 = DV.mark(lambda e: e.scalar_tensor_tensor(v_, d_, float(D), v_, ALU.is_lt, ALU.mult), .74)
            DV.wait(t3)
            t3 = DV.mark(lambda e: e.scalar_tensor_tensor(fT, fT, D / 128.0, d_, ALU.mult, ALU.add), .74)
            DV.wait(t3, t4)
            k_, r_ = wkr[:, 0, c], wkr[:, 1, c]
            DV.mark(lambda e: e.tensor_scalar(k_, fT, 1.0, None, ALU.add), .41)
            t5 = DV.mark(lambda e: e.scalar_tensor_tensor(r_, ri, 1.0, v_, ALU.add, ALU.mult), .74)
            t_prep["rk", part] = t5
            for w in range(wa, wz):
                k16[w] = k_[:, 128 * (w - wa):128 * (w - wa) + 128]
                r16[w] = r_[:, 128 * (w - wa):128 * (w - wa) + 128]

        t_rk = {}

        def windows_turn(w):
            bank = "PM1"
            yield PE, lambda: [t_prep.get(("rk", 0 if w < parts[0][1] else 1), LATER), free[bank]], [bank]
            PE.wait(t_prep["rk", 0 if w < parts[0][1] else 1], free[bank], t_id16)
            v = P[bank][:, :].bitcast(F16)
            PE.run(lambda e: e.transpose(v[:, 0:128], r16[w], id16[:, :]), .06)
            t = PE.mark(lambda e: e.transpose(v[:, 128:256], k16[w], id16[:, :]), .06)
            t_prep["turn"] = t
            yield AC, lambda: [t], []
            AC.wait(t)
            AC.run(lambda e: e.activation(rT[:, 128 * w:128 * w + 128], v[:, 0:128], ACT.Copy), .2)
            t2 = AC.mark(lambda e: e.activation(kT[:, 128 * w:128 * w + 128], v[:, 128:256], ACT.Copy), .2)
            free[bank] = t_rk[w] = t2
            held.discard(bank)

        t_junk = []

        def counts(w):
            pw = min(128, NW - 128 * w)
            d_ = wdf[0:pw, 128 * w:128 * w + 128]
            DV.wait(t_cst, *t_pe)
            for i in range(D):
                if i:
                    yield DV, lambda: [], []
                n = len(t_junk)
                if n > 1:
                    DV.wait(*t_junk[n - 2])
                j0, j1 = (HT[0:pw, 1, 128 * x:128 * x + 128] for x in (n % 2 * 2, n % 2 * 2 + 1))
                t = DV.mark(lambda e, i=i, j0=j0: e.tensor_scalar(j0, d_, float(i), 0.0, ALU.is_equal, ALU.add,
                                                                  accum_out=cs[0:pw, 0, w, i:i + 1]))
                t2 = DV.mark(lambda e, i=i, j1=j1: e.scalar_tensor_tensor(j1, d_, float(i), wew[0:pw, 128 * w:128 * w + 128],
                                                                          ALU.is_equal, ALU.mult,
                                                                          accum_out=cs[0:pw, 1, w, i:i + 1]))
                t_junk.append((t, t2))
            t_prep["j"] = t2

        d_cs = dsem("d_cs")

        def spread_counts():
            SP.wait(t_prep["j"])
            for i in range(2):
                t = SP.dma(lambda e, i=i: e.dma_start(
                    cs_d[i].rearrange("(c w d) -> w c d", w=128, d=D), cs[:, i, :, :]), d_cs)
            return t

        def gather_counts(t):
            nonlocal t_cs
            SP.wait(t)
            for i in range(2):
                t = SP.dma(lambda e, i=i: e.dma_start(
                    csr[:, i, :], cs_d[i, 0:NP].rearrange("(b p) -> b p", p=128)), d_cs)
            t_cs = t

        t_cs = None

        def turn_counts():
            PE.wait(t_cs, free["PM0"])
            PE.run(lambda e: e.transpose(P["PM0"][:, 0:NB], csr[:, 0, :], idn[0:NB, 0:NB]))
            t = PE.mark(lambda e: e.transpose(P["PM0"][:, 64:64 + NB], csr[:, 1, :], idn[0:NB, 0:NB]))
            t_prep["cT"] = t

        def keep_counts():
            DV.wait(t_prep["cT"])
            t = DV.mark(lambda e: e.tensor_scalar(inv[:, 0, :], P["PM0"][:, 0:NB], 1.0, None, ALU.max))
            t_prep["sw"] = free["PM0"] = DV.mark(lambda e: e.tensor_copy(sw[:, :], P["PM0"][:, 64:64 + NB]))
            DV.wait(t)
            t_prep["inv"] = DV.mark(lambda e: e.reciprocal(inv[:, 1, :], inv[:, 0, :]))

        t_base = {}

        def add_hi(b):
            DV.wait(t_prep["sw"], *t_quad[b // 4])
            t_base[b] = DV.mark(lambda e: e.scalar_tensor_tensor(
                xs[:, b, :], R[:, b, :], sw[:, b:b + 1], xs[:, b, :], ALU.mult, ALU.add), .26)

        def scales():
            DV.wait(t_w, t_c32)
            for i in range(2):
                t = DV.mark(lambda e, i=i: e.scalar_tensor_tensor(diag, wn[:, i, :], 1.0, wn[:, i, :], ALU.mult,
                                                                  ALU.mult, accum_out=sc[:, i:i + 1]))
                DV.wait(t)
            AC.wait(t)
            t = AC.mark(lambda e: e.activation(sc[:, 0:2], sc[:, 0:2], ACT.Sqrt))
            t2 = AC.mark(lambda e: e.activation(sc[:, 2:3], bcol[:, :], ACT.Abs))
            t_prep["sc"] = (t, t2)

        def powers():
            DV.wait(*t_prep["sc"])
            t = DV.mark(lambda e: e.tensor_tensor(sc[:, 0:1], sc[:, 0:1], sc[:, 1:2], ALU.add))
            DV.wait(t)
            t = DV.mark(lambda e: e.scalar_tensor_tensor(sc[:, 0:1], sc[:, 0:1], 11.5, sc[:, 2:3], ALU.mult, ALU.add))
            DV.wait(t)
            t = DV.mark(lambda e: e.tensor_scalar(sc[:, 0:1], sc[:, 0:1], 1e-30, 1e30, ALU.max, ALU.min))
            DV.wait(t)
            t = DV.mark(lambda e: e.tensor_scalar(sci[:, 0:1], sc[:, 0:1].bitcast(I32), 0x7F800000, None, ALU.bitwise_and))
            DV.wait(t)
            t = DV.mark(lambda e: e.tensor_scalar(sci[:, 1:2], sci[:, 0:1], -1.0, float(254 << 23), ALU.mult, ALU.add))
            t2 = DV.mark(lambda e: e.tensor_scalar(sc[:, 4:5], sci[:, 0:1].bitcast(F32), 2.0 ** -14, None, ALU.mult))
            DV.wait(t, t2)
            t = DV.mark(lambda e: e.tensor_scalar(sc[:, 3:4], sci[:, 1:2].bitcast(F32), 2.0 ** 14, None, ALU.mult))
            DV.wait(t)
            t = DV.mark(lambda e: e.tensor_scalar(diag, idn, sc[:, 3:4], None, ALU.mult))
            t2 = DV.mark(lambda e: e.tensor_scalar(W2L, W2L, sc[:, 4:5], None, ALU.mult))
            t3 = DV.mark(lambda e: e.tensor_scalar(W2R, W2R, sc[:, 4:5], None, ALU.mult))
            t_prep["w2"] = (t2, t3)
            return t

        def powers_turned(t):
            PE.wait(t, t_cst, free["PM1"])
            t_prep["sT"] = PE.mark(mm(P["PM1"][:, 0:128], ones[:, :], diag, True, True))

        def scaled_weights():
            DV.wait(t_prep["sT"])
            t1 = DV.mark(lambda e: e.scalar_tensor_tensor(W1L, W1L, 1.0 / HSCALE, P["PM1"][:, 0:128], ALU.mult, ALU.mult))
            t2 = DV.mark(lambda e: e.scalar_tensor_tensor(W1R, W1R, 1.0 / HSCALE, P["PM1"][:, 0:128], ALU.mult, ALU.mult))
            t = free["PM1"] = DV.mark(lambda e: e.tensor_tensor(
                brow[:, 0, :], brow[:, 0, :], P["PM1"][0:1, 0:128], ALU.mult))
            t_prep["w1"] = (t1, t2)
            return t

        def bias_rows(t):
            PE.wait(t, *t_prep["w1"])
            t_prep["bT"] = PE.mark(mm(P["PM1"][:, 0:256], ones[0:1, :], brow[:, :, :].rearrange("o a f -> o (a f)"), True, True))

        def keep_biases():
            DV.wait(t_prep["bT"])
            t_prep["w"] = free["PM1"] = DV.mark(lambda e: e.tensor_copy(
                bb[:, :, :].rearrange("p a f -> p (a f)"), P["PM1"][:, 0:256]))

        n_prod, half_built = [(0, 0, 0)], []
        t_c, t_cst_half, t_ring, t_used = {}, {}, {}, {}
        d_cb = [dsem(f"d_cb{i}") for i in range(2)]
        t_row, t_made = {}, {}
        quads = [(hh, w, min(w + 4, S.windows(hh))) for hh in range(NH) for w in range(0, S.windows(hh), 4)]
        CB = ("PC0", "PC1", "PV1")

        def built(hh):
            return cb[:, (hh % 2) * CW:(hh % 2) * CW + (NB + 1) * S.width(hh)].rearrange("p (q k) -> p q k", q=NB + 1)

        def count_quad(i):
            hh, a, z = quads[i]
            w0 = HW * hh + a
            n = z - a
            R_ = i % QN
            DV.wait(t_rk[w0 // 128], t_ring.get(i - QN), t_cst)
            r_o, k_o = ohr[:, R_, :, 0:n], ohk[:, R_, 0:KEY, 0:n]
            DV.run(lambda e: e.tensor_tensor(
                r_o, IK[:, 0:128, 0:n], rT[:, w0:w0 + n].unsqueeze(1).to_broadcast([128, 128, n]), ALU.is_equal), .335)
            t_made[i] = DV.mark(lambda e: e.tensor_tensor(
                k_o, IK[:, 0:KEY, 0:n], kT[:, w0:w0 + n].unsqueeze(1).to_broadcast([128, KEY, n]), ALU.is_equal), .58)

        def count_quads():
            for i, (hh, a, z) in enumerate(quads):
                yield DV, lambda: [t_rk.get((HW * hh + a) // 128, LATER), t_ring.get(i - QN, LATER) if i >= QN else None], []
                count_quad(i)

        def spare_read():
            return [*t_h0.values(), t_w16, t_drel, *t_prep.get("over", [LATER])]

        def keep_counts_of(hh, w, bank, t):
            AC.wait(t)
            if hh < 2:
                AC.wait(*spare_read())
            else:
                AC.wait(t_cst_half[hh - 2], t_row[hh - 2], t_used.get(hh - 2))
            o = built(hh)[:, :, D * w:D * w + 2 * D].rearrange("p q (w d) -> p w q d", w=2)
            s_ = P[bank][:, 0:2 * KX].rearrange("p (w q d) -> p w q d", w=2, d=D)
            t_c[hh] = free[bank] = AC.mark(lambda e: e.activation(o, s_, ACT.Copy, saturate=False), .47)
            held.discard(bank)

        def store_half(hh):
            SP.wait(t_c[hh])
            t_cst_half[hh] = SP.dma(lambda e: e.dma_start(
                c_d[hh, :, 0:NB * S.width(hh)], cb[:, (hh % 2) * CW:(hh % 2) * CW + NB * S.width(hh)]), d_cb[hh % 2], 6.0)
            half_built.append(hh)

        def count_products():
            turn_ = 0
            for i, (hh, a, z) in enumerate(quads):
                n = z - a
                R_ = i % QN
                for j in range(0, n, 2):
                    bank = CB[turn_ % 3]
                    turn_ += 1
                    new = a == 0 and j == 0
                    yield (PE, lambda: [t_made.get(i, LATER), free[bank],
                                        t_row.get(hh - 2, LATER) if new and hh >= 2 else None],
                           [bank] + ([f"C{hh % 2}"] if new else []))
                    if new:
                        held.discard(f"C{hh % 2}")
                    n_prod[0] = (hh, a, j + 2)
                    PE.wait(t_made[i], free[bank])
                    PE.run(mm(P[bank][:, 0:KX], ohr[:, R_, :, j], ohk[:, R_, :, j], True, True), .105)
                    t = PE.mark(mm(P[bank][:, KX:2 * KX], ohr[:, R_, :, j + 1], ohk[:, R_, :, j + 1], True, True), .105)
                    yield AC, lambda: [t, *(spare_read() if hh < 2 else [])], []
                    keep_counts_of(hh, a + j, bank, t)
                t_ring[i] = t
                if z == S.windows(hh):
                    store_half(hh)
                    start(row_check(hh), .5)
            n_prod[0] = (NH, 0, 0)

        def row_check(hh):
            yield DV, lambda: [t_c[hh]], []
            DV.wait(t_c[hh], t_row.get(hh - 1))
            t_row[hh] = DV.mark(lambda e: e.tensor_scalar(junk[:, 0:S.width(hh)], built(hh)[:, NB, :], 15.0, 0.0,
                                                          ALU.is_gt, ALU.add, accum_out=rmax[:, hh:hh + 1]), .4)

        NK = S.nk
        span = [min(512, S.starts[k + 1] - S.starts[k] + (128 if k < NK - 1 else 0)) for k in range(NK)]
        t_ev, t_X, t_h1, t_Hfree, t_R = {}, {}, {}, [None, None], {}

        def step_blocks(k):
            return list(range(S.starts[k] // 128, S.starts[k + 1] // 128))

        def step_evac(k, last_tile):
            assert k == 0 or k - 1 in t_X
            AC.wait(t_l0[last_tile], t_X.get(k - 1), t_prep["over"][0])
            w = span[k]
            a = AC.mark(lambda e: e.activation(AT[:, k % 2, 0:w], P["PA"][:, 0:w], ACT.Copy), .06 + w / 1220)
            b = AC.mark(lambda e: e.activation(BT[:, k % 2, 0:w], P["PB"][:, 0:w], ACT.Copy), .06 + w / 1220)
            free["PA"], free["PB"] = a, b
            t_ev[k] = (a, b)

        def turn(h, bl, tH, bank, ring):
            m = len(bl)
            yield PE, lambda: [tH, free[bank]], [bank, f"HT{ring}"]
            PE.wait(tH, free[bank], t_id16)
            for i, b in enumerate(bl):
                o = P[bank][:, 128 * i:128 * i + 128]
                PE.run(mm(o, h[:, 0, b, :], id16[:, :], True, False), .06)
                f = mm(o, h[:, 1, b, :], id16[:, :], False, True)
                if i < m - 1:
                    PE.run(f, .06)
            t = PE.mark(f, .06)
            yield AC, lambda: [t, t_ht[ring]], []
            AC.wait(t, t_ht[ring], t_prep["j"])
            t_turned[ring] = free[bank] = AC.mark(lambda e: e.activation(HT[:, ring, 0:128 * m], P[bank][:, 0:128 * m], ACT.Copy))
            held.discard(bank)

        def self_term(bl, ring, bank, w, j):
            yield PE, lambda: [t_turned[ring], free[bank], t_prep.get("w", LATER)], [bank]
            PE.wait(t_turned[ring], free[bank], t_prep["w"], t_cst)
            late = j == 0 and bl[0] in S.late
            if late:
                PE.run(mm(P[bank][:, 256:384], HT[:, ring, 0:128], W1L, True, True))
            for i, b in enumerate(bl):
                f = mm(P[bank][:, 128 * i:128 * i + 128], HT[:, ring, 128 * i:128 * i + 128], w, True, True)
                if b != bl[-1]:
                    PE.run(f)
            t = PE.mark(f)
            t_ht[ring] = t
            held.discard(f"HT{ring}")
            if late:
                b, = bl
                hi, lo = h1[:, 0, b, :], h1[:, 1, b, :]
                yield AC, lambda: [t], []
                AC.wait(t)
                t_late = AC.mark(lambda e: e.activation(hi, P[bank][:, 256:384], ACT.Copy), .23)
                yield DV, lambda: [t_late], []
                DV.wait(t_late)
                t_g[b] = DV.mark(lambda e: e.tensor_tensor(lo, P[bank][:, 256:384], hi, ALU.subtract), .2)
            tb = t_base.get(bl[-1]) if j == 0 else t_T.get(bl[-1])
            yield DV, lambda: [t], []
            DV.wait(t, tb)
            free[bank] = DV.mark(lambda e: e.tensor_tensor(
                R[:, bl[0]:bl[-1] + 1, :], P[bank][:, 0:128 * len(bl)].rearrange("p (b f) -> p b f", f=128),
                bb[:, j, :].unsqueeze(1).to_broadcast([128, len(bl), 128]), ALU.add), .47)
            held.discard(bank)
            for b in bl:
                t_R[j, b] = free[bank]

        t_turned, t_g = {}, {}

        def step(k):
            bl = step_blocks(k)
            b0, b1, m = bl[0], bl[-1] + 1, len(bl)
            yield DV, lambda: [t_prep.get("sw", LATER), *[t for b in bl for t in t_quad.get(b // 4, [LATER])]], []
            for b in bl:
                add_hi(b)
            yield PE, lambda: [*t_ev[k], free["PM0"]], ["PM0"]
            PE.wait(*t_ev[k], free["PM0"], t_wsc)
            for i, b in enumerate(bl):
                o = P["PM0"][:, 128 * i:128 * i + 128]
                at = 128 * b - S.starts[k]
                ops = [(AT[:, k % 2, at:at + 128], WJ), (BT[:, k % 2, at:at + 128], WE)]
                if i == 0 and k > 0:
                    over = S.starts[k] - S.starts[k - 1]
                    ops += [(AT[:, (k - 1) % 2, over:over + 128], WJ), (BT[:, (k - 1) % 2, over:over + 128], WE)]
                for j, (l, r) in enumerate(ops):
                    f = mm(o, l, r, j == 0, j == len(ops) - 1)
                    if b != bl[-1] or j < len(ops) - 1:
                        PE.run(f)
            t_X[k] = PE.mark(f)
            xk = xs[:, b0:b1, :].rearrange("p b f -> p (b f)")
            yield DV, lambda: [t_X[k], *[t_base.get(b, LATER) for b in bl]], []
            DV.wait(t_X[k], *[t_base[b] for b in bl])
            t = free["PM0"] = DV.mark(lambda e: e.tensor_tensor(xk, P["PM0"][:, 0:128 * m], xk, ALU.add), .47)
            held.discard("PM0")
            DV.wait(t)
            for b in bl:
                t = DV.mark(lambda e, b=b: e.bn_stats(st6[:, b, :], xs[:, b, :]))
            DV.wait(t)
            for b in bl:
                t = DV.mark(lambda e, b=b: e.bn_aggr(mv[:, b, :], st6[:, b, :]), .08)
            DV.wait(t)
            t1 = DV.mark(lambda e: e.tensor_scalar(sd[:, b0:b1], mv[:, b0:b1, 1], 1e-5, HSCALE ** -2, ALU.add, ALU.mult), .08)
            yield AC, lambda: [t1], []
            AC.wait(t1)
            t2 = AC.mark(lambda e: e.activation(sd[:, b0:b1], sd[:, b0:b1], ACT.Sqrt), .1)
            yield DV, lambda: [t2], []
            DV.wait(t2)
            t = DV.mark(lambda e: e.reciprocal(rs[:, b0:b1], sd[:, b0:b1]), .11)
            DV.wait(t)
            t3 = DV.mark(lambda e: e.scalar_tensor_tensor(
                nb_[:, b0:b1], mv[:, b0:b1, 0], -1.0, rs[:, b0:b1], ALU.mult, ALU.mult), .08)
            yield AC, lambda: [t3, t_Hfree[k % 2], t_prep.get("w", LATER), t_prep.get("sw", LATER)], []
            AC.wait(t3, t_Hfree[k % 2], t_prep["w"], t_prep["sw"])
            Hk = H[:, k % 2, 0:128 * m]
            for i, b in enumerate(bl):
                t = AC.mark(lambda e, b=b, i=i: e.activation(H[:, k % 2, 128 * i:128 * i + 128], xs[:, b, :], ACT.Relu,
                                                             bias=nb_[:, b:b + 1], scale=rs[:, b:b + 1]), .39)
            if b1 > XB:
                yield AC, lambda: [], [f"S{2 * per}", f"S{2 * per + 1}"]
                held.difference_update((f"S{2 * per}", f"S{2 * per + 1}"))
                for i in (0, 1):
                    AC.wait(ring_free.get(2 * per + i))
                    DV.wait(ring_free.get(2 * per + i))
            AC.wait(t, t_prep["turn"], t_prep["j"])
            DV.wait(t_prep["turn"], t_prep["j"])
            if bl[0] in S.late:
                b, = bl
                t_h1[b] = t
                done_blocks[0] = b + 1
                yield PE, lambda: [t, free["PM1"]], ["PM1", "HT1"]
                PE.wait(t, free["PM1"], t_c32)
                t = PE.mark(lambda e: e.transpose(P["PM1"][:, 0:128], H[:, k % 2, 0:128], idn), .22)
                t_Hfree[k % 2] = t
                yield AC, lambda: [t, t_ht[1]], []
                AC.wait(t, t_ht[1])
                t_turned[1] = free["PM1"] = AC.mark(lambda e: e.activation(HT[:, 1, 0:128], P["PM1"][:, 0:128], ACT.Copy), .17)
                held.discard("PM1")
                yield from self_term(bl, 1, "PM0", W1R, 0)
                return
            hi = h1[:, 0, b0:b1, :].rearrange("p b f -> p (b f)")
            lo = h1[:, 1, b0:b1, :].rearrange("p b f -> p (b f)")
            t4 = AC.mark(lambda e: e.activation(hi, Hk, ACT.Copy))
            yield DV, lambda: [t4], []
            DV.wait(t4)
            t = DV.mark(lambda e: e.tensor_tensor(lo, Hk, hi, ALU.subtract), .47)
            t_Hfree[k % 2] = t
            for b in bl:
                t_h1[b] = t
            done_blocks[0] = bl[-1] + 1
            yield from turn(h1, bl, t, "PM1", 1)
            yield from self_term(bl, 1, "PM0", W1R, 0)

        t_T = {}
        ring_free = {}
        d_cl = [dsem(f"d_cl{i}") for i in range(10)]
        LAST = len(S.qg) - 1
        big = max(z - a for a, z in S.qg) * HW * D
        per = min(4, (CW - TAIL) // big)
        assert per > 1
        XB = NB - -(-big // 256)
        spare = [h1r[:, :].bitcast(FP8)[:, 256 * (NB * a + XB):256 * (NB * a + NB)] for a in (0, 1)]
        t_agg = {}

        def load_part(gi, hh, s):
            q0, q1 = S.qg[gi]
            wd = S.width(hh)
            half = s // per
            SP.wait(t_cst_half[hh], ring_free.get(s))
            for h in (NH - 1, NH - 2):
                if h % 2 == half:
                    SP.wait(t_cst_half[h], t_row[h], t_used.get(h))
            o = cb[:, half * CW + (s % per) * big:half * CW + (s % per) * big + (q1 - q0) * wd]
            return s, SP.dma(lambda e: e.dma_start(o, c_d[hh, :, q0 * wd:q1 * wd]), d_cl[s]), o

        def product(bank, h, th, o, q0, a, z, q1, wd, tload, n=None):
            n = n or wd
            if a == q0:
                PE.wait(tload, free[bank])
            for q in range(a, z):
                PE.wait(th[q])
                r = o[:, (q - q0) * wd:(q - q0) * wd + n]
                PE.run(mm(P[bank][:, 0:n], h[:, 0, q, :], r, q == q0, False), n / 2.35e3)
                f = mm(P[bank][:, 0:n], h[:, 1, q, :], r, False, q == q1 - 1)
                if q < z - 1:
                    PE.run(f, n / 2.35e3)
            return PE.mark(f, n / 2.35e3)

        accs = ["PV0"]
        t_aggfree = [None]
        done_blocks = [0]
        conv_todo = [(gi, hh) for gi in range(LAST + 1) for hh in range(NH)]

        def conv1_choice():
            if t_aggfree[0] is None:
                return None
            if not loading[0]:
                for hh in half_built:
                    if hh + 2 > n_prod[0][0]:
                        gs = [gi for gi in range(LAST + 1) if (gi, hh) in conv_todo and S.qg[gi][1] <= done_blocks[0]]
                        while gs and gs[-1] - gs[0] >= len(gs):
                            gs.pop()
                        if gs:
                            q0, q1 = S.qg[gs[0]][0] * S.width(hh), S.qg[gs[-1]][1] * S.width(hh)
                            return gs, hh, None, t_c[hh], cb[:, (hh % 2) * CW + q0:(hh % 2) * CW + q1]
            for x in conv_todo:
                if x in fetched and S.qg[x[0]][1] <= done_blocks[0]:
                    return [x[0]], x[1], *fetched[x]
            return None

        def conv1_stream():
            jobs = 0
            while conv_todo:
                bank = accs[jobs % len(accs)]
                jobs += 1
                pick = [None]

                def needs():
                    pick[0] = conv1_choice()
                    if pick[0] is None or (pick[0][2] is None and f"C{pick[0][1] % 2}" in held):
                        return [LATER]
                    return [pick[0][3], later(free[bank], JSLACK)]

                yield PE, needs, [bank]
                gs, hh, s, tl, o = pick[0]
                for gi in gs:
                    conv_todo.remove((gi, hh))
                if s is None:
                    held.add(f"C{hh % 2}")
                q0, q1 = S.qg[gs[0]][0], S.qg[gs[-1]][1]
                for a in range(q0, q1, PIECE):
                    z = min(q1, a + PIECE)
                    if a > q0:
                        yield PE, lambda: [], []
                    t = product(bank, h1, t_h1, o, q0, a, z, q1, S.width(hh), tl)
                if s is None:
                    t_used[hh] = t
                    held.discard(f"C{hh % 2}")
                else:
                    ring_free[s] = t
                    held.discard(f"S{s}")
                if not conv_todo:
                    last_conv1[0] = t
                start(conv1_sum(hh, bank, t, gs), .5)

        def early_loader():
            n = 0
            while not loading[0]:
                pick = [None]

                def needs():
                    pick[0] = None
                    for x in conv_todo:
                        if S.qg[x[0]][1] <= done_blocks[0] and x not in fetched and x[1] + 2 <= n_prod[0][0]:
                            pick[0] = x
                            break
                    late = loading[0] or done_blocks[0] + 2 * 3 > XB
                    return [] if late else [LATER] if pick[0] is None else [t_cst_half[pick[0][1]]]

                yield SP, needs, [f"S{2 * per + n % 2}"]
                s = 2 * per + n % 2
                if pick[0] is None or loading[0] or done_blocks[0] + 2 * 3 > XB:
                    held.discard(f"S{s}")
                    return
                n += 1
                gi, hh = pick[0]
                q0, q1 = S.qg[gi]
                wd = S.width(hh)
                o = spare[s - 2 * per][:, 0:(q1 - q0) * wd]
                SP.wait(t_cst_half[hh], ring_free.get(s), t_prep["turn"], t_prep["j"])
                fetched[pick[0]] = s, load_now(o, hh, q0 * wd, q1 * wd, d_cl[s]), o

        def load_now(o, hh, a, z, ds):
            return SP.dma(lambda e: e.dma_start(o, c_d[hh, :, a:z]), ds, 4.0)

        d_tail = dsem("d_tail")

        def load_tails():
            nonlocal t_tail
            yield SP, lambda: [LATER if n_prod[0][0] < NH else t_ring[len(quads) - 1], *[t_row.get(h, LATER) for h in range(NH)]], ["C0", "C1"]
            held.difference_update(("C0", "C1"))
            begun = t_ring[len(quads) - 1], *t_cst_half.values(), *t_row.values(), *t_used.values()
            DV.wait(*begun)
            for v in tails:
                t_pad = DV.mark(lambda e, v=v: e.memset(v[:, :, S.n:].bitcast(F16), 0.0), .1)
            SP.wait(*begun)
            began = SP.at
            for hh in range(NH):
                wd = S.width(hh)
                yield SP, lambda: [began + TGAP * hh], []
                for q, v in zip(S.late[::2], tails):
                    t = SP.dma(lambda e, hh=hh, wd=wd, q=q, v=v: e.dma_start(
                        v[:, :, HW * D * hh:HW * D * hh + wd],
                        c_d[hh, :, q * wd:(q + 2) * wd].rearrange("p (q k) -> p q k", q=2)), d_tail, 4.0)
            t_tail = (t, t_pad)

        t_tail = None
        TGAP = 4.0

        def loader():
            yield SP, lambda: [LATER if n_prod[0][0] < NH else None, *[t_row.get(h, LATER) for h in range(NH)]], ["C0", "C1"]
            held.difference_update(("C0", "C1"))
            accs[:] = ["PV0", "PV1"]
            loading[0] = True
            n = 0
            todo = [x for x in conv_todo if x not in fetched]
            for i, x in enumerate(todo):
                s = n % (2 * per)
                n += 1
                yield SP, lambda: [], [f"S{s}"]
                fetched[x] = load_part(*x, s)
            yield SP, lambda: [t_yb.get(b, LATER) for b in range(NB)], [f"S{j}" for j in range(per)]
            SP.wait(*t_yb.values())
            yield from load_half(0)
            yield SP, lambda: [last_conv1[0] or LATER, *[t_h2d.get(h, LATER) for h in range(NH)]], [f"S{j}" for j in range(per, 2 * per)]
            SP.wait(last_conv1[0], *t_Y.values())
            for hh in range(1, NH):
                if HW * D * hh < S.cut:
                    yield from load_half(hh)

        fetched, loading = {}, [False]

        def conv1_sum(hh, bank, t, gs):
            wd = S.width(hh)
            c = agg[:, HW * D * hh:HW * D * hh + wd]
            p = P[bank][:, 0:wd]
            first = hh not in sums_begun
            sums_begun.add(hh)
            if first:
                yield AC, lambda: [t], []
                AC.wait(t, t_aggfree[0])
                t_agg[hh] = free[bank] = AC.mark(lambda e: e.activation(c, p, ACT.Copy), .35)
            else:
                yield DV, lambda: [t, t_agg.get(hh, LATER)], [f"A{hh}"]
                DV.wait(t, t_agg[hh])
                t_agg[hh] = free[bank] = DV.mark(lambda e: e.tensor_tensor(c, p, c, ALU.add), .4)
                held.discard(f"A{hh}")
            held.discard(bank)
            sums_left[hh] -= len(gs)
            if not sums_left[hh]:
                t_sum[hh] = t_agg[hh]

        t_sum, sums_left = {}, [len(S.qg)] * NH
        PIECE = 4
        sums_begun = set()

        def soon(hh):
            return S.late[:1 if hh < SOON else 2]

        def late_products(o, b, qs, begins, ends=True):
            ops = [(q - S.late[0], a) for q in qs for a in (0, 1)]
            for n, (q, a) in enumerate(ops):
                f = mm(o, tails[q // 2][:, q % 2, 128 * b:128 * b + 128], h1[:, a, S.late[q], :], begins and n == 0, ends and n == len(ops) - 1)
                if n < len(ops) - 1:
                    PE.run(f, .055)
            return PE.mark(f, .055)

        def node1_early(hh):
            bl = batch(hh)
            bank = ("PC0", "PC1")[hh % 2]
            yield PE, lambda: [t_sum.get(hh, LATER), t_sum.get(max(0, hh - 1), LATER), t_aggfree[0] or LATER,
                               *[t_R.get((0, b), LATER) for b in bl], later(free[bank], ESLACK),
                               *[t_g.get(q, LATER) for q in soon(hh)], *(t_tail or [LATER])], [bank]
            PE.wait(t_sum[hh], t_sum.get(hh - 1), free[bank], t_aggfree[0], t_prep["w"], *[t_g[q] for q in soon(hh)], *t_tail)
            for j, b in enumerate(bl):
                o = P[bank][:, 128 * j:128 * j + 128]
                PE.run(mm(o, agg[:, 128 * b:128 * b + 128], W1L, True, False))
                t = late_products(o, b, soon(hh), False)
            for b in bl:
                t_yb[b] = t
            yield DV, lambda: [t], []
            DV.wait(t, t_prep["inv"])
            for j, b in enumerate(bl):
                DV.wait(t_R[0, b])
                t_R["e", b] = DV.mark(lambda e, j=j, b=b: e.scalar_tensor_tensor(
                    R[:, b, :], P[bank][:, 128 * j:128 * j + 128], inv[:, 1, b:b + 1], R[:, b, :],
                    ALU.mult, ALU.add), .27)
            free[bank] = t_R["e", bl[-1]]
            held.discard(bank)

        def clear_agg():
            DV.wait(t_h0d, t_qht[NQ - 1])
            t_aggfree[0] = DV.mark(lambda e: e.memset(agg[:, S.n:NP], 0.0)) if NP > S.n else t_qht[NQ - 1]

        def batch(hh):
            a = 0 if hh == 0 else HW * D * hh // 128
            z = NB if hh == NH - 1 else HW * D * (hh + 1) // 128
            return list(range(a, z))

        t_Y, t_hi, t_h2, t_lo, t_h2d = {}, {}, {}, {}, {}
        d_h2 = dsem("d_h2")
        Tb = [v[:, i, :] for v in (AT, BT) for i in (0, 1)]

        def node1(hh):
            bl = batch(hh)
            m = len(bl)
            bank = (AHEAD1 if hh < len(AHEAD1) else AHEAD1[:4])[hh % (len(AHEAD1) if hh < len(AHEAD1) else 4)]
            qs = S.late[len(soon(hh)):]
            if hh < len(AHEAD1):
                yield PE, lambda: [*[t_g.get(q, LATER) for q in qs[:-1]], free[bank], t_ev.get(NK - 1, [LATER])[0], *(t_tail or [LATER])], [bank]
                PE.wait(*[t_g[q] for q in qs[:-1]], free[bank], *t_tail)
                PE.run(mm(P[bank][:, 0:128 * m], zero16[:, :], any16[:, 0:128 * m], True, False), .06 * m)
                for i, b in enumerate(bl):
                    late_products(P[bank][:, 128 * i:128 * i + 128], b, qs[:-1], False, False)
                yield PE, lambda: [t_g.get(qs[-1], LATER)], []
                PE.wait(t_g[qs[-1]])
                for i, b in enumerate(bl):
                    t = late_products(P[bank][:, 128 * i:128 * i + 128], b, qs[-1:], False, i == m - 1)
            else:
                yield PE, lambda: [*[t_g.get(q, LATER) for q in qs], free[bank]], [bank]
                PE.wait(*[t_g[q] for q in qs], free[bank], *t_tail)
                for i, b in enumerate(bl):
                    t = late_products(P[bank][:, 128 * i:128 * i + 128], b, qs, True)
            t_Y[hh] = t
            yield DV, lambda: [t, *[t_R.get(("e", b), LATER) for b in bl]], [f"T{hh % 4}"]
            DV.wait(t, t_X[NK - 1], t_prep["inv"], t_lo.get(hh - 4))
            Tk = Tb[hh % 4]
            for i, b in enumerate(bl):
                DV.wait(t_R["e", b])
                t_T[b] = DV.mark(lambda e, i=i, b=b: e.scalar_tensor_tensor(
                    Tk[:, 128 * i:128 * i + 128], P[bank][:, 128 * i:128 * i + 128], inv[:, 1, b:b + 1], R[:, b, :],
                    ALU.mult, ALU.add), .27)
            t = free[bank] = t_T[bl[-1]]
            held.discard(bank)
            hi, lo = (h2[:, a, bl[0]:bl[-1] + 1, :] for a in (0, 1))
            T3 = Tk[:, 0:128 * m].rearrange("p (b f) -> p b f", f=128)
            yield AC, lambda: [t, t_l0[NT - 1]], []
            AC.wait(t, t_l0[NT - 1])
            t1 = AC.mark(lambda e: e.activation(hi, T3, ACT.Relu), .1 + .1 * m)
            if PO.at + .1 + .27 * m < DV.at + LOD * m:
                t = AC.mark(lambda e: e.activation(T3, T3, ACT.Relu), .1 + .1 * m)
                yield PO, lambda: [t], []
                PO.wait(t)
                t_lo[hh] = PO.mark(lambda e: e.tensor_tensor(lo, T3, hi, ALU.subtract), .1 + .27 * m)
            else:
                yield DV, lambda: [t1], []
                DV.wait(t1)
                t_lo[hh] = DV.mark(lambda e: e.scalar_tensor_tensor(lo, T3, 0.0, hi, ALU.max, ALU.subtract), .06 + .13 * m)
            held.discard(f"T{hh % 4}")
            SP.wait(t_lo[hh])
            t_h2d[hh] = SP.dma(lambda e: e.dma_start(
                h2_d.rearrange("(b p) f -> p b f", p=128)[:, bl[0]:bl[-1] + 1, :],
                l0[:, 128 * bl[0]:128 * bl[-1] + 128].bitcast(F16).rearrange("p (b f) -> p b f", f=256)), d_h2)
            for b in bl:
                t_h2[b] = t_lo[hh]
            start(self2(hh, bl), SELF2 - .01 * hh)

        SELF2, GLAT, EARLY, LOD = .7, 10.0, .6, .5
        SOON = 20
        AHEAD1 = ("PA", "PB", "PV0", "PV1", "PC0", "PC1")
        JSLACK, ESLACK, URGE, SOONER = 0.0, 0.0, 50, 6.0

        def self2(hh, bl):
            yield PE, lambda: [t_h2d.get(h, LATER) for h in range(NH)], []
            yield from turn(h2, bl, t_lo[hh], "PM1", hh % 2)
            yield from self_term(bl, hh % 2, "PB", W2R, 1)

        t_yb = {}

        d_l2 = [dsem(f"d_l2{i}") for i in range(2)]
        load2, half_free = {}, {}
        t_a2 = {}
        accs2 = ["PC0", "PC1"]

        def load_half(hh):
            wd = S.width(hh)
            s = hh % 2
            if hh >= 2:
                yield SP, lambda: [half_free.get(hh - 2, LATER)], []
                SP.wait(half_free[hh - 2])
            SP.wait(t_cst_half[hh])
            for i in range(s * per, s * per + per):
                SP.wait(ring_free.get(i))
            for h in (NH - 1, NH - 2):
                if h % 2 == s:
                    SP.wait(t_cst_half[h], t_row[h], t_used.get(h))
            o = cb[:, s * CW:s * CW + NB * wd]
            load2[hh] = (SP.dma(lambda e: e.dma_start(o, c_d[hh, :, 0:NB * wd]), d_l2[s], 8.0 if hh < 2 else 5.0), o)

        def conv2_half(hh):
            wd = S.width(hh)
            need_wd = min(wd, S.cut - HW * D * hh)
            bank = accs2[hh % 2]
            for a in range(0, NB, PIECE):
                z = min(NB, a + PIECE)
                need = lambda: [t_h2.get(q, LATER) for q in range(a, z)]
                if a == 0:
                    yield PE, lambda: [load2[hh][0] if hh in load2 else LATER, free[bank], *[t_yb.get(b, LATER) for b in range(NB)]] + need(), [bank]
                else:
                    yield PE, need, []
                t = product(bank, h2, t_h2, load2[hh][1], 0, a, z, NB, wd, load2[hh][0], need_wd)
            half_free[hh] = t
            c = agg[:, HW * D * hh:HW * D * hh + need_wd]
            last = min(NB - 1, (HW * D * hh + need_wd - 1) // 128)
            start(conv2_out(hh, bank, t, c, need_wd, last), .5)

        def conv2_out(hh, bank, t, c, wd, last):
            yield AC, lambda: [t, t_yb.get(last, LATER)], []
            AC.wait(t, t_yb[last])
            t_a2[hh] = free[bank] = AC.mark(lambda e: e.activation(c, P[bank][:, 0:wd], ACT.Copy), .35)
            held.discard(bank)

        t_o, t_st = {}, {}
        d_o = [dsem(f"d_o{i}") for i in range(2)]
        ov = out.rearrange("(b p) f -> p b f", p=128)

        GA2 = min(16, NB * 128 // (128 + OW // 2))
        ga2 = h1r[:, 0:128 * GA2].bitcast(F16).rearrange("p (n f) -> p n f", n=GA2)
        GA2 -= GA2 % 4
        oh2 = h1r[:, 128 * GA2:128 * GA2 + OW * GA2 // 2].bitcast(F16).rearrange("p (n c j) -> p n c j", n=GA2 // 4, j=4)
        d_g2 = [dsem(f"d_g2{i}") for i in range(GA2)]
        t_g2, t_oh2, t_m2 = {}, {}, {}
        T2 = 4 * S.g2
        N2 = max(S.bank2.values()) + 1
        last_conv1 = [None]

        def gathers2():
            yield PO, lambda: [t_h2d.get(hh, LATER) for hh in range(NH)] + [last_conv1[0] or LATER], []
            PO.wait(max(t_h2d.values(), key=lambda t: t[1]), last_conv1[0])
            for t in range(T2, NT):
                if t - T2 >= GA2:
                    yield PO, lambda: [t_m2.get(t - GA2, LATER)], []
                gather2(t)

        def gather2(t):
            PO.wait(t_m2.get(t - GA2))
            t_g2[t] = PO.dma(lambda e: e.indirect_dma_start(
                ga2[:, t % GA2, :], None, h2_d, bass.IndirectOffsetOnAxis(src_n[:, t:t + 1], 0)), d_g2[t % GA2], GLAT)

        def onehots2():
            yield DV, lambda: [last_conv1[0] or LATER, t_Y.get(NH - 1, LATER)], []
            DV.wait(last_conv1[0], *t_Y.values())
            for g in range(S.g2, G):
                old = 4 * g + 3 - GA2
                yield DV, lambda: [t_m2.get(old, LATER) if old >= T2 else None], []
                DV.wait(t_m2.get(old))
                t_oh2[g] = equal(oh2[:, g % (GA2 // 4), 0:S.wid[g], :], g)

        def tiles2():
            for t in range(T2, NT):
                g = t // 4
                j = S.bank2[g]
                bank = ("PV0", "PV1")[j % 2]
                new = t == T2 or (t % 4 == 0 and S.bank2[g - 1] != j)
                last = t == NT - 1 or (t % 4 == 3 and S.bank2[g + 1] != j)
                yield PE, lambda: [t_g2.get(t, LATER), t_oh2.get(g, LATER), free[bank]], [bank] if new else []
                if new:
                    PE.wait(free[bank], last_conv1[0])
                    PE.run(mm(P[bank][:, :], zero16[:, :], any16, True, False))
                at = S.base[t] - S.from2 - STEP * j
                w = S.wid[g]
                PE.wait(t_g2[t], t_oh2[g])
                PE.run(mm(P[bank][:, at:at + w], ga2[:, t % GA2, 0:128], oh2[:, g % (GA2 // 4), 0:w, t % 4], False, False), w / 2.4e3)
                t_m2[t] = PE.mark(mm(P[bank][:, at:at + w], ga2[:, t % GA2, 128:256], oh2[:, g % (GA2 // 4), 0:w, t % 4], False, last), w / 2.4e3)
                if last:
                    start(sums2(j, bank, t_m2[t]), .5)

        def sums2(j, bank, t):
            c0 = S.from2 + STEP * j
            c1 = min(NP, c0 + 512)
            yield AC, lambda: [t, t_yb.get((c1 - 1) // 128, LATER)], []
            AC.wait(t, t_yb[(c1 - 1) // 128])
            a = t
            if c1 - c0 > 128:
                a = free[bank] = AC.mark(lambda e: e.activation(agg[:, c0 + 128:c1], P[bank][:, 128:c1 - c0], ACT.Copy), .45)
            if j:
                yield DV, lambda: [t, a, t_a2.get(("e", j - 1), LATER)], []
                DV.wait(t, a, t_a2["e", j - 1])
                a = free[bank] = DV.mark(lambda e: e.tensor_tensor(
                    agg[:, c0:c0 + 128], P[bank][:, 0:128], agg[:, c0:c0 + 128], ALU.add))
            t_a2["e", j] = a
            held.discard(bank)

        def batch2():
            out_ = []
            ends = -(-S.cut // 128)
            for hh in range(NH):
                if HW * D * hh < S.cut <= HW * D * (hh + 1):
                    out_.append((list(range(batch(hh)[0], ends)), [hh, max(0, hh - 1), *([("e", 0)] if S.cut % 128 else [])]))
                elif HW * D * hh < S.cut:
                    out_.append((batch(hh), [hh, max(0, hh - 1)]))
            for j in range(N2):
                b0 = ends if j == 0 else (S.from2 + STEP * j) // 128
                b1 = NB if j == N2 - 1 else (S.from2 + STEP * j + STEP) // 128
                out_.append((list(range(b0, b1)), [("e", j)]))
            assert sorted(b for bl, _ in out_ for b in bl) == list(range(NB))
            d = len(out_) - N2 - 1
            if len(out_[d][0]) + len(out_[-1][0]) <= 4:
                return [[x] for x in out_[:d] + out_[d + 1:-1]] + [[out_[-1], out_[d]]]
            return [[x] for x in out_]

        def node2(n, groups):
            Tk = Tb[n % 2]
            s = (sm, sm2)[n % 2]
            m = 0
            for g, (bl, sums) in enumerate(groups):
                bank = ("PM0", "PA")[(n + g) % 2]
                yield PE, lambda: [*[t_a2.get(x, LATER) for x in sums], free[bank]], [bank] + ([f"T{n % 2}"] if g == 0 else [])
                PE.wait(*[t_a2[x] for x in sums], free[bank], t_prep["w"])
                for i, b in enumerate(bl):
                    f = mm(P[bank][:, 128 * i:128 * i + 128], agg[:, 128 * b:128 * b + 128], W2L, True, True)
                    if b != bl[-1]:
                        PE.run(f)
                t1 = PE.mark(f)
                yield DV, lambda: [t1, t_st.get(n % 2), *[t_R.get((1, b), LATER) for b in bl]], []
                DV.wait(t1, t_st.get(n % 2), *t_lo.values())
                for i, b in enumerate(bl):
                    DV.wait(t_R[1, b])
                    t = DV.mark(lambda e, i=i, b=b, bank=bank, m=m: e.scalar_tensor_tensor(
                        Tk[:, 128 * (m + i):128 * (m + i) + 128], P[bank][:, 128 * i:128 * i + 128], inv[:, 1, b:b + 1], R[:, b, :],
                        ALU.mult, ALU.add), .27)
                free[bank] = t
                held.discard(bank)
                DV.wait(t)
                a, z = m, m + len(bl)
                t2 = DV.mark(lambda e, a=a, z=z: e.tensor_reduce(s[:, 0, a:z], Tk[:, 128 * a:128 * z].rearrange("p (b f) -> p b f", f=128),
                                                                 AX.X, ALU.max, negate=True), .47)
                yield AC, lambda: [t2], []
                AC.wait(t2, *t_Hfree)
                for i in range(a, z):
                    t = AC.mark(lambda e, i=i: e.activation(Hj[:, 128 * i:128 * i + 128], Tk[:, 128 * i:128 * i + 128], ACT.Exp,
                                                            bias=s[:, 0, i:i + 1], accum_out=s[:, 1, i:i + 1]), .75 if i == a else .3)
                m = z
            AC.wait(t)
            t3 = AC.mark(lambda e: e.activation(s[:, 2, 0:m], s[:, 1, 0:m], ACT.Ln), 1.4)
            yield DV, lambda: [t3], []
            DV.wait(t3)
            t = DV.mark(lambda e: e.tensor_tensor(s[:, 3, 0:m], s[:, 2, 0:m], s[:, 0, 0:m], ALU.subtract), .08)
            DV.wait(t)
            at = 0
            for bl, _ in groups:
                for b in bl:
                    t = DV.mark(lambda e, i=at, b=b: e.scalar_tensor_tensor(
                        Tk[:, 128 * i:128 * i + 128], Tk[:, 128 * i:128 * i + 128], s[:, 3, i:i + 1], xs[:, b, :],
                        ALU.subtract, ALU.add), .27)
                    at += 1
                SP.wait(t)
                t_st[n % 2] = SP.dma(lambda e, bl=bl, a=at - len(bl), z=at: e.dma_start(
                    ov[:, bl[0]:bl[-1] + 1, :], Tk[:, 128 * a:128 * z].rearrange("p (b f) -> p b f", f=128)), d_o[n % 2])
            held.discard(f"T{n % 2}")

        Hj = H[:, :, :].rearrange("p a k -> p (a k)")
        sm2 = sb("sm2", [128, 4, 4])

        def make_flag():
            yield DV, lambda: [t_prep.get("inv", LATER), *[t_row.get(h, LATER) for h in range(NH)],
                               *[t_h1.get(b, LATER) for b in range(NB)]], []
            DV.wait(t_prep["j"], t_drel, *t_row.values(), *t_h1.values())
            bad = fl[:, 1:2]
            DV.mark(lambda e: e.tensor_reduce(fl[:, 0:1], rmax[:, :], AX.X, ALU.add))
            DV.mark(lambda e: e.tensor_reduce(fl[:, 2:3], cs[:, 0, :, :].rearrange("p c d -> p (c d)"), AX.X, ALU.add))
            t = DV.mark(lambda e: e.tensor_scalar(junk[:, 0:NB], mv[:, :, 1], 1e30, 0.0, ALU.is_lt, ALU.add,
                                                  accum_out=fl[:, 10:11]))
            DV.wait(t, *t_prep["over"])
            DV.mark(lambda e: e.tensor_scalar(fl[:, 3:4], fl[:, 7:8], 1 / WSCALE, None, ALU.is_ge))
            DV.mark(lambda e: e.tensor_scalar(fl[:, 4:5], fl[:, 9:10], 1 / ESCALE, None, ALU.is_ge))
            t = DV.mark(lambda e: e.tensor_scalar(bad, fl[:, 5:6], 0.0, None, ALU.is_gt))
            for at, limit, op in ((6, 1.0, ALU.is_lt), (7, WMAX, ALU.is_gt), (8, -WMAX, ALU.is_lt),
                                  (10, NB - 0.5, ALU.is_lt)):
                DV.wait(t)
                t = DV.mark(lambda e, at=at, limit=limit, op=op: e.scalar_tensor_tensor(
                    bad, fl[:, at:at + 1], limit, bad, op, ALU.add))
            yield PE, lambda: [t, free["PM1"]], ["PM1"]
            PE.wait(t, t_cst, free["PM1"])
            t2 = PE.mark(mm(P["PM1"][0:1, 0:5], ones[:, 0:1], fl[:, 0:5], True, True))
            yield DV, lambda: [t2], []
            DV.wait(t2)
            t = free["PM1"] = DV.mark(lambda e: e.tensor_copy(flag_f[:, 0:5], P["PM1"][0:1, 0:5]))
            held.discard("PM1")
            DV.wait(t)
            DV.mark(lambda e: e.tensor_scalar(flag_f[:, 2:3], flag_f[:, 2:3], float(S.e), None, ALU.not_equal))
            t = DV.mark(lambda e: e.tensor_scalar(flag_f[:, 3:5], flag_f[:, 3:5], 0.0, None, ALU.is_equal))
            DV.wait(t)
            t = DV.mark(lambda e: e.tensor_reduce(flag_f[:, 5:6], flag_f[:, 0:4], AX.X, ALU.add))
            DV.wait(t)
            t_prep["flag"] = DV.mark(lambda e: e.tensor_tensor(flag[:, :], flag_f[:, 5:6], flag_f[:, 4:5], ALU.add))

        PO.wait(t_h0d, t_nat, t_last)
        NQ = -(-NB // 4)
        def reach():
            yield DV, lambda: [t_drel], []
            past = AT[:, :, :].rearrange("p a k -> p (a k)")[:, 0:NT]
            DV.wait(t_drel, t_w16)
            t = DV.mark(lambda e: e.tensor_tensor(
                past.rearrange("p (g j) -> p g j", j=4), drel[:, :].rearrange("p (g j) -> p g j", j=4),
                lastb.unsqueeze(2).to_broadcast([128, G, 4]), ALU.subtract), .94)
            DV.wait(t, t_cst)
            a = DV.mark(lambda e: e.tensor_reduce(fl[:, 5:6], past, AX.X, ALU.max), .94)
            b = DV.mark(lambda e: e.tensor_reduce(fl[:, 6:7], drel[:, :], AX.X, ALU.min), .94)
            c = DV.mark(lambda e: e.tensor_reduce(fl[:, 7:8], ew_n, AX.X, ALU.max), .94)
            d = DV.mark(lambda e: e.tensor_reduce(fl[:, 8:9], ew_n, AX.X, ALU.min), .94)
            t_prep["over"] = (a, b, c, d)
            t_prep["over"] = (c, d)

        def quads_of_blocks():
            began = PE.at
            for i in range(NQ):
                yield PE, lambda: [began + QGAP * (i - QE)], []
                yield from quad(i)
            clear_agg()

        def windows():
            for part, (wa, wz) in enumerate(parts):
                yield DV, lambda: [t_win[wz - 1], t_prep.get(("rk", part - 1), LATER) if part else None], []
                windows_elementwise(part)
                for w in range(wa, wz):
                    yield from windows_turn(w)

        def window_counts():
            began = DV.at
            for w in range(WG):
                yield DV, lambda: [began + GAP * w,
                                   t_prep.get(("rk", 0 if w < parts[0][1] else 1), LATER)], []
                yield from counts(w)
            yield SP, lambda: [t_prep["j"] if len(t_rk) == WG else LATER], []
            t = spread_counts()
            yield SP, lambda: [t], []
            gather_counts(t)
            yield PE, lambda: [t_cs, free["PM0"]], ["PM0"]
            turn_counts()
            yield DV, lambda: [t_prep["cT"]], []
            keep_counts()
            held.discard("PM0")

        def scaling():
            yield DV, lambda: [t_w, t_c32], []
            scales()
            yield DV, lambda: [*t_prep["sc"]], []
            t = powers()
            yield PE, lambda: [t, free["PM1"]], ["PM1"]
            powers_turned(t)
            yield DV, lambda: [t_prep["sT"]], []
            t = scaled_weights()
            yield PE, lambda: [t], []
            bias_rows(t)
            yield DV, lambda: [t_prep["bT"]], []
            keep_biases()
            held.discard("PM1")

        NQ = -(-NB // 4)
        LEAD, GAP, QGAP = 6, 7.0, 16.0
        ends = {max(g for g in range(G) if S.bank[g] == k): k for k in range(NK)}
        onehot(0)
        onehot(1)
        for t in range(min(NT, GAN)):
            gather(t)
        def tiles():
            for t in range(NT):
                yield PE, lambda: [t_ga.get(t, LATER), t_oh.get(t // 4, LATER), t_sp.get(t // 4, LATER)], []
                tile(t)
                if t % 4 == 3 and t // 4 in ends:
                    k = ends[t // 4]
                    yield AC, lambda: [t_l0[t], t_X.get(k - 1, LATER) if k else None, t_prep.get("over", [LATER])[0]], []
                    step_evac(k, t)
                    start(step(k), 1.0)

        def onehots():
            for g in range(2, G):
                yield DV, lambda: [t_l0.get(4 * (g - OHN) + 3, LATER) if g >= OHN else None], []
                onehot(g)

        def splits():
            for g in range(G):
                yield AC, lambda: [t_ea.get(g, LATER), t_l0.get(4 * (g - ESN) + 3, LATER) if g >= ESN else None], []
                split_hi(g)
                yield DV, lambda: [t_eh[g]], []
                split_lo(g)

        def gathers():
            for t in range(GAN, NT):
                yield PO, lambda: [t_l0.get(t - GAN, LATER)], []
                if t == NT - URGE:
                    PO.at -= SOONER
                gather(t)

        def edge_loads():
            for g in range(EAN, G):
                yield SP, lambda: [t_sp.get(g - EAN, LATER)], []
                load_ea(g)

        for favour, g in ((3.0, tiles), (3.0, onehots), (3.0, splits), (3.0, gathers), (3.0, edge_loads), (.5, reach), (.5, quads_of_blocks), (.5, windows), (.3, window_counts),
                          (.5, scaling), (.4, count_products), (.2, count_quads), (0, conv1_stream), (0, loader), (0, early_loader), (.1, load_tails),
                          (0, make_flag)):
            start(g(), favour)
        for hh in range(NH):
            start(node1_early(hh), EARLY)
            start(node1(hh), .8 - .01 * hh)
            if HW * D * hh < S.cut:
                start(conv2_half(hh), -.01 * hh)
        for n, groups in enumerate(batch2()):
            start(node2(n, groups), .4)
        for favour, g in ((2.0, gathers2), (2.0, onehots2), (2.0, tiles2)):
            start(g(), favour)
        run_tasks()
        SP.wait(*t_st.values())

        g1, g2 = xs[:, :, :].rearrange("p b f -> p (b f)"), agg[:, :]
        places = {}
        at = 0
        for n, w in (("C", 129), ("msg", 257), ("rsum", 258), ("eq", 128), ("eqw", 128), ("junk", 128)):
            places[n] = g1[:, at:at + w]
            at += w
        at = 0
        for n, w in (("nA", 258), ("nX", 128), ("nH", 128), ("tT", 512), ("o1", 128)):
            places[n] = g2[:, at:at + w]
            at += w
        places |= {"drow": l0[:, 0:128].bitcast(I32), "col": l0[:, 128:136], "coli": l0[:, 136:140].bitcast(I32),
                   "s1": l0[:, 140:160], "o2": l0[:, 160:288],
                   "idn": idn, "bb": bb, "Wall": W,
                   "W": {"WI": WI, "WJ": WJ, "WE": WE, "WS": WS, "W1L": W1L, "W1R": W1R, "W2L": W2L, "W2R": W2R}}
        loops = general_path(nc, T, S, out, sem, places, P)
        ends_ = [(q.sem, q.n) for q in (PE, DV, AC, PO)] + [t_st[0], t_st[1]]

        def finish(e, q, name):
            q.wait(t_prep["flag"])
            for f in q.ops:
                f(e)
            v = e.value_load(flag[0:1, 0:1], min_val=0, max_val=1 << 20)
            with e.If(v != 0):
                for x, n in ends_:
                    e.wait_ge(x, n)
                for L in loops:
                    if not L.ops[name]:
                        continue
                    if L.rounds == 1:
                        for f in L.ops[name]:
                            f(e, 0)
                        continue
                    with e.Fori(0, L.rounds) as i:
                        for f in L.ops[name]:
                            f(e, i)
            e.end_ifs()

        block = ctx.enter_context(nc.Block())

        @block.sync
        def _(e):
            finish(e, SP, "SP")

        @block.gpsimd
        def _(e):
            finish(e, PO, "PO")

        @block.scalar
        def _(e):
            finish(e, AC, "AC")

        @block.tensor
        def _(e):
            finish(e, PE, "PE")

        @block.vector
        def _(e):
            finish(e, DV, "DV")


def arrays_of(S, x, src, dst, edge_attr_128, edge_weight, L0_gnn_W_msg, L0_gnn_W_self,
              L1_gnn_W1_l, L1_gnn_b1_l, L1_gnn_W1_r, L1_gnn_W2_l, L1_gnn_b2_l, L1_gnn_W2_r):
    import numpy as np

    def rows(a, n, fill=0):
        a = np.asarray(a)
        o = np.full((n,) + a.shape[1:], fill, a.dtype)
        o[:len(a)] = a
        return o

    def natural(a):
        return np.ascontiguousarray(a.reshape(S.nt, 128).T)

    A = {"x": rows(x, S.np), "ea": rows(edge_attr_128, S.ep)}
    A["src"], A["dst"], A["ew"] = rows(src, S.ep), rows(dst, S.ep, S.np - 1), rows(edge_weight, S.ep)
    for k in ("src", "dst", "ew"):
        A[k + "_n"] = natural(A[k])
    A["heads"] = np.ascontiguousarray(rows(A["dst"][::64], S.hb * 128, S.np - 1).reshape(S.hb, 128).T)
    b64 = rows(A["dst"], S.hb * 128 * 64, S.np - 1).reshape(S.hb * 128, 64)
    before = np.concatenate([np.zeros_like(b64[:1]), b64[:-1]])
    fill = lambda a: rows(a, S.hb * 128 * 64)
    for k, a in (("blocks", b64), ("before", before), ("src_b", fill(A["src"])), ("ew_b", fill(A["ew"]))):
        A[k] = np.ascontiguousarray(a.reshape(S.hb, 128, 64).transpose(1, 0, 2))
    Wm = np.asarray(L0_gnn_W_msg)
    w1l, w1r, w2l, w2r = (np.asarray(w) for w in (L1_gnn_W1_l, L1_gnn_W1_r, L1_gnn_W2_l, L1_gnn_W2_r))
    A["W"] = np.stack([Wm[0:128], np.asarray(L0_gnn_W_self), Wm[128:256], Wm[256:384], w1l.T, w1r.T, w2l.T, w2r.T], 1)
    A["Wn"] = np.stack([w1l, w1r], 1)
    A["b"] = np.stack([np.asarray(L1_gnn_b1_l), np.asarray(L1_gnn_b2_l)])
    i128 = np.arange(128)
    w5 = D * (i128[:, None] + 128 * np.arange(S.wg)[None, :])
    A["c32"] = np.concatenate([np.eye(128), w5], 1).astype(np.float32)
    A["gen"] = np.concatenate([np.tri(128, k=-1), S.np + i128[:, None]], 1).astype(np.float32)
    A["rows"] = np.concatenate([np.array(S.base) - 1, S.wid])[None].astype(np.float32)
    return A


def kernel(**inputs):
    import numpy as _np
    import concourse.bacc as _bacc
    from concourse import mybir as _mybir
    from concourse.bass_utils import run_bass_kernel_spmd as _run

    S = FULL
    A = arrays_of(S, **{k: _np.asarray(v) for k, v in inputs.items()})
    nc = _bacc.Bacc("TRN2", target_bir_lowering=False, num_devices=1)
    arrays, T = {}, {}
    for name, a in A.items():
        a = _np.ascontiguousarray(a)
        arrays[f"in_{name}_dram"] = a
        T[name] = nc.dram_tensor(f"in_{name}_dram", a.shape, _mybir.dt.from_np(a.dtype), kind="ExternalInput").ap()
    out = nc.dram_tensor("out_0_dram", (S.np, 128), F32, kind="ExternalOutput").ap()
    gnn_kernel(nc, T, S, out)
    r = _run(nc, [arrays], core_ids=[0])
    return r.results[0]["out_0_dram"][:S.n]
```
